# Optimizing a Trainium2 kernel written in Bass

```python
import numpy as np
import jax
import jax.numpy as jnp

def _softmax(x, axis=-1):
    return jax.nn.softmax(x, axis=axis)

def _gelu(x):
    return jax.nn.gelu(x, approximate=True)

def _silu(x):
    return jax.nn.silu(x)

def _sigmoid(x):
    return jax.nn.sigmoid(x)

def _layernorm(x, axis=-1, eps=1e-05):
    m = jnp.mean(x, axis=axis, keepdims=True)
    v = jnp.var(x, axis=axis, keepdims=True)
    return (x - m) / jnp.sqrt(v + eps)

def _scatter_add(tgt, idx, src, axis=0):
    return tgt.at[idx].add(src)

def _segment_sum(src, seg, n):
    return jax.ops.segment_sum(src, seg, n)
kernel_name = 'mk_vit_tower_d2_tok_img256_r4_279d0f'

def setup_inputs(seed: int=0):
    np.random.seed(seed)
    _w = jnp.asarray

    def _rec_inputs():
        import jax
        import jax.numpy as jnp
        _rk = jax.random.key(seed)
        x = -7.10856e-05 + 0.999911 * jax.random.normal(jax.random.fold_in(_rk, 1), (128, 1, 96, 96), jnp.float32)
        return x
    x = _rec_inputs()

    def _L0_tok_setup():
        import jax, jax.numpy as jnp
        import numpy as np
        INV_SQRT2 = 0.7071067811865476

        def haar_dwt2(x):
            lo = (x[..., ::2] + x[..., 1::2]) * INV_SQRT2
            hi = (x[..., ::2] - x[..., 1::2]) * INV_SQRT2
            cA = (lo[..., ::2, :] + lo[..., 1::2, :]) * INV_SQRT2
            cH = (lo[..., ::2, :] - lo[..., 1::2, :]) * INV_SQRT2
            cV = (hi[..., ::2, :] + hi[..., 1::2, :]) * INV_SQRT2
            cD = (hi[..., ::2, :] - hi[..., 1::2, :]) * INV_SQRT2
            return (cA, (cH, cV, cD))

        def wavedec2_maps(x, levels):
            a = x
            details = []
            for _ in range(levels):
                a, d = haar_dwt2(a)
                details.append(d)
            maps = [a]
            for d in reversed(details):
                maps.extend(d)
            return maps
        key = jax.random.key(seed)
        k1, k2 = jax.random.split(key)
        B, H, W_img = (64, 256, 256)
        x = jax.random.normal(k1, (B, 1, H, W_img), dtype=jnp.float32)
        n_maps = 1 + 3 * 2
        W = jax.random.normal(k2, (n_maps, 64), dtype=jnp.float32) * (1.0 / np.sqrt(n_maps))
        b = jnp.zeros((64,), dtype=jnp.float32)
        return {'x': x, 'W': W, 'b': b}
    _L0_tok_all = _L0_tok_setup()
    _L0_tok_in = {k: v for k, v in _L0_tok_all.items() if k in ('W', 'b')}
    del _L0_tok_all

    def _L0_attn_setup():
        import jax, jax.numpy as jnp
        import numpy as np
        B, S, F, H = (4, 256, 64, 8)
        SCALE = float(F) ** 0.5
        key = jax.random.key(seed)
        ks = jax.random.split(key, 5)
        return {'q_input': jax.random.normal(ks[0], (B, S, F), dtype=jnp.float32), 'Wq': jax.random.normal(ks[1], (F, F * H), dtype=jnp.float32) * 0.02, 'Wk': jax.random.normal(ks[2], (F, F * H), dtype=jnp.float32) * 0.02, 'Wv': jax.random.normal(ks[3], (F, F * H), dtype=jnp.float32) * 0.02, 'Wo': jax.random.normal(ks[4], (F * H, F), dtype=jnp.float32) * 0.02}
    _L0_attn_all = _L0_attn_setup()
    _L0_attn_in = {k: v for k, v in _L0_attn_all.items() if k in ('Wq', 'Wk', 'Wv', 'Wo')}
    del _L0_attn_all

    def _L0_ffn_setup():
        import jax, jax.numpy as jnp
        import numpy as np
        E = 8
        K = 2
        D = 64
        H = 128
        DOUT = 64
        EPS = 1e-05
        key = jax.random.key(seed)
        ks = jax.random.split(key, 9)
        s = 0.02
        return {'x': jax.random.normal(ks[0], (4, 2048, D), jnp.float32), 'gamma': 1.0 + 0.05 * jax.random.normal(ks[1], (D,), jnp.float32), 'beta': 0.05 * jax.random.normal(ks[2], (D,), jnp.float32), 'Wr': 0.01 * jax.random.normal(ks[3], (D, E), jnp.float32), 'br': jnp.zeros((E,), jnp.float32), 'W1': s * jax.random.normal(ks[4], (E, D, H), jnp.float32), 'b1': s * jax.random.normal(ks[5], (E, H), jnp.float32), 'W2': s * jax.random.normal(ks[6], (E, H, DOUT), jnp.float32), 'b2': s * jax.random.normal(ks[7], (E, DOUT), jnp.float32)}
    _L0_ffn_all = _L0_ffn_setup()
    _L0_ffn_in = {k: v for k, v in _L0_ffn_all.items() if k in ('gamma', 'beta', 'Wr', 'br', 'W1', 'b1', 'W2', 'b2')}
    del _L0_ffn_all

    def _L1_attn_setup():
        import jax, jax.numpy as jnp
        import numpy as np
        BN_EPS = 1e-05
        key = jax.random.key(seed)
        ks = jax.random.split(key, 12)
        B, N, d_e, d_a = (16, 512, 64, 64)
        s_e = 1.0 / np.sqrt(d_e)
        return {'x': jax.random.normal(ks[0], (B, N, d_e), dtype=jnp.float32), 'Wq': jax.random.uniform(ks[1], (d_e, d_a), jnp.float32, -s_e, s_e), 'bq': jax.random.uniform(ks[2], (d_a,), jnp.float32, -s_e, s_e), 'Wk': jax.random.uniform(ks[3], (d_e, d_a), jnp.float32, -s_e, s_e), 'bk': jax.random.uniform(ks[4], (d_a,), jnp.float32, -s_e, s_e), 'Wv': jax.random.uniform(ks[5], (d_e, d_e), jnp.float32, -s_e, s_e), 'bv': jax.random.uniform(ks[6], (d_e,), jnp.float32, -s_e, s_e), 'Wl': jax.random.uniform(ks[7], (d_e, d_e), jnp.float32, -s_e, s_e), 'bl': jax.random.uniform(ks[8], (d_e,), jnp.float32, -s_e, s_e), 'gamma': jnp.ones((d_e,), jnp.float32), 'beta': jnp.zeros((d_e,), jnp.float32)}
    _L1_attn_all = _L1_attn_setup()
    _L1_attn_in = {k: v for k, v in _L1_attn_all.items() if k in ('Wq', 'bq', 'Wk', 'bk', 'Wv', 'bv', 'Wl', 'bl', 'gamma', 'beta')}
    del _L1_attn_all

    def _L1_ffn_setup():
        import jax, jax.numpy as jnp
        import numpy as np
        BN_EPS = 0.001

        def _bn(h, g, b, m, v):
            return g * (h - m) * jax.lax.rsqrt(v + BN_EPS) + b
        key = jax.random.key(seed)
        ks = jax.random.split(key, 8)
        B, F, Df = (64, 64, 64)
        E, H, D = (8, 64, 64)
        s1 = 1.0 / np.sqrt(Df)
        s2 = 1.0 / np.sqrt(H)
        return {'x': jax.random.normal(ks[0], (B, F, Df), jnp.float32), 'Wr': jax.random.normal(ks[1], (Df, E), jnp.float32) * s1, 'br': jnp.zeros((E,), jnp.float32), 'W1': jax.random.normal(ks[2], (E, Df, H), jnp.float32) * s1, 'b1': jnp.zeros((E, H), jnp.float32), 'g1': jnp.ones((E, H), jnp.float32), 'be1': jnp.zeros((E, H), jnp.float32), 'm1': jnp.zeros((E, H), jnp.float32), 'v1': jnp.ones((E, H), jnp.float32), 'W2': jax.random.normal(ks[3], (E, H, H), jnp.float32) * s2, 'b2': jnp.zeros((E, H), jnp.float32), 'g2': jnp.ones((E, H), jnp.float32), 'be2': jnp.zeros((E, H), jnp.float32), 'm2': jnp.zeros((E, H), jnp.float32), 'v2': jnp.ones((E, H), jnp.float32), 'Wo': jax.random.normal(ks[4], (E, H, D), jnp.float32) * s2, 'bo': jnp.zeros((E, D), jnp.float32)}
    _L1_ffn_all = _L1_ffn_setup()
    _L1_ffn_in = {k: v for k, v in _L1_ffn_all.items() if k in ('Wr', 'br', 'W1', 'b1', 'g1', 'be1', 'm1', 'v1', 'W2', 'b2', 'g2', 'be2', 'm2', 'v2', 'Wo', 'bo')}
    del _L1_ffn_all
    return {'x': x, 'L0_tok_W': _L0_tok_in['W'], 'L0_tok_b': _L0_tok_in['b'], 'L0_attn_Wq': _L0_attn_in['Wq'], 'L0_attn_Wk': _L0_attn_in['Wk'], 'L0_attn_Wv': _L0_attn_in['Wv'], 'L0_attn_Wo': _L0_attn_in['Wo'], 'L0_ffn_gamma': _L0_ffn_in['gamma'], 'L0_ffn_beta': _L0_ffn_in['beta'], 'L0_ffn_Wr': _L0_ffn_in['Wr'], 'L0_ffn_br': _L0_ffn_in['br'], 'L0_ffn_W1': _L0_ffn_in['W1'], 'L0_ffn_b1': _L0_ffn_in['b1'], 'L0_ffn_W2': _L0_ffn_in['W2'], 'L0_ffn_b2': _L0_ffn_in['b2'], 'L1_attn_Wq': _L1_attn_in['Wq'], 'L1_attn_bq': _L1_attn_in['bq'], 'L1_attn_Wk': _L1_attn_in['Wk'], 'L1_attn_bk': _L1_attn_in['bk'], 'L1_attn_Wv': _L1_attn_in['Wv'], 'L1_attn_bv': _L1_attn_in['bv'], 'L1_attn_Wl': _L1_attn_in['Wl'], 'L1_attn_bl': _L1_attn_in['bl'], 'L1_attn_gamma': _L1_attn_in['gamma'], 'L1_attn_beta': _L1_attn_in['beta'], 'L1_ffn_Wr': _L1_ffn_in['Wr'], 'L1_ffn_br': _L1_ffn_in['br'], 'L1_ffn_W1': _L1_ffn_in['W1'], 'L1_ffn_b1': _L1_ffn_in['b1'], 'L1_ffn_g1': _L1_ffn_in['g1'], 'L1_ffn_be1': _L1_ffn_in['be1'], 'L1_ffn_m1': _L1_ffn_in['m1'], 'L1_ffn_v1': _L1_ffn_in['v1'], 'L1_ffn_W2': _L1_ffn_in['W2'], 'L1_ffn_b2': _L1_ffn_in['b2'], 'L1_ffn_g2': _L1_ffn_in['g2'], 'L1_ffn_be2': _L1_ffn_in['be2'], 'L1_ffn_m2': _L1_ffn_in['m2'], 'L1_ffn_v2': _L1_ffn_in['v2'], 'L1_ffn_Wo': _L1_ffn_in['Wo'], 'L1_ffn_bo': _L1_ffn_in['bo']}

def reference(x, L0_tok_W, L0_tok_b, L0_attn_Wq, L0_attn_Wk, L0_attn_Wv, L0_attn_Wo, L0_ffn_gamma, L0_ffn_beta, L0_ffn_Wr, L0_ffn_br, L0_ffn_W1, L0_ffn_b1, L0_ffn_W2, L0_ffn_b2, L1_attn_Wq, L1_attn_bq, L1_attn_Wk, L1_attn_bk, L1_attn_Wv, L1_attn_bv, L1_attn_Wl, L1_attn_bl, L1_attn_gamma, L1_attn_beta, L1_ffn_Wr, L1_ffn_br, L1_ffn_W1, L1_ffn_b1, L1_ffn_g1, L1_ffn_be1, L1_ffn_m1, L1_ffn_v1, L1_ffn_W2, L1_ffn_b2, L1_ffn_g2, L1_ffn_be2, L1_ffn_m2, L1_ffn_v2, L1_ffn_Wo, L1_ffn_bo):
    import jax
    import jax.numpy as jnp

    def _L0_tok_ref(x, W, b):
        import jax, jax.numpy as jnp
        import numpy as np
        INV_SQRT2 = 0.7071067811865476

        def haar_dwt2(x):
            lo = (x[..., ::2] + x[..., 1::2]) * INV_SQRT2
            hi = (x[..., ::2] - x[..., 1::2]) * INV_SQRT2
            cA = (lo[..., ::2, :] + lo[..., 1::2, :]) * INV_SQRT2
            cH = (lo[..., ::2, :] - lo[..., 1::2, :]) * INV_SQRT2
            cV = (hi[..., ::2, :] + hi[..., 1::2, :]) * INV_SQRT2
            cD = (hi[..., ::2, :] - hi[..., 1::2, :]) * INV_SQRT2
            return (cA, (cH, cV, cD))

        def wavedec2_maps(x, levels):
            a = x
            details = []
            for _ in range(levels):
                a, d = haar_dwt2(a)
                details.append(d)
            maps = [a]
            for d in reversed(details):
                maps.extend(d)
            return maps
        imgs = x[:, 0]
        B = imgs.shape[0]
        maps = wavedec2_maps(imgs, 2)
        proc = [jax.image.resize(m, (B, 8, 8), method='bilinear') for m in maps]
        feat = jnp.stack(proc, axis=1)
        feat = feat.reshape(B, feat.shape[1], 64).transpose(0, 2, 1)
        return feat @ W + b

    def _L0_attn_ref(q_input, Wq, Wk, Wv, Wo):
        import jax, jax.numpy as jnp
        import numpy as np
        B, S, F, H = (4, 256, 64, 8)
        SCALE = float(F) ** 0.5
        b, s, f = q_input.shape
        h = Wq.shape[1] // f
        q = (q_input.reshape(b * s, f) @ Wq).reshape(b, s, f, h)
        k = (q_input.reshape(b * s, f) @ Wk).reshape(b, s, f, h)
        v = (q_input.reshape(b * s, f) @ Wv).reshape(b, s, f, h)
        qkt = jnp.einsum('bifh,bjfh->bijh', q, k)
        attn = jax.nn.sigmoid(qkt * SCALE)
        wv = jnp.einsum('bijh,bjfh->bifh', attn, v)
        wv = wv.reshape(b * s, f * h)
        out = jax.nn.relu(wv @ Wo)
        return out.reshape(b, s, f)

    def _L0_ffn_ref(x, gamma, beta, Wr, br, W1, b1, W2, b2):
        import jax, jax.numpy as jnp
        import numpy as np
        E = 8
        K = 2
        D = 64
        H = 128
        DOUT = 64
        EPS = 1e-05
        mu = jnp.mean(x, axis=-1, keepdims=True)
        var = jnp.mean(jnp.square(x - mu), axis=-1, keepdims=True)
        xn = (x - mu) * jax.lax.rsqrt(var + EPS) * gamma + beta
        logits = jnp.einsum('bsd,de->bse', xn, Wr) + br
        top_vals, top_idx = jax.lax.top_k(logits, K)
        w = jax.nn.softmax(top_vals, axis=-1)
        w_full = jnp.einsum('bsk,bske->bse', w, jax.nn.one_hot(top_idx, E, dtype=w.dtype))
        y = jnp.zeros(x.shape[:-1] + (DOUT,), x.dtype)
        for e in range(E):
            h = jax.nn.gelu(jnp.einsum('bsd,dh->bsh', xn, W1[e]) + b1[e], approximate=False)
            y_e = jnp.einsum('bsh,hd->bsd', h, W2[e]) + b2[e]
            y = y + y_e * w_full[..., e, None]
        return y

    def _L1_attn_ref(x, Wq, bq, Wk, bk, Wv, bv, Wl, bl, gamma, beta):
        import jax, jax.numpy as jnp
        import numpy as np
        BN_EPS = 1e-05
        q = x @ Wq + bq
        k = x @ Wk + bk
        v = x @ Wv + bv
        d_a = q.shape[-1]
        score = jnp.einsum('bnd,bmd->bnm', q, k) / jnp.asarray(d_a, q.dtype)
        score = jax.nn.softmax(score, axis=2)
        attn = jnp.einsum('bnm,bmd->bnd', score, v)
        h = attn @ Wl + bl
        mean = jnp.mean(h, axis=(0, 1))
        var = jnp.mean((h - mean) ** 2, axis=(0, 1))
        y = jax.nn.relu((h - mean) * jax.lax.rsqrt(var + BN_EPS) * gamma + beta)
        return y + x

    def _L1_ffn_ref(x, Wr, br, W1, b1, g1, be1, m1, v1, W2, b2, g2, be2, m2, v2, Wo, bo):
        import jax, jax.numpy as jnp
        import numpy as np
        BN_EPS = 0.001

        def _bn(h, g, b, m, v):
            return g * (h - m) * jax.lax.rsqrt(v + BN_EPS) + b
        feat = jnp.mean(x, axis=0)
        w = jax.nn.softmax(feat @ Wr + br, axis=-1)
        h = jnp.einsum('bfd,edh->bfeh', x, W1) + b1
        h = jax.nn.relu(_bn(h, g1, be1, m1, v1))
        h = jnp.einsum('bfeh,ehk->bfek', h, W2) + b2
        h = jax.nn.relu(_bn(h, g2, be2, m2, v2))
        y = jnp.einsum('bfeh,ehd->bfed', h, Wo) + bo
        return jnp.einsum('bfed,fe->bfd', y, w)
    h = _L0_tok_ref(x, L0_tok_W, L0_tok_b)
    h = h + _L0_attn_ref(_layernorm(h, axis=-1), L0_attn_Wq, L0_attn_Wk, L0_attn_Wv, L0_attn_Wo)
    h = h + _L0_ffn_ref(_layernorm(h, axis=-1), L0_ffn_gamma, L0_ffn_beta, L0_ffn_Wr, L0_ffn_br, L0_ffn_W1, L0_ffn_b1, L0_ffn_W2, L0_ffn_b2)
    h = h + _L1_attn_ref(_layernorm(h, axis=-1), L1_attn_Wq, L1_attn_bq, L1_attn_Wk, L1_attn_bk, L1_attn_Wv, L1_attn_bv, L1_attn_Wl, L1_attn_bl, L1_attn_gamma, L1_attn_beta)
    h = h + _L1_ffn_ref(_layernorm(h, axis=-1), L1_ffn_Wr, L1_ffn_br, L1_ffn_W1, L1_ffn_b1, L1_ffn_g1, L1_ffn_be1, L1_ffn_m1, L1_ffn_v1, L1_ffn_W2, L1_ffn_b2, L1_ffn_g2, L1_ffn_be2, L1_ffn_m2, L1_ffn_v2, L1_ffn_Wo, L1_ffn_bo)
    return h

_drawn_inputs = setup_inputs


def setup_inputs(seed=0):
    import zlib

    import numpy as np

    out = dict(_drawn_inputs(seed))
    spreads = {'L0_tok_b': (0.0, 0.1),
     'L0_ffn_br': (0.0, 0.361),
     'L1_attn_gamma': (1.0, 0.2),
     'L1_attn_beta': (0.0, 0.388),
     'L1_ffn_br': (0.0, 0.8),
     'L1_ffn_b1': (0.0, 0.8),
     'L1_ffn_g1': (1.0, 0.6),
     'L1_ffn_be1': (0.0, 0.8),
     'L1_ffn_m1': (0.0, 0.8),
     'L1_ffn_v1': (1.0, 0.6),
     'L1_ffn_b2': (0.0, 0.52),
     'L1_ffn_g2': (1.0, 0.6),
     'L1_ffn_be2': (0.0, 0.694),
     'L1_ffn_m2': (0.0, 0.545),
     'L1_ffn_v2': (1.0, 0.6),
     'L1_ffn_bo': (0.0, 0.416)}
    factors = {'L0_ffn_gamma': 8.0,
     'L0_ffn_beta': 8.0,
     'L0_ffn_Wr': 3.348,
     'L0_ffn_W1': 3.846,
     'L0_ffn_b1': 8.0,
     'L0_ffn_W2': 3.669,
     'L0_ffn_b2': 3.851,
     'L1_attn_Wq': 8.0,
     'L1_attn_bq': 23.216,
     'L1_attn_Wk': 8.0,
     'L1_attn_bk': 64.0,
     'L1_attn_bv': 64.0,
     'L1_attn_bl': 64.0}
    for name, (base, spread) in spreads.items():
        noise = np.random.default_rng([zlib.crc32(name.encode()), seed]).standard_normal(out[name].shape)
        drawn = base * np.exp(spread * noise) if base else spread * noise
        out[name] = jnp.asarray(drawn.astype(out[name].dtype))
    for name, factor in factors.items():
        out[name] = (out[name] * factor).astype(out[name].dtype)
    return out
```

```python
from contextlib import ExitStack

import concourse.bass as bass
from concourse import mybir

F32 = mybir.dt.float32
F16 = mybir.dt.float16
I32 = mybir.dt.int32
ALU = mybir.AluOpType
ACT = mybir.ActivationFunctionType
AX = mybir.AxisListType
DS = bass.ds

P = 128
B = 128
S = 64
D = 64
R = 96
TILES = B // 2
CT = 4
CHUNKS = TILES // CT
CN = CT * P
HEADS = 8
E = 8
H0 = 128
NMAPS = 7
GROUP = 16
GROUPS = B // GROUP
EPS = 1e-5
BN_EPS_ATT = 1e-5
BN_EPS_FFN = 1e-3
RING = 6

SEG = {}
_at = 0
for _name, _width in (("M", HEADS * D), ("N", HEADS * D), ("W1", E * H0), ("R", E),
                      ("Q", D), ("K", D), ("V", D), ("U", E * D)):
    SEG[_name] = (_at, _at + _width)
    _at += _width
WCOLS = _at
SEGS = list(SEG)

POOL_CONSTS = 5 + E
FTOK_ONES = 1
PERMUTED = 5
TURNED_READY = 16
EPS_ADDED = 22
PRODUCTS_READY = 35
WMAX_READY = 47
SPLIT_READY = 64
PREP_AT = (2, 3, 4, 5)
RT_TANH = 13
RT_STEPS = 18
GATE_SHIFTED = 4
GATE_STEPS = 11


class Chunk:

    def __init__(self, c, u, near, looped):
        self.c, self.u, self.near, self.looped = c, u, near, looped


def all_chunks(eng, body):
    for c in (0, 1):
        body(Chunk(c, c, c, False))
    with eng.Fori(1, CHUNKS // 2 - 1) as i:
        for u in (0, 1):
            body(Chunk(i * 2 + u, u, 2 + u, True))
    for c in (CHUNKS - 2, CHUNKS - 1):
        body(Chunk(c, c % 2, c, False))


def wait_if(eng, sem, value):
    if isinstance(value, int) and value <= 0:
        return
    eng.wait_ge(sem, value)


class BankRing:

    def __init__(self, full, emptied):
        self.full, self.emptied, self.order, self.index = full, emptied, [], {}

    def plan(self, stage, chunk, names):
        for name, engine in names:
            self.index[stage, chunk, name] = len(self.order)
            self.order.append(engine)

    def fills(self, n):
        return n + 1 - self.order[:n + 1].count("-")

    def _value(self, ck, at):
        v0 = at(ck.near)
        if not ck.looped:
            return v0
        slope = (at(ck.near + 2) - v0) // 2
        for j in range(0, CHUNKS - 4, 2):
            assert at(ck.near + j) == v0 + slope * j
        return ck.c * slope + (v0 - slope * ck.near)

    def slot(self, ck, stage, name):
        n = self.index[stage, ck.near, name] % RING
        assert not ck.looped or self.index[stage, ck.near + 2, name] % RING == n
        return n

    def filled(self, ck, stage, name, back=0):
        return self._value(ck, lambda c: self.fills(self.index[stage, c - back, name]))

    def _emptied(self, ck, stage, name, uses_back):
        def place(c):
            n = self.index[stage, c, name] - uses_back
            while n >= 0 and self.order[n] == "-":
                n -= RING
            return n

        if place(ck.near) < 0:
            return None, 0
        e = self.order[place(ck.near)]

        def at(c):
            n = place(c)
            assert self.order[n] == e
            return self.order[:n + 1].count(e)

        return self.emptied[e], self._value(ck, at)

    def wait_free(self, pe, ck, stage, name, wait=wait_if):
        sem, value = self._emptied(ck, stage, name, RING)
        wait(pe, sem, value)

    def wait_emptied(self, eng, ck, stage, name, wait=wait_if):
        sem, value = self._emptied(ck, stage, name, 0)
        wait(eng, sem, value)


ATT_Q = [("q0", "V"), ("q1", "A"), ("q2", "V"), ("q3", "A")]
ATT_V = [("v0", "V"), ("v1", "V"), ("v2", "A"), ("v3", "V")]
ATT_S = [("s0", "A"), ("s1", "A"), ("s2", "A"), ("s3", "A")]


def plan_ring(ring):
    for c in range(CHUNKS):
        ring.plan("att", c, ATT_Q + ATT_V + ATT_S)
    ring.plan("up", 0, [(f"e{e}", "A") for e in range(E)])
    for c in range(CHUNKS):
        for t in range(CT):
            if c + 1 < CHUNKS:
                ring.plan("up", c + 1, [(f"e{e}", "A") for e in (2 * t, 2 * t + 1)])
            ring.plan("down", c, [(f"t{t}", "V")])
    ring.plan("soft", 0, [("qk", "V"), ("v", "V"), ("s", "V")])
    for c in range(CHUNKS):
        ring.plan("soft", c, [("pt", "A"), ("skip", "-")])
        if c + 1 < CHUNKS:
            ring.plan("soft", c + 1, [("qk", "V"), ("v", "V")])
        if c + 1 < CHUNKS:
            ring.plan("soft", c + 1, [("s", "V")])
        ring.plan("soft", c, [("o", "V")])
    ring.plan("one", 0, [(f"p{k}", "AV"[k % 2]) for k in range(4)])
    for c in range(CHUNKS):
        for k in range(4):
            if c + 1 < CHUNKS:
                ring.plan("one", c + 1, [(f"p{k}", "AV"[k % 2])])
            ring.plan("two", c, [(f"p{k}", "AV"[k % 2 if k != 3 else 0])])
            if k == 1 and c >= 1:
                ring.plan("three", c - 1, [("y", "V")])
    ring.plan("three", CHUNKS - 1, [("y", "V")])


def vit_tower(nc, x, tok_W, tok_b, a_Wq, a_Wk, a_Wv, a_Wo, f_gamma, f_beta, f_Wr, f_br, f_W1, f_b1, f_W2, f_b2,
              s_Wq, s_bq, s_Wk, s_bk, s_Wv, s_bv, s_Wl, s_bl, s_gamma, s_beta,
              g_Wr, g_br, g_W1, g_b1, g_g1, g_be1, g_m1, g_v1, g_W2, g_b2, g_g2, g_be2, g_m2, g_v2, g_Wo, g_bo,
              shape_consts, out):
    with ExitStack() as ctx:
        def sb(name, shape, dt=F32):
            return ctx.enter_context(nc.sbuf_tensor(name, shape, dt))

        def sem(name):
            return ctx.enter_context(nc.semaphore(name))

        bank = [ctx.enter_context(nc.psum_tensor(f"bank{i}", [P, 512], F32)) for i in range(8)]

        h = sb("h", [P, TILES, D])
        consts = sb("consts", [P, 32 + P + S])
        resize = consts[0:R, 0:32]
        ident = consts[:, 32:32 + P]
        fold = consts[:, 32 + P:32 + P + S]
        ident16 = sb("ident16", [P, P], F16)
        ones = sb("ones", [P, P])

        wcat = sb("wcat", [P, WCOLS])
        whi = sb("whi", [P, WCOLS], F16)
        wlo = sb("wlo", [P, WCOLS], F16)
        wscale = sb("wscale", [P, len(SEGS)])
        winv = sb("winv", [P, len(SEGS)])
        wmax = sb("wmax", [P, 2, len(SEGS)])

        def seg(t, name):
            a, b = SEG[name]
            return t[:, a:b]

        def scale_of(t, name):
            k = SEGS.index(name)
            return t[:, k:k + 1]

        arena = sb("arena", [P, 8192])
        wb = sb("wb", [NMAPS + 1, D])
        rawqkv = arena[0:D, 0:1536].rearrange("g (w n) -> g w n", w=3)
        permqkv = arena[0:D, 1536:3072].rearrange("g (w a n) -> g w a n", w=3, a=4)
        wo_a = sb("wo_a", [P, HEADS, D])
        wT = arena[:, 3072:4608].rearrange("p (w a c g) -> p w a c g", w=3, a=4, c=2)
        w1raw = arena[:, 4608:5632]
        wrraw = sb("wrraw", [P, E])
        gamma0 = sb("gamma0", [P, 1])
        beta0 = sb("beta0", [D, 1])
        beta0_b = sb("beta0_b", [D, P])
        br_b = sb("br_b", [P, E])
        w2 = sb("w2", [P, E, D])
        b2blk = sb("b2blk", [CT * E, CT * D])
        rows = sb("rows", [48, P])
        cols = sb("cols", [P, 48])
        b1c = sb("b1c", [P, E])
        sig_scale = sb("sig_scale", [P, 1])
        wv1raw = sb("wv1raw", [D, D])
        wl1 = sb("wl1", [D, D])
        wv1T = sb("wv1T", [D, 2, D])
        bqk = sb("bqk", [P, 2])
        bv_c = sb("bv_c", [D, 1])
        bv_b = sb("bv_b", [D, P])
        vbias = sb("vbias", [P, D])
        bl_b = sb("bl_b", [P, D])
        bn_g = sb("bn_g", [P, D])
        bn_b = sb("bn_b", [P, D])
        u1raw = arena[:, 5632:6144].rearrange("p (e n) -> p e n", e=E)
        bnrow = arena[:, 6144:7168].rearrange("p (c n) -> p c n", c=2)
        s1row = sb("s1row", [P, E * D])
        bnrow2 = sb("bnrow2", [P, 2, 4, D])
        s2row = sb("s2row", [P, 4, D])
        u2raw = sb("u2raw", [P, 4, D])
        u2 = sb("u2", [P, 4, D])
        uo = sb("uo", [P, 4, D])
        t12 = sb("t12", [P, 2, 4])
        tmp4 = sb("tmp4", [P, 3, 4])
        wr1 = sb("wr1", [D, E])
        br1_b = sb("br1_b", [S, E])
        bo1 = sb("bo1", [E, D])

        late = sb("late", [P, TILES * D])

        stage = sb("stage", [P, 4 * GROUP * R])
        img = stage[0:R, :].rearrange("r (g b c) -> r g b c", g=4, b=GROUP)
        zbuf = sb("zbuf", [R, 2, 4, P])
        fbuf = sb("fbuf", [P, 2, 56])
        ftok = late[0:NMAPS + 1, 0:2 * GROUP * S].rearrange("m (u n) -> m u n", u=2)

        st = sb("st", [P, CT, 6])
        mv = sb("mv", [P, CT, 2])
        rstd = sb("rstd", [P, 4, CT])
        cent = sb("cent", [P, CT, D])
        xn = sb("xn", [P, CT, 2, D])
        xcat = sb("xcat", [P, CT, 2 * D], F16)
        x16 = sb("x16", [P, 2, CN], F16)
        x32 = sb("x32", [P, 2, CN])
        qbuf = arena[:, 0:2048].rearrange("p (a n) -> p a n", a=4)
        vbuf = arena[:, 2048:4096].rearrange("p (t n) -> p t n", t=CT)
        abuf = arena[:, 4096:6144].rearrange("p (t n) -> p t n", t=CT)
        gbuf = arena[:, 0:8192].rearrange("p (u e n) -> p u e n", u=2, e=E)
        resid = sb("resid", [P, 2, CT, D])
        lg = sb("lg", [P, 10, CT, E])
        top = sb("top", [P, 8, CT])
        iota = sb("iota", [P, CT, E])
        wtT = sb("wtT", [CT * E, P])
        prod = late[:, 0:CT * E * D].rearrange("p (t e d) -> p t e d", t=CT, e=E)
        part = late[:, CT * E * D:CT * (E + 6) * D].rearrange("p (t e d) -> p t e d", t=CT, e=6)
        qk = sb("qk", [P, 2, 2, 256])
        vv = sb("vv", [P, 2, 256])
        sc = sb("sc", [P, 256])
        pr = sb("pr", [P, 2, 256])
        mx = sb("mx", [P, 2, CT])
        rs = sb("rs", [P, 2, CT])
        pT = sb("pT", [P, 256])
        ao = late[:, :].rearrange("p (t d) -> p t d", t=TILES)
        mean_b = sb("mean_b", [P, D])
        bnA = sb("bnA", [P, D])
        sq = sb("sq", [P, 2, CT * D])
        x16all = sb("x16all", [P, TILES * P], F16)
        feat = sb("feat", [D, S])
        gl = sb("gl", [S, 4, E])
        gs = sb("gs", [S, 4])
        gwb = sb("gwb", [P, 4, S])
        gwx = sb("gwx", [S, E, D])
        gwT = sb("gwT", [E, 2, S])
        bow = sb("bow", [P, D])
        h1 = arena[:, 0:4096].rearrange("p (u a n) -> p u a n", u=2, a=4)
        h2 = arena[:, 4096:8192].rearrange("p (u a n) -> p u a n", u=2, a=4)
        h2w = stage[:, 0:8 * CN].rearrange("p (u a n) -> p u a n", u=2, a=4)
        zero = sb("zero", [1, 512])
        minus_half = sb("minus_half", [P, 1])
        ln_eps = sb("ln_eps", [P, CT])

        s_const, s_wa, s_wf = sem("consts_loaded"), sem("attention_weights_loaded"), sem("other_weights_loaded")
        s_b2 = sem("b2_blocks_loaded")
        s_img = [sem(f"images_loaded{i}") for i in range(4)]
        prep_pe, prep_dve, prep_pool = sem("prep_pe"), sem("prep_dve"), sem("prep_pool")
        rows_done, z_copied, maps_done, maps_copied = (sem("rows_resized"), sem("rows_copied"), sem("maps_done"),
                                                       sem("maps_copied"))
        ft_done, ft_copied, tok_done, h_ready = (sem("maps_turned"), sem("turned_copied"), sem("tokens_done"),
                                                 sem("tokens_copied"))
        ring_full = sem("ring_full")
        act_emptied, dve_emptied = sem("act_emptied"), sem("dve_emptied")
        ln_stats, ln_aggr, ln_step = sem("ln_stats"), sem("ln_aggr"), sem("ln_step")
        n_cent, n_scaled, n_hi, n_split = sem("norm_centred"), sem("norm_scaled"), sem("norm_hi"), sem("norm_split")
        x16_turned, x16_ready = sem("x16_turned"), sem("x16_ready")
        x32_turned, x32_ready = sem("x32_turned"), sem("x32_ready")
        av_done, av_relu, att_added = sem("av_done"), sem("av_relu"), sem("attention_added")
        rt_done, rt_step, rt_tanh = sem("router_done"), sem("router_step"), sem("router_tanh")
        wt_turned, wt_ready, b2_done, b2_added = (sem("weights_turned"), sem("weights_turned_copied"),
                                                  sem("b2_done"), sem("b2_added"))
        tree_step, moe_added = sem("expert_sum_step"), sem("experts_added")
        hx_added = sem("hx_added")
        sm_max, sm_exp, sm_sum = sem("score_max"), sem("score_exp"), sem("score_sum")
        sm_inv, out_even = sem("score_inverse"), sem("even_tiles_done")
        bn_sum, bn_mean, bn_cent, bn_sq, bn_var, bn_coef = (sem("bn_sum"), sem("bn_mean"), sem("bn_centred"),
                                                            sem("bn_squared"), sem("bn_var"), sem("bn_coef"))
        bn_app, bn_step, bn_eps, bn_root = sem("bn_applied"), sem("bn_step"), sem("bn_eps"), sem("bn_root")
        feat_done, gate_step, gate_pe = sem("feat_done"), sem("gate_step"), sem("gate_pe")
        gate_exp = sem("gate_exp")
        bow_added, weighed, stored = sem("bo_added"), sem("hidden_weighed"), sem("stored")

        ring = BankRing(ring_full, {"A": act_emptied, "V": dve_emptied})
        plan_ring(ring)

        def wait_apart(eng, sem, value):
            if not isinstance(value, int):
                value = eng.to_reg(value)
                eng.wait_ge(s_const, 16)
            wait_if(eng, sem, value)

        def bank_of(ck, stage, name):
            return bank[ring.slot(ck, stage, name)]

        def tiles_of(t, ck):
            return t[:, ck.c * CT:ck.c * CT + CT, :] if isinstance(ck.c, int) else t[:, DS(ck.c * CT, CT), :]

        def bc(ap, shape):
            return ap.to_broadcast(shape)

        def minus_half_like(ap):
            half = minus_half[:, 0:1] if len(ap.shape) == 2 else minus_half[:, 0:1].unsqueeze(2)
            return bc(half, list(ap.shape))

        def ring_who(stage, k):
            return ring.order[ring.index[stage, 2, f"p{k}"]]

        def three_chunk(ck):
            if not ck.looped:
                return Chunk(ck.c - 1, 1 - ck.u, ck.near - 1, False)
            return Chunk(ck.c - 1, 1 - ck.u, ck.near - 1, True)

        block = ctx.enter_context(nc.Block())

        ATT_LOADS, TOKEN_W_LOADS = [], []
        for i, w in enumerate((a_Wq, a_Wk, a_Wv)):
            ATT_LOADS.append((rawqkv[:, i, :], w))
        for q in (0, D):
            ATT_LOADS.append((wo_a[q:q + D], a_Wo.rearrange("(k h) d -> k h d", h=HEADS)))
        for i, m in enumerate((0, 2, 1, 3, 5, 4, 6)):
            TOKEN_W_LOADS.append((wb[i:i + 1, :], tok_W[m:m + 1, :]))
        TOKEN_W_LOADS.append((wb[NMAPS:NMAPS + 1, :], tok_b.rearrange("(a d) -> a d", a=1)))
        for q in (0, D):
            ATT_LOADS += [(w1raw[q:q + D, :].rearrange("p (e n) -> p e n", e=E), f_W1.rearrange("e d n -> d e n")),
                          (wrraw[q:q + D, :], f_Wr),
                          (gamma0[q:q + D, :], f_gamma.rearrange("(d a) -> d a", a=1)),
                          (seg(wcat, "Q")[q:q + D, :], s_Wq), (seg(wcat, "K")[q:q + D, :], s_Wk),
                          (u1raw[q:q + D], g_W1.rearrange("e d n -> d e n"))]
        ATT_LOADS += [(beta0[:, :], f_beta.rearrange("(d a) -> d a", a=1)),
                      (wv1raw[:, :], s_Wv), (wl1[:, :], s_Wl),
                      (bv_c[:, :], s_bv.rearrange("(d a) -> d a", a=1)),
                      (br_b[:, :], f_br.partition_broadcast(P)),
                      (bl_b[:, :], s_bl.partition_broadcast(P)),
                      (bn_g[:, :], s_gamma.partition_broadcast(P)),
                      (bn_b[:, :], s_beta.partition_broadcast(P)),
                      (bnrow[:, 0, :], g_g1.rearrange("e n -> (e n)").partition_broadcast(P)),
                      (bnrow[:, 1, :], g_v1.rearrange("e n -> (e n)").partition_broadcast(P)),
                      (w2[:, :, :], f_W2.rearrange("e n d -> n e d")),
                      (u2raw[:, :, :], g_W2.rearrange("(a e) n k -> (e n) a k", e=2)),
                      (uo[:, :, :], g_Wo.rearrange("(a e) n k -> (e n) a k", e=2)),
                      (rows[40:48, :], f_b1),
                      (wr1[:, :], g_Wr), (br1_b[:, :], g_br.partition_broadcast(S)), (bo1[:, :], g_bo)]
        for e2 in (0, 1):
            for k, v in enumerate((g_g2, g_v2)):
                ATT_LOADS.append((bnrow2[e2 * D:e2 * D + D, k], v.rearrange("(a e) n -> e a n", e=2)[e2]
                                  .partition_broadcast(D)))
            for k, v in enumerate((s_bq, s_bk)):
                ATT_LOADS.append((bqk[e2 * D:e2 * D + D, k:k + 1], v.rearrange("(d a) -> d a", a=1)))
        for k, v in enumerate((g_b1, g_g1, g_be1, g_m1, g_v1, g_b2, g_g2, g_be2, g_m2, g_v2)):
            ATT_LOADS.append((rows[4 * k:4 * k + 4, :], v.rearrange("(a e) n -> a (e n)", e=2)))
        B2_LOADS = [(b2blk[E * t:E * t + E, D * t:D * t + D], f_b2) for t in range(CT)]

        LOADS = 16 * len(ATT_LOADS)

        @block.sync
        def _(sp):
            sp.dma_start(consts[:, :], shape_consts).then_inc(s_const, 16)
            for g in range(4):
                sp.dma_start(img[:, g], x[g * GROUP:(g + 1) * GROUP, 0].rearrange("b r c -> r b c")
                             ).then_inc(s_img[g], 16)
            for dst, src in TOKEN_W_LOADS:
                sp.dma_start(dst, src).then_inc(s_wa, 16)
            for dst, src in ATT_LOADS[:12]:
                sp.dma_start(dst, src).then_inc(s_wf, 16)
            for g in range(4, GROUPS):
                sp.wait_ge(rows_done, g - 3)
                sp.dma_start(img[:, g % 4], x[g * GROUP:(g + 1) * GROUP, 0].rearrange("b r c -> r b c")
                             ).then_inc(s_img[g % 4], 16)

            out_v = out.rearrange("(n p) t d -> (p t) n d", p=2)

            def store(ck):
                ring.wait_emptied(sp, ck, "three", "y")
                sp.dma_start(tiles_of(out_v, ck), tiles_of(h, ck)).then_inc(stored, 16)

            all_chunks(sp, store)
            sp.wait_ge(stored, 16 * CHUNKS)

        @block.gpsimd
        def _(pool):
            nc.gpsimd.memset(b2blk[:, :], 0.0).then_inc(prep_pool, 1)
            nc.gpsimd.memset(ones[:, :], 1.0).then_inc(prep_pool, 1)
            nc.gpsimd.memset(zero[:, :], 0.0).then_inc(prep_pool, 1)
            for e in range(E):
                nc.gpsimd.memset(iota[:, :, e:e + 1], float(e)).then_inc(prep_pool, 1)
            nc.gpsimd.memset(minus_half[:, :], -0.5).then_inc(prep_pool, 1)
            nc.gpsimd.memset(ln_eps[:, :], EPS).then_inc(prep_pool, 1)
            pool.wait_ge(prep_pool, POOL_CONSTS)
            for dst, src in B2_LOADS:
                pool.dma_start(dst, src).then_inc(s_b2, 16)
            def inverse_root(dst, src):
                return nc.gpsimd.tensor_tensor(dst, src, minus_half_like(src), ALU.pow)

            pool.wait_ge(prep_dve, EPS_ADDED)
            inverse_root(s1row[:, :], s1row[:, :]).then_inc(prep_pool, 1)
            inverse_root(s2row[:, :, :], s2row[:, :, :]).then_inc(prep_pool, 1)
            inverse_root(tmp4[:, 0:2, :], tmp4[:, 0:2, :]).then_inc(prep_pool, 1)
            pool.wait_ge(prep_dve, WMAX_READY)
            nc.gpsimd.partition_all_reduce(wmax[:, 1, :], wmax[:, 0, :], P, bass.bass_isa.ReduceOp.max
                                           ).then_inc(prep_pool, 1)

            def normalise(ck, n, free_sem, free_value, with_xn_reader=None, twice=False, stage=0, double=False):
                pool.wait_ge(ln_aggr, n + 1)
                base = (2 * n if stage < 2 else 2 * n + 5 * CHUNKS) if not double else 7 * n - 5 * CHUNKS
                k = [0]

                def ln(ins):
                    k[0] += 1
                    ins.then_inc(ln_step, 1)

                def ln_wait():
                    pool.wait_ge(ln_step, base + k[0])

                var = mv[:, :, 1]
                ln(nc.gpsimd.tensor_tensor(rstd[:, 1, :], var, ln_eps[:, :], ALU.add))
                ln_wait()
                ln(inverse_root(rstd[:, 2 if double else 0, :], rstd[:, 1, :]))
                nc.gpsimd.tensor_tensor(cent[:, :, :], tiles_of(h, ck), bc(mv[:, :, 0:1], [P, CT, D]), ALU.subtract
                                        ).then_inc(n_cent, 1)
                if double:
                    ln_wait()
                    ln(nc.gpsimd.tensor_tensor(rstd[:, 3, :], rstd[:, 2, :], var, ALU.mult))
                    ln_wait()
                    ln(nc.gpsimd.tensor_tensor(rstd[:, 1, :], rstd[:, 3, :], rstd[:, 2, :], ALU.mult))
                    ln_wait()
                    ln(nc.gpsimd.tensor_tensor(rstd[:, 3, :], rstd[:, 1, :], ln_eps[:, :], ALU.add))
                    ln_wait()
                    ln(inverse_root(rstd[:, 1, :], rstd[:, 3, :]))
                    ln_wait()
                    ln(nc.gpsimd.tensor_tensor(rstd[:, 0, :], rstd[:, 1, :], rstd[:, 2, :], ALU.mult))
                ln_wait()
                pool.wait_ge(n_cent, n + 1)
                wait_if(pool, free_sem, free_value)
                if with_xn_reader:
                    wait_if(pool, *with_xn_reader)
                if twice:
                    nc.gpsimd.tensor_tensor(xn[:, :, :, :], bc(cent[:, :, :].unsqueeze(2), [P, CT, 2, D]),
                                            bc(rstd[:, 0, :].unsqueeze(2).unsqueeze(3), [P, CT, 2, D]), ALU.mult
                                            ).then_inc(n_scaled, 1)
                else:
                    nc.gpsimd.tensor_tensor(xn[:, :, 0, :], cent[:, :, :], bc(rstd[:, 0, :].unsqueeze(2), [P, CT, D]),
                                            ALU.mult).then_inc(n_scaled, 1)
                wait_apart(pool, n_scaled, n + 1)
                nc.gpsimd.tensor_copy(xcat[:, :, 0:D], xn[:, :, 0, :]).then_inc(n_hi, 1)
                pool.wait_ge(n_hi, n + 1)
                nc.gpsimd.tensor_tensor(xcat[:, :, D:2 * D], xn[:, :, 0, :], xcat[:, :, 0:D], ALU.subtract
                                        ).then_inc(n_split, 1)

            def norm_att(ck):
                normalise(ck, ck.c, x32_turned, ck.c, twice=True)

            def attention_body(ck):
                if ck.looped or ck.c + 2 < CHUNKS:
                    norm_att(Chunk(ck.c + 2, ck.u, ck.near + 2, ck.looped))
                pool.wait_ge(av_relu, ck.c + 1)
                nc.gpsimd.tensor_tensor(tiles_of(h, ck), tiles_of(h, ck), resid[:, ck.u], ALU.add
                                        ).then_inc(att_added, 1)

            pool.wait_ge(h_ready, GROUPS)
            norm_att(Chunk(0, 0, 0, False))
            norm_att(Chunk(1, 1, 1, False))
            all_chunks(pool, attention_body)

            def norm_moe(ck):
                normalise(ck, ck.c + CHUNKS, x16_turned, ck.c + CHUNKS, double=True)

            def moe_body(ck):
                if ck.looped or ck.c + 2 < CHUNKS:
                    norm_moe(Chunk(ck.c + 2, ck.u, ck.near + 2, ck.looped))
                ring.wait_emptied(pool, ck, "down", f"t{CT - 1}")
                wait_if(pool, moe_added, ck.c)
                nc.gpsimd.tensor_tensor(part[:, :, 0:4, :], prod[:, :, 0:4, :], prod[:, :, 4:8, :], ALU.add
                                        ).then_inc(tree_step, 1)
                pool.wait_ge(tree_step, ck.c * 3 + 1)
                nc.gpsimd.tensor_tensor(part[:, :, 4:6, :], part[:, :, 0:2, :], part[:, :, 2:4, :], ALU.add
                                        ).then_inc(tree_step, 1)
                pool.wait_ge(tree_step, ck.c * 3 + 2)
                nc.gpsimd.tensor_tensor(part[:, :, 0, :], part[:, :, 4, :], part[:, :, 5, :], ALU.add
                                        ).then_inc(tree_step, 1)
                pool.wait_ge(tree_step, ck.c * 3 + 3)
                pool.wait_ge(b2_added, ck.c + 1)
                nc.gpsimd.tensor_tensor(tiles_of(h, ck), tiles_of(h, ck), part[:, :, 0, :], ALU.add
                                        ).then_inc(moe_added, 1)

            for c in range(2):
                norm_moe(Chunk(c, c % 2, c, False))
            all_chunks(pool, moe_body)

            def norm_soft(ck):
                n = ck.c + 2 * CHUNKS
                normalise(ck, n, x16_turned, n, stage=2)
                nc.gpsimd.tensor_tensor(tiles_of(h, ck), tiles_of(h, ck), xn[:, :, 0, :], ALU.add).then_inc(hx_added, 1)
                pool.wait_ge(hx_added, ck.c + 1)

            def soft_body(ck):
                norm_soft(ck)

            all_chunks(pool, soft_body)

            def bn_centre(ck):
                pool.wait_ge(bn_mean, 1)
                nc.gpsimd.tensor_tensor(tiles_of(ao, ck), tiles_of(ao, ck), bc(mean_b[:, :].unsqueeze(1), [P, CT, D]),
                                        ALU.subtract).then_inc(bn_cent, 1)

            all_chunks(pool, bn_centre)
            pool.wait_ge(bn_eps, 1)
            inverse_root(bnA[:, :], bnA[:, :]).then_inc(bn_root, 1)

            def norm_dense(ck):
                n = ck.c + 3 * CHUNKS
                normalise(ck, n, x16_turned, n, (feat_done, ck.c), stage=3)

            def bn_apply(ck):
                pool.wait_ge(bn_coef, 1)
                pool.wait_ge(bn_cent, CHUNKS)
                nc.gpsimd.tensor_tensor(tiles_of(ao, ck), tiles_of(ao, ck), bc(bnA[:, :].unsqueeze(1), [P, CT, D]),
                                        ALU.mult).then_inc(bn_app, 1)
                if not ck.looped and ck.c == 0:
                    return
                norm_dense(Chunk(ck.c - 1, 1 - ck.u, ck.near - 1, ck.looped))

            all_chunks(pool, bn_apply)
            norm_dense(Chunk(CHUNKS - 1, 1, CHUNKS - 1, False))

            def add_bo(ck):
                pool.wait_ge(gate_step, GATE_STEPS)
                nc.gpsimd.tensor_tensor(tiles_of(h, ck), tiles_of(h, ck), bc(bow[:, :].unsqueeze(1), [P, CT, D]),
                                        ALU.add).then_inc(bow_added, 1)

            def dense_body(ck):
                add_bo(ck)
                for k in range(4):
                    ring.wait_emptied(pool, ck, "two", f"p{k}")
                    if k == 0 and (ck.looped or ck.c >= 2):
                        pool.wait_ge(ring_full, ring.filled(ck, "three", "y", 2))
                    nc.gpsimd.tensor_tensor(h2w[:, ck.u, k, :].rearrange("p (b f) -> p b f", f=S),
                                            h2[:, ck.u, k, :].rearrange("p (b f) -> p b f", f=S),
                                            bc(gwb[:, k, :].unsqueeze(1), [P, 2 * CT, S]), ALU.mult
                                            ).then_inc(weighed, 1)

            all_chunks(pool, dense_body)

        @block.scalar
        def _(act):
            def copy(dst, src):
                return nc.scalar.activation(dst, src, ACT.Copy)

            for dst, src in ATT_LOADS[12:]:
                act.dma_start(dst, src).then_inc(s_wf, 16)

            def tok_copies(g):
                u = g % 2
                act.wait_ge(rows_done, g + 1)
                if g >= 2:
                    act.wait_ge(maps_done, g - 1)
                copy(zbuf[:, u].rearrange("c o (b i) -> c o b i", b=GROUP),
                     bank[u][0:R, :].rearrange("c (b o i) -> c o b i", b=GROUP, o=4)).then_inc(z_copied, 1)
                act.wait_ge(ft_done, g + 1)
                if g >= 2:
                    act.wait_ge(tok_done, g - 1)
                else:
                    act.wait_ge(prep_dve, FTOK_ONES)
                for q in (0, 1):
                    last = copy(ftok[0:NMAPS, u].rearrange("m (b j) -> m b j", j=8)[:, :, 4 * q:4 * q + 4],
                                bank[4 + q][0:NMAPS, :].rearrange("m (j b) -> m b j", j=4))
                last.then_inc(ft_copied, 1)

            for g in range(GROUPS):
                tok_copies(g)

            def att_x16(ck):
                act.wait_ge(x16_turned, ck.c + 1)
                if ck.looped or ck.c >= 2:
                    act.wait_ge(av_done, ck.c - 1)
                copy(x16[:, ck.u, :], bank[6][:, :].bitcast(F16)[:, 0:CN]).then_inc(x16_ready, 1)

            def att_empty(ck, name, dst, func=None):
                act.wait_ge(ring_full, ring.filled(ck, "att", name))
                if func is None:
                    copy(dst, bank_of(ck, "att", name)[:, :]).then_inc(act_emptied, 1)
                else:
                    nc.scalar.activation(dst, bank_of(ck, "att", name)[:, :], func, scale=sig_scale[:, 0:1]
                                         ).then_inc(act_emptied, 1)

            def attention_body(ck):
                wait_if(act, av_done, ck.c)
                for k, (name, who) in enumerate(ATT_Q):
                    if who == "A":
                        att_empty(ck, name, qbuf[:, k, :])
                if ck.looped or ck.c + 1 < CHUNKS:
                    att_x16(Chunk(ck.c + 1, 1 - ck.u, ck.near + 1, ck.looped))
                for t, (name, who) in enumerate(ATT_V):
                    if who == "A":
                        att_empty(ck, name, vbuf[:, t, :])
                for t in range(CT):
                    att_empty(ck, f"s{t}", abuf[:, t, :], ACT.Sigmoid)
                act.wait_ge(av_done, ck.c + 1)
                if ck.looped or ck.c >= 2:
                    act.wait_ge(att_added, ck.c - 1)
                nc.scalar.activation(resid[:, ck.u].rearrange("p t d -> p (t d)"), bank[7][:, 0:CT * D], ACT.Relu,
                                     scale=scale_of(wscale, "N")).then_inc(av_relu, 1)

            act.wait_ge(prep_dve, SPLIT_READY)
            att_x16(Chunk(0, 0, 0, False))
            all_chunks(act, attention_body)

            def moe_x16(ck):
                act.wait_ge(x16_turned, ck.c + CHUNKS + 1)
                if ck.looped or ck.c >= 2:
                    act.wait_ge(ring_full, ring.filled(ck, "up", f"e{E - 1}", 2))
                copy(x16[:, ck.u, :], bank[6][:, :].bitcast(F16)[:, 0:CN]).then_inc(x16_ready, 1)

            def gelu(ck, e):
                act.wait_ge(ring_full, ring.filled(ck, "up", f"e{e}"))
                nc.scalar.activation(gbuf[:, ck.u, e, :], bank_of(ck, "up", f"e{e}")[:, :], ACT.Gelu,
                                     bias=b1c[:, e:e + 1], scale=scale_of(wscale, "W1")).then_inc(act_emptied, 1)

            def router_tanh(ck):
                act.wait_ge(rt_step, ck.c * RT_STEPS + RT_TANH)
                nc.scalar.activation(top[:, 3, :], top[:, 2, :], ACT.Tanh, scale=0.5).then_inc(rt_tanh, 1)

            def moe_body(ck):
                nx = Chunk(ck.c + 1, 1 - ck.u, ck.near + 1, ck.looped)
                if ck.looped or ck.c + 1 < CHUNKS:
                    router_tanh(nx)
                    for t in range(CT):
                        for e in (2 * t, 2 * t + 1):
                            if e == 0 and (ck.looped or ck.c >= 1):
                                act.wait_ge(ring_full, ring.filled(ck, "down", f"t{CT - 1}", 1))
                            gelu(nx, e)
                        if t == 2 and (ck.looped or ck.c + 2 < CHUNKS):
                            moe_x16(Chunk(ck.c + 2, ck.u, ck.near + 2, ck.looped))

            moe_x16(Chunk(0, 0, 0, False))
            router_tanh(Chunk(0, 0, 0, False))
            act.wait_ge(av_done, CHUNKS)
            for e in range(E):
                gelu(Chunk(0, 0, 0, False), e)
            moe_x16(Chunk(1, 1, 1, False))
            all_chunks(act, moe_body)

            def soft_x16(ck):
                act.wait_ge(x16_turned, ck.c + 2 * CHUNKS + 1)
                if ck.looped or ck.c >= 2:
                    act.wait_ge(ring_full, ring.filled(ck, "soft", "v", 2))
                copy(x16[:, ck.u, :], bank[6][:, :].bitcast(F16)[:, 0:CN]).then_inc(x16_ready, 1)

            def soft_exp(ck):
                ring.wait_emptied(act, ck, "soft", "s")
                if ck.looped or ck.c >= 2:
                    act.wait_ge(ring_full, ring.filled(ck, "soft", "pt", 2))
                    act.wait_ge(sm_sum, ck.c - 1)
                nc.scalar.activation(pr[:, ck.u, :], sc[:, :], ACT.Exp, scale=1.0 / D).then_inc(sm_exp, 1)

            def soft_body(ck):
                act.wait_ge(ring_full, ring.filled(ck, "soft", "pt"))
                if ck.looped or ck.c >= 1:
                    act.wait_ge(ring_full, ring.filled(ck, "soft", "o", 1))
                copy(pT[:, :], bank_of(ck, "soft", "pt")[:, 0:256]).then_inc(act_emptied, 1)
                if ck.looped or ck.c + 2 < CHUNKS:
                    soft_x16(Chunk(ck.c + 2, ck.u, ck.near + 2, ck.looped))
                if ck.looped or ck.c + 1 < CHUNKS:
                    soft_exp(Chunk(ck.c + 1, 1 - ck.u, ck.near + 1, ck.looped))

            act.wait_ge(ring_full, ring.fills(ring.index["up", CHUNKS - 1, "e7"]))
            soft_x16(Chunk(0, 0, 0, False))
            soft_exp(Chunk(0, 0, 0, False))
            soft_x16(Chunk(1, 1, 1, False))
            all_chunks(act, soft_body)

            def bn_square(ck):
                act.wait_ge(bn_cent, ck.c + 1)
                if ck.looped or ck.c >= 2:
                    act.wait_ge(bn_var, ck.c - 1)
                nc.scalar.activation(sq[:, ck.u, 0:CT * D].rearrange("p (t d) -> p t d", t=CT), tiles_of(ao, ck),
                                     ACT.Square).then_inc(bn_sq, 1)

            all_chunks(act, bn_square)

            def dense_x16(ck):
                act.wait_ge(x16_turned, ck.c + 3 * CHUNKS + 1)
                dst = x16all[:, ck.c * CN:ck.c * CN + CN] if not ck.looped else x16all[:, DS(ck.c * CN, CN)]
                copy(dst, bank[6][:, :].bitcast(F16)[:, 0:CN]).then_inc(x16_ready, 1)

            all_chunks(act, dense_x16)

            act.wait_ge(gate_step, GATE_SHIFTED)
            nc.scalar.activation(gl[:, 2, :], gl[:, 1, :], ACT.Exp, accum_out=gs[:, 1:2]).then_inc(gate_exp, 1)

            def dense_relu(ck, stage, k, dst, bias):
                act.wait_ge(ring_full, ring.filled(ck, stage, f"p{k}"))
                nc.scalar.activation(dst, bank_of(ck, stage, f"p{k}")[:, :], ACT.Relu, bias=bias
                                     ).then_inc(act_emptied, 1)

            def dense_body(ck):
                if ck.looped or ck.c >= 2:
                    act.wait_ge(weighed, ck.c * 4 - 4)
                for k in range(4):
                    if ring_who("one", k) == "A" and (ck.looped or ck.c + 1 < CHUNKS):
                        dense_relu(Chunk(ck.c + 1, 1 - ck.u, ck.near + 1, ck.looped), "one", k,
                                   h1[:, 1 - ck.u, k, :], t12[:, 0, k:k + 1])
                    if ring_who("two", k) == "A":
                        dense_relu(ck, "two", k, h2[:, ck.u, k, :], t12[:, 1, k:k + 1])

            for k in range(4):
                if ring_who("one", k) == "A":
                    dense_relu(Chunk(0, 0, 0, False), "one", k, h1[:, 0, k, :], t12[:, 0, k:k + 1])
            all_chunks(act, dense_body)

        @block.vector
        def _(dve):
            v = nc.vector
            step = [0]

            def link(ins):
                step[0] += 1
                ins.then_inc(prep_dve, 1)
                dve.wait_ge(prep_dve, step[0])

            link(v.memset(ftok[:, :, :], 1.0))
            assert step[0] == FTOK_ONES
            dve.wait_ge(s_const, 16)
            link(v.tensor_copy(ident16[:, :], ident))

            def prep_turned():
                dve.wait_ge(s_wf, LOADS)
                for w in range(3):
                    link(v.tensor_copy(permqkv[:, w].rearrange("g a (e k) -> g a e k", e=2),
                                       rawqkv[:, w, :].rearrange("g (k a e) -> g a e k", a=4, e=2)))
                assert step[0] == PERMUTED
                dve.wait_ge(prep_pe, 1)
                for w in (0, 1):
                    for c in (0, 1):
                        link(v.tensor_copy(wT[:, w, :, c, :],
                                           bank[6][:, 256 * w:256 * w + 256].rearrange("p (a g) -> p a g", a=4)))
                dve.wait_ge(prep_pe, 2)
                for c in (0, 1):
                    link(v.tensor_copy(wT[:, 2, :, c, :], bank[7][:, 0:256].rearrange("p (a g) -> p a g", a=4)))
                    link(v.tensor_copy(wv1T[:, c, :], bank[7][0:D, 256:320]))
                link(v.tensor_copy(cols[:, :], bank[7][:, 320:368]))
                link(v.tensor_copy(bv_b[:, :], bc(bv_c[:, 0:1], [D, P])))
                link(v.tensor_copy(beta0_b[:, :], bc(beta0[:, 0:1], [D, P])))
                assert step[0] == TURNED_READY
                link(v.tensor_scalar(seg(wcat, "W1"), w1raw[:, :], gamma0[:, 0:1], None, ALU.mult))
                link(v.tensor_scalar(seg(wcat, "R"), wrraw[:, :], gamma0[:, 0:1], None, ALU.mult))
                link(v.tensor_scalar(s1row[:, :], bnrow[:, 1, :], BN_EPS_FFN, None, ALU.add))
                link(v.tensor_scalar(s2row[:, :, :], bnrow2[:, 1], BN_EPS_FFN, None, ALU.add))
                for l in (0, 1):
                    link(v.tensor_scalar(tmp4[:, l, :], cols[:, 20 * l + 16:20 * l + 20], BN_EPS_FFN, None, ALU.add))
                assert step[0] == EPS_ADDED
                dve.wait_ge(prep_pool, POOL_CONSTS + 3)
                link(v.tensor_tensor(s1row[:, :], s1row[:, :], bnrow[:, 0, :], ALU.mult))
                link(v.tensor_tensor(seg(wcat, "U"), u1raw[:, :, :].rearrange("p e n -> p (e n)"), s1row[:, :], ALU.mult))
                link(v.tensor_tensor(s2row[:, :, :], s2row[:, :, :], bnrow2[:, 0], ALU.mult))
                for l in (0, 1):
                    b_, g_, be_, m_ = (cols[:, 20 * l + 4 * k:20 * l + 4 * k + 4] for k in range(4))
                    link(v.tensor_tensor(tmp4[:, l, :], tmp4[:, l, :], g_, ALU.mult))
                    link(v.tensor_tensor(tmp4[:, 2, :], b_, m_, ALU.subtract))
                    link(v.tensor_tensor(tmp4[:, 2, :], tmp4[:, 2, :], tmp4[:, l, :], ALU.mult))
                    link(v.tensor_tensor(t12[:, l, :], tmp4[:, 2, :], be_, ALU.add))

            def prep_products():
                dve.wait_ge(prep_pe, 4)
                link(v.tensor_copy(seg(wcat, "M"), bank[6][:, :]))
                link(v.tensor_copy(seg(wcat, "N"), bank[7][:, :]))
                assert step[0] == PRODUCTS_READY

            def prep_small():
                dve.wait_ge(prep_pe, 5)
                link(v.tensor_copy(seg(wcat, "V"), bank[7][:, 0:D]))
                link(v.tensor_tensor(vbias[:, :], bank[7][:, 64:128], bl_b[:, :], ALU.add))
                link(v.tensor_tensor(br_b[:, :], bank[7][:, 128:128 + E], br_b[:, :], ALU.add))
                link(v.tensor_tensor(b1c[:, :], bank[7][:, 192:192 + E], cols[:, 40:48], ALU.add))
                for k, name in enumerate(SEGS):
                    link(v.tensor_reduce(wmax[:, 0, k:k + 1], seg(wcat, name), AX.X, ALU.max, apply_absolute_value=True))
                assert step[0] == WMAX_READY

            def prep_split():
                dve.wait_ge(prep_pool, POOL_CONSTS + 4)
                link(v.tensor_scalar(wscale[:, :], wmax[:, 1, :], 2.0 ** -100, 2.0 ** 100, ALU.max, ALU.min))
                link(v.tensor_scalar(wscale[:, :].bitcast(I32), wscale[:, :].bitcast(I32), 0x7F800000, None,
                                     ALU.bitwise_and))
                link(v.reciprocal(winv[:, :], wscale[:, :]))
                for name in SEGS:
                    link(v.tensor_scalar(seg(wcat, name), seg(wcat, name), scale_of(winv, name), None, ALU.mult))
                link(v.tensor_copy(whi[:, :], wcat[:, :]))
                link(v.tensor_tensor(wlo[:, :], wcat[:, :], whi[:, :], ALU.subtract))
                link(v.tensor_scalar(sig_scale[:, :], scale_of(wscale, "M"), 8.0, None, ALU.mult))
                link(v.tensor_scalar(t12[:, 0, :], t12[:, 0, :], scale_of(winv, "U"), None, ALU.mult))
                link(v.tensor_scalar(s2row[:, :, :], s2row[:, :, :], scale_of(wscale, "U"), None, ALU.mult))
                link(v.tensor_tensor(u2[:, :, :], u2raw[:, :, :], s2row[:, :, :], ALU.mult))
                assert step[0] == SPLIT_READY

            def tok_maps(g):
                dve.wait_ge(maps_done, g + 1)
                if g >= 2:
                    dve.wait_ge(ft_done, g - 1)
                v.tensor_copy(fbuf[:, g % 2, :], bank[2][:, 0:56]).then_inc(maps_copied, 1)

            def tok_h(g):
                dve.wait_ge(tok_done, g + 1)
                n = GROUP // 2
                v.tensor_copy(h[:, g * n:(g + 1) * n, :].rearrange("p t d -> p (t d)"), bank[3][:, :]
                              ).then_inc(h_ready, 1)

            tok_maps(0)
            for g in range(GROUPS):
                if g + 1 < GROUPS:
                    tok_maps(g + 1)
                tok_h(g)
                if g in PREP_AT:
                    (prep_turned, prep_products, prep_small, prep_split)[PREP_AT.index(g)]()

            def statistics(ck, n, ready=None):
                if ready:
                    wait_apart(dve, *ready)
                for t in range(CT):
                    src = h[:, ck.c * CT + t, :] if not ck.looped else h[:, DS(ck.c * CT + t, 1), :]
                    v.bn_stats(st[:, t, :], src).then_inc(ln_stats, 1)
                wait_apart(dve, ln_stats, n * CT + CT)
                wait_apart(dve, n_scaled, n)
                for t in range(CT):
                    last = v.bn_aggr(mv[:, t, :], st[:, t, :])
                last.then_inc(ln_aggr, 1)
                dve.wait_ge(ln_aggr, n + 1)

            def att_empty(ck, name, dst):
                dve.wait_ge(ring_full, ring.filled(ck, "att", name))
                v.tensor_copy(dst, bank_of(ck, "att", name)[:, :]).then_inc(dve_emptied, 1)

            def att_x32(ck):
                dve.wait_ge(x32_turned, ck.c + 1)
                if ck.looped or ck.c >= 2:
                    dve.wait_ge(av_done, ck.c - 1)
                v.tensor_copy(x32[:, ck.u, :], bank[6][:, :]).then_inc(x32_ready, 1)

            def attention_body(ck):
                wait_if(dve, av_done, ck.c)
                for k, (name, who) in enumerate(ATT_Q):
                    if who == "V":
                        att_empty(ck, name, qbuf[:, k, :])
                if ck.looped or ck.c + 2 < CHUNKS:
                    statistics(Chunk(ck.c + 2, ck.u, ck.near + 2, ck.looped), ck.c + 2)
                for t, (name, who) in enumerate(ATT_V):
                    if who == "V":
                        att_empty(ck, name, vbuf[:, t, :])
                if ck.looped or ck.c + 1 < CHUNKS:
                    att_x32(Chunk(ck.c + 1, 1 - ck.u, ck.near + 1, ck.looped))

            dve.wait_ge(h_ready, GROUPS)
            statistics(Chunk(0, 0, 0, False), 0)
            statistics(Chunk(1, 1, 1, False), 1)
            att_x32(Chunk(0, 0, 0, False))
            all_chunks(dve, attention_body)

            def stats_moe(ck):
                statistics(ck, ck.c + CHUNKS, (att_added, ck.c + 1))

            def router(ck):
                k = [0]
                base = ck.c * RT_STEPS

                def rt(ins):
                    k[0] += 1
                    ins.then_inc(rt_step, 1)
                    dve.wait_ge(rt_step, base + k[0])

                L, Q, one, two = lg[:, 0], lg[:, 1], lg[:, 2], lg[:, 3]
                wide = [P, CT, E]
                dve.wait_ge(rt_done, ck.c + 1)
                rt(v.scalar_tensor_tensor(out=L, in0=bank[7][:, 0:CT * E].rearrange("p (t e) -> p t e", t=CT),
                                          scalar=scale_of(wscale, "R"), in1=bc(br_b[:, :].unsqueeze(1), wide),
                                          op0=ALU.mult, op1=ALU.add))
                for r, (src, hot) in enumerate(((L, one), (Q, two))):
                    rt(v.tensor_reduce(top[:, r, :], src, AX.X, ALU.max))
                    rt(v.tensor_tensor(lg[:, 4], src, bc(top[:, r, :].unsqueeze(2), wide), ALU.is_lt))
                    rt(v.scalar_tensor_tensor(out=lg[:, 5], in0=lg[:, 4], scalar=float(E), in1=iota[:, :, :],
                                              op0=ALU.mult, op1=ALU.add))
                    rt(v.tensor_reduce(top[:, 4 + r, :], lg[:, 5], AX.X, ALU.min))
                    rt(v.tensor_tensor(hot, iota[:, :, :], bc(top[:, 4 + r, :].unsqueeze(2), wide), ALU.is_equal))
                    if r == 0:
                        rt(v.scalar_tensor_tensor(out=Q, in0=hot, scalar=-3.0e38, in1=L, op0=ALU.mult, op1=ALU.add))
                rt(v.tensor_tensor(top[:, 2, :], top[:, 0, :], top[:, 1, :], ALU.subtract))
                assert k[0] == RT_TANH
                dve.wait_ge(rt_tanh, ck.c + 1)
                rt(v.tensor_scalar(top[:, 6, :], top[:, 3, :], 0.5, 0.5, ALU.mult, ALU.add))
                rt(v.tensor_scalar(top[:, 7, :], top[:, 3, :], -0.5, 0.5, ALU.mult, ALU.add))
                rt(v.tensor_tensor(lg[:, 6], one, bc(top[:, 6, :].unsqueeze(2), wide), ALU.mult))
                rt(v.tensor_tensor(lg[:, 7], two, bc(top[:, 7, :].unsqueeze(2), wide), ALU.mult))
                rt(v.tensor_tensor(lg[:, 8 + ck.u], lg[:, 6], lg[:, 7], ALU.add))
                assert k[0] == RT_STEPS

            def router_turned(ck):
                dve.wait_ge(wt_turned, ck.c + 1)
                v.tensor_copy(wtT[:, :], bank[7][0:CT * E, 128:256]).then_inc(wt_ready, 1)

            def router_b2(ck):
                dve.wait_ge(b2_done, ck.c + 1)
                v.tensor_tensor(tiles_of(h, ck), tiles_of(h, ck), bank[7][:, 256:512].rearrange("p (t d) -> p t d", t=CT),
                                ALU.add).then_inc(b2_added, 1)

            def moe_body(ck):
                nx = Chunk(ck.c + 1, 1 - ck.u, ck.near + 1, ck.looped)
                more = ck.looped or ck.c + 1 < CHUNKS
                if ck.looped or ck.c + 2 < CHUNKS:
                    stats_moe(Chunk(ck.c + 2, ck.u, ck.near + 2, ck.looped))
                if more:
                    router(nx)
                wait_if(dve, tree_step, ck.c * 3 - 2)
                for t in range(CT):
                    if t == 2 and more:
                        router_turned(nx)
                    if t == 3 and more:
                        router_b2(nx)
                    dve.wait_ge(ring_full, ring.filled(ck, "down", f"t{t}"))
                    v.tensor_tensor(prod[:, t], bank_of(ck, "down", f"t{t}")[:, :].rearrange("p (e d) -> p e d", e=E),
                                    bc(lg[:, 8 + ck.u, t, :].unsqueeze(2), [P, E, D]), ALU.mult)\
                        .then_inc(dve_emptied, 1)

            for c in range(2):
                stats_moe(Chunk(c, c % 2, c, False))
            c0 = Chunk(0, 0, 0, False)
            router(c0)
            router_turned(c0)
            router_b2(c0)
            all_chunks(dve, moe_body)

            def stats_soft(ck):
                statistics(ck, ck.c + 2 * CHUNKS, (moe_added, ck.c + 1))

            def soft_proj(ck):
                dve.wait_ge(ring_full, ring.filled(ck, "soft", "qk"))
                if ck.looped or ck.c >= 2:
                    dve.wait_ge(ring_full, ring.filled(ck, "soft", "s", 2))
                for k, name in enumerate("QK"):
                    last = v.tensor_scalar(qk[:, ck.u, k, :], bank_of(ck, "soft", "qk")[:, 256 * k:256 * k + 256],
                                           scale_of(wscale, name), bqk[:, k:k + 1], ALU.mult, ALU.add)
                last.then_inc(dve_emptied, 1)
                dve.wait_ge(ring_full, ring.filled(ck, "soft", "v"))
                if ck.looped or ck.c >= 2:
                    dve.wait_ge(ring_full, ring.filled(ck, "soft", "o", 2))
                v.scalar_tensor_tensor(out=vv[:, ck.u].rearrange("p (t d) -> p t d", d=D),
                                       in0=bank_of(ck, "soft", "v")[:, 0:256].rearrange("p (t d) -> p t d", d=D),
                                       scalar=scale_of(wscale, "V"), in1=bc(vbias[:, :].unsqueeze(1), [P, CT, D]),
                                       op0=ALU.mult, op1=ALU.add).then_inc(dve_emptied, 1)

            def soft_shift(ck):
                s = bank_of(ck, "soft", "s")[:, 0:256].rearrange("p (t j) -> p t j", t=CT)
                dve.wait_ge(ring_full, ring.filled(ck, "soft", "s"))
                v.tensor_reduce(mx[:, ck.u, :], s, AX.X, ALU.max).then_inc(sm_max, 1)
                dve.wait_ge(sm_max, ck.c + 1)
                wait_if(dve, sm_exp, ck.c)
                v.tensor_tensor(sc[:, :].rearrange("p (t j) -> p t j", t=CT), s,
                                bc(mx[:, ck.u, :].unsqueeze(2), [P, CT, S]), ALU.subtract).then_inc(dve_emptied, 1)

            def soft_sum(ck):
                dve.wait_ge(sm_exp, ck.c + 1)
                v.tensor_reduce(rs[:, 0, :], pr[:, ck.u, :].rearrange("p (t j) -> p t j", t=CT), AX.X, ALU.add
                                ).then_inc(sm_sum, 1)
                dve.wait_ge(sm_sum, ck.c + 1)
                v.reciprocal(rs[:, 1, :], rs[:, 0, :]).then_inc(sm_inv, 1)

            def soft_body(ck):
                nx = Chunk(ck.c + 1, 1 - ck.u, ck.near + 1, ck.looped)
                more = ck.looped or ck.c + 1 < CHUNKS
                if ck.looped or ck.c + 2 < CHUNKS:
                    stats_soft(Chunk(ck.c + 2, ck.u, ck.near + 2, ck.looped))
                soft_sum(ck)
                if more:
                    soft_proj(nx)
                    soft_shift(nx)
                dve.wait_ge(ring_full, ring.filled(ck, "soft", "o"))
                dve.wait_ge(sm_inv, ck.c + 1)
                v.tensor_tensor(tiles_of(ao, ck), bank_of(ck, "soft", "o")[:, 0:256].rearrange("p (t d) -> p t d", d=D),
                                bc(rs[:, 1, :].unsqueeze(2), [P, CT, D]), ALU.mult).then_inc(dve_emptied, 1)

            for c in range(2):
                stats_soft(Chunk(c, c % 2, c, False))
            dve.wait_ge(moe_added, CHUNKS)
            soft_proj(Chunk(0, 0, 0, False))
            soft_shift(Chunk(0, 0, 0, False))
            all_chunks(dve, soft_body)

            N = float(B * S)
            s4 = bank[7][:, 0:CT * D].rearrange("p (t d) -> p d t", t=CT)
            k = step[0]
            dve.wait_ge(bn_sum, CHUNKS)
            link(v.tensor_reduce(mean_b[:, :], s4, AX.X, ALU.add))
            v.tensor_scalar(mean_b[:, :], mean_b[:, :], 1.0 / N, None, ALU.mult).then_inc(bn_mean, 1)
            dve.wait_ge(bn_var, CHUNKS)
            link(v.tensor_reduce(bnA[:, :], s4, AX.X, ALU.add))
            v.tensor_scalar(bnA[:, :], bnA[:, :], 1.0 / N, BN_EPS_ATT, ALU.mult, ALU.add).then_inc(bn_eps, 1)
            dve.wait_ge(bn_root, 1)
            v.tensor_tensor(bnA[:, :], bnA[:, :], bn_g[:, :], ALU.mult).then_inc(bn_coef, 1)

            def bn_add(ck):
                dve.wait_ge(bn_app, ck.c + 1)
                v.tensor_tensor(tiles_of(ao, ck), tiles_of(ao, ck), bc(bn_b[:, :].unsqueeze(1), [P, CT, D]), ALU.add
                                ).then_inc(bn_step, 1)
                dve.wait_ge(bn_step, ck.c * 2 + 1)
                v.scalar_tensor_tensor(out=tiles_of(h, ck), in0=tiles_of(ao, ck), scalar=0.0, in1=tiles_of(h, ck),
                                       op0=ALU.max, op1=ALU.add).then_inc(bn_step, 1)
                statistics(ck, ck.c + 3 * CHUNKS, (bn_step, ck.c * 2 + 2))

            dve.wait_ge(hx_added, CHUNKS)
            all_chunks(dve, bn_add)

            g = [0]

            def gate(ins):
                g[0] += 1
                ins.then_inc(gate_step, 1)
                dve.wait_ge(gate_step, g[0])

            dve.wait_ge(feat_done, CHUNKS)
            gate(v.tensor_scalar(feat[:, :], bank[7][0:D, 0:S], 1.0 / B, None, ALU.mult))
            dve.wait_ge(gate_pe, 1)
            gate(v.tensor_tensor(gl[:, 0, :], bank[6][0:S, 0:E], br1_b[:, :], ALU.add))
            gate(v.tensor_reduce(gs[:, 0:1], gl[:, 0, :], AX.X, ALU.max))
            gate(v.tensor_scalar(gl[:, 1, :], gl[:, 0, :], gs[:, 0:1], None, ALU.subtract))
            assert g[0] == GATE_SHIFTED
            dve.wait_ge(gate_exp, 1)
            gate(v.reciprocal(gs[:, 2:3], gs[:, 1:2]))
            gate(v.tensor_scalar(gl[:, 3, :], gl[:, 2, :], gs[:, 2:3], None, ALU.mult))
            gate(v.tensor_copy(gwx[:, :, :], bc(gl[:, 3, :].unsqueeze(2), [S, E, D])))
            dve.wait_ge(gate_pe, 2)
            gate(v.tensor_copy(gwT[:, 0, :], bank[6][0:E, 256:256 + S]))
            gate(v.tensor_copy(gwT[:, 1, :], bank[6][0:E, 256:256 + S]))
            gate(v.tensor_copy(gwb[:, :, :], bank[7][:, 0:4 * S].rearrange("p (a f) -> p a f", a=4)))
            dve.wait_ge(gate_pe, 3)
            gate(v.tensor_copy(bow[:, :], bank[6][:, 384:384 + D]))
            assert g[0] == GATE_STEPS

            def dense_relu(ck, stage, k, dst, bias):
                dve.wait_ge(ring_full, ring.filled(ck, stage, f"p{k}"))
                v.tensor_scalar(dst, bank_of(ck, stage, f"p{k}")[:, :], bias, 0.0, ALU.add, ALU.max
                                ).then_inc(dve_emptied, 1)

            def third(ck):
                dve.wait_ge(ring_full, ring.filled(ck, "three", "y"))
                dve.wait_ge(bow_added, ck.c + 1)
                v.tensor_tensor(tiles_of(h, ck), tiles_of(h, ck),
                                bank_of(ck, "three", "y")[:, 0:CT * D].rearrange("p (t d) -> p t d", t=CT), ALU.add
                                ).then_inc(dve_emptied, 1)

            def dense_body(ck):
                if ck.looped or ck.c >= 2:
                    dve.wait_ge(weighed, ck.c * 4 - 4)
                for k in range(4):
                    if ring_who("one", k) == "V" and (ck.looped or ck.c + 1 < CHUNKS):
                        dense_relu(Chunk(ck.c + 1, 1 - ck.u, ck.near + 1, ck.looped), "one", k,
                                   h1[:, 1 - ck.u, k, :], t12[:, 0, k:k + 1])
                    if ring_who("two", k) == "V":
                        dense_relu(ck, "two", k, h2[:, ck.u, k, :], t12[:, 1, k:k + 1])
                    if k == 1 and (ck.looped or ck.c >= 1):
                        third(three_chunk(ck))

            for k in range(4):
                if ring_who("one", k) == "V":
                    dense_relu(Chunk(0, 0, 0, False), "one", k, h1[:, 0, k, :], t12[:, 0, k:k + 1])
            all_chunks(dve, dense_body)
            third(Chunk(CHUNKS - 1, 1, CHUNKS - 1, False))

        @block.tensor
        def _(pe):
            mm = nc.tensor.matmul

            def fmm(out, lhsT, rhs, start=True, stop=True):
                return mm(out, lhsT, rhs, start=start, stop=stop)

            def two_pass(out, xs, name, lo, hi, x_moving):
                a = SEG[name][0]
                for i, w in enumerate((whi, wlo)):
                    wp = w[:, a + lo:a + hi]
                    last = fmm(out, wp if x_moving else xs, xs if x_moving else wp, start=(i == 0), stop=(i == 1))
                return last

            pe.wait_ge(s_const, 16)

            def prep_turn():
                pe.wait_ge(s_wf, LOADS)
                pe.wait_ge(prep_pool, POOL_CONSTS)

                pe.wait_ge(prep_dve, PERMUTED)

                for w in (0, 1):
                    for a in range(4):
                        last = nc.tensor.transpose(bank[6][:, 256 * w + 64 * a:256 * w + 64 * a + 64], permqkv[:, w, a, :],
                                                   ident[0:D, 0:D])
                last.then_inc(prep_pe, 1)
                for a in range(4):
                    nc.tensor.transpose(bank[7][:, 64 * a:64 * a + 64], permqkv[:, 2, a, :], ident[0:D, 0:D])
                nc.tensor.transpose(bank[7][0:D, 256:320], wv1raw[:, :], ident[0:D, 0:D])
                nc.tensor.transpose(bank[7][:, 320:368], rows[:, :], ident[0:48, 0:48]).then_inc(prep_pe, 1)

            def prep_products():
                pe.wait_ge(prep_dve, TURNED_READY)
                for e2 in (0, 1):
                    if e2 == 1:
                        pe.wait_ge(prep_pe, 3)
                    half = slice(64 * e2, 64 * e2 + 64)
                    for a in range(4):
                        hd = 2 * a + e2
                        fmm(bank[6][:, 64 * hd:64 * hd + 64], wT[half, 0, a].rearrange("p c g -> p (c g)"),
                            wT[half, 1, a, 0, :])
                        last = fmm(bank[7][:, (4 * e2 + a) * 64:(4 * e2 + a) * 64 + 64],
                                   wT[half, 2, a].rearrange("p c g -> p (c g)"), wo_a[half, hd, :])
                    last.then_inc(prep_pe, 1)

            def prep_small():
                pe.wait_ge(prep_dve, PRODUCTS_READY)
                fmm(bank[7][:, 0:D], wv1T[:, :, :].rearrange("p c g -> p (c g)"), wl1[:, :])
                fmm(bank[7][:, 64:128], bv_b[:, :], wl1[:, :])
                fmm(bank[7][:, 128:128 + E], beta0_b[:, :], wrraw[0:D, :])
                for e in range(E):
                    last = fmm(bank[7][:, 192 + e:193 + e], w1raw[0:D, H0 * e:H0 * e + H0], beta0[:, 0:1])
                last.then_inc(prep_pe, 1)

            def tok_rows(g):
                u = g % 2
                pe.wait_ge(s_img[g % 4], 16 * (g // 4 + 1))
                if g >= 2:
                    pe.wait_ge(z_copied, g - 1)
                for b in range(GROUP):
                    last = fmm(bank[u][0:R, 32 * b:32 * b + 32], img[:, g % 4, b, :], resize)
                last.then_inc(rows_done, 1)

            MAPS = ((0, 16, 0), (0, 16, 16), (24, 32, 32), (16, 32, 40))

            def tok_maps(g):
                u = g % 2
                pe.wait_ge(z_copied, g + 1)
                wait_if(pe, maps_copied, g)
                for o, (lo, hi, at) in enumerate(MAPS):
                    last = fmm(bank[2][:, at:at + hi - lo], zbuf[:, u, o, :], resize[:, lo:hi])
                last.then_inc(maps_done, 1)

            def tok_turn(g):
                u = g % 2
                pe.wait_ge(maps_copied, g + 1)
                if g >= 1:
                    pe.wait_ge(ft_copied, g)
                for j in range(8):
                    last = nc.tensor.transpose(bank[4 + j // 4][0:NMAPS, 128 * (j % 4):128 * (j % 4) + 128],
                                               fbuf[:, u, :].rearrange("p (m j) -> p j m", j=8)[:, j, :], ident)
                last.then_inc(ft_done, 1)

            def tok_project(g):
                u = g % 2
                pe.wait_ge(ft_copied, g + 1)
                if g >= 1:
                    pe.wait_ge(h_ready, g)
                for t in range(GROUP // 2):
                    last = fmm(bank[3][:, 64 * t:64 * t + 64], ftok[:, u, P * t:P * t + P], wb[:, :])
                last.then_inc(tok_done, 1)

            pe.wait_ge(s_wa, 16 * len(TOKEN_W_LOADS))
            tok_rows(0)
            tok_maps(0)
            for g in range(GROUPS):
                if g + 1 < GROUPS:
                    tok_rows(g + 1)
                tok_turn(g)
                tok_project(g)
                if g + 1 < GROUPS:
                    tok_maps(g + 1)
                if g in PREP_AT[:3]:
                    (prep_turn, prep_products, prep_small)[PREP_AT.index(g)]()

            def turn16(dst, n, split_value):
                pe.wait_ge(n_split, split_value)
                d = dst[:, :].bitcast(F16)
                for t in range(CT):
                    last = nc.tensor.transpose(d[:, P * t:P * t + P], xcat[:, t, :], ident16[:, :])
                return last

            def att_turn16(ck):
                wait_if(pe, x32_ready, ck.c)
                turn16(bank[6], ck.c, ck.c + 1).then_inc(x16_turned, 1)

            def att_turn32(ck):
                pe.wait_ge(x16_ready, ck.c + 1)
                for t in range(CT):
                    last = nc.tensor.transpose(bank[6][:, P * t:P * t + P],
                                               xn[:, t, :, :].rearrange("p c d -> p (c d)"), ident)
                last.then_inc(x32_turned, 1)

            def attention_body(ck):
                more = ck.looped or ck.c + 1 < CHUNKS
                nx = Chunk(ck.c + 1, 1 - ck.u, ck.near + 1, ck.looped)
                xs = x16[:, ck.u, :]
                pe.wait_ge(x16_ready, ck.c + 1)
                for a in range(4):
                    ring.wait_free(pe, ck, "att", f"q{a}")
                    two_pass(bank_of(ck, "att", f"q{a}")[:, :], xs, "M", P * a, P * a + P, True
                             ).then_inc(ring_full, 1)
                if more:
                    att_turn16(nx)
                for t in range(CT):
                    ring.wait_free(pe, ck, "att", f"v{t}")
                    bk = bank_of(ck, "att", f"v{t}")
                    for b in (0, 1):
                        xb = xs[:, P * t + S * b:P * t + S * b + S]
                        for i, w in enumerate((whi, wlo)):
                            for e2 in (0, 1):
                                a0 = SEG["N"][0] + 256 * e2
                                last = fmm(bk[64 * e2:64 * e2 + 64, 256 * b:256 * b + 256], xb, w[:, a0:a0 + 256],
                                           start=(i == 0), stop=(i == 1))
                    last.then_inc(ring_full, 1)
                if more:
                    att_turn32(nx)
                pe.wait_ge(x32_ready, ck.c + 1)
                for a in range(4):
                    ring.wait_emptied(pe, ck, "att", f"q{a}", wait_apart)
                for t in range(CT):
                    ring.wait_free(pe, ck, "att", f"s{t}", wait_apart)
                    bk = bank_of(ck, "att", f"s{t}")
                    for b in (0, 1):
                        at = P * t + S * b
                        for e2 in (0, 1):
                            half = slice(64 * e2, 64 * e2 + 64)
                            last = fmm(bk[half, 256 * b:256 * b + 256], x32[half, ck.u, at:at + S],
                                       qbuf[half, :, at:at + S])
                    last.then_inc(ring_full, 1)
                wait_if(pe, av_relu, ck.c)
                for t in range(CT):
                    ring.wait_emptied(pe, ck, "att", f"v{t}")
                    ring.wait_emptied(pe, ck, "att", f"s{t}")
                    for a in range(4):
                        for b in (0, 1):
                            cs = slice(256 * b + 64 * a, 256 * b + 64 * a + 64)
                            last = fmm(bank[7][64 * b:64 * b + 64, D * t:D * t + D], abuf[:, t, cs], vbuf[:, t, cs],
                                       start=(a == 0), stop=(a == 3))
                last.then_inc(av_done, 1)

            pe.wait_ge(prep_dve, SPLIT_READY)
            pe.wait_ge(h_ready, GROUPS)
            att_turn16(Chunk(0, 0, 0, False))
            att_turn32(Chunk(0, 0, 0, False))
            all_chunks(pe, attention_body)

            def moe_turn(ck):
                if not ck.looped and ck.c == 0:
                    pe.wait_ge(x32_ready, CHUNKS)
                pe.wait_ge(x16_ready, ck.c + CHUNKS)
                turn16(bank[6], ck.c, ck.c + CHUNKS + 1).then_inc(x16_turned, 1)

            def moe_router(ck):
                pe.wait_ge(x16_ready, ck.c + CHUNKS + 1)
                wait_if(pe, b2_added, ck.c)
                for t in range(CT):
                    last = two_pass(bank[7][:, E * t:E * t + E], x16[:, ck.u, P * t:P * t + P], "R", 0, E, False)
                last.then_inc(rt_done, 1)

            def moe_up(ck, e):
                ring.wait_free(pe, ck, "up", f"e{e}")
                two_pass(bank_of(ck, "up", f"e{e}")[:, :], x16[:, ck.u, :], "W1", H0 * e, H0 * e + H0, True
                         ).then_inc(ring_full, 1)

            def moe_b2_turn(ck):
                pe.wait_ge(rt_step, ck.c * RT_STEPS + RT_STEPS)
                nc.tensor.transpose(bank[7][0:CT * E, 128:256], lg[:, 8 + ck.u].rearrange("p t e -> p (t e)"), ident
                                    ).then_inc(wt_turned, 1)

            def moe_b2(ck):
                pe.wait_ge(wt_ready, ck.c + 1)
                fmm(bank[7][:, 256:512], wtT[:, :], b2blk[:, :]).then_inc(b2_done, 1)

            def moe_down(ck, t):
                ring.wait_free(pe, ck, "down", f"t{t}")
                for e in range(E):
                    last = fmm(bank_of(ck, "down", f"t{t}")[:, D * e:D * e + D], gbuf[:, ck.u, e, P * t:P * t + P],
                               w2[:, e, :])
                last.then_inc(ring_full, 1)

            def moe_body(ck):
                more = ck.looped or ck.c + 1 < CHUNKS
                nx = Chunk(ck.c + 1, 1 - ck.u, ck.near + 1, ck.looped)
                if more:
                    moe_router(nx)
                for t in range(CT):
                    if more:
                        moe_up(nx, 2 * t)
                        moe_up(nx, 2 * t + 1)
                    if t == 0:
                        ring.wait_emptied(pe, ck, "up", f"e{E - 1}")
                    moe_down(ck, t)
                    if t == 1 and more:
                        moe_b2_turn(nx)
                    if t == 2 and more:
                        moe_b2(nx)
                    if t == 2 and (ck.looped or ck.c + 2 < CHUNKS):
                        moe_turn(Chunk(ck.c + 2, ck.u, ck.near + 2, ck.looped))

            c0 = Chunk(0, 0, 0, False)
            pe.wait_ge(av_relu, CHUNKS)
            moe_turn(c0)
            moe_router(c0)
            for e in range(E):
                moe_up(c0, e)
            moe_turn(Chunk(1, 1, 1, False))
            moe_b2_turn(c0)
            pe.wait_ge(s_b2, 16 * len(B2_LOADS))
            moe_b2(c0)
            all_chunks(pe, moe_body)

            def soft_turn(ck):
                pe.wait_ge(x16_ready, ck.c + 2 * CHUNKS)
                turn16(bank[6], ck.c, ck.c + 2 * CHUNKS + 1).then_inc(x16_turned, 1)

            def soft_proj(ck):
                pe.wait_ge(x16_ready, ck.c + 2 * CHUNKS + 1)
                xs = x16[:, ck.u, :].rearrange("p (t b i) -> p t b i", t=CT, b=2)
                ring.wait_free(pe, ck, "soft", "qk")
                bk = bank_of(ck, "soft", "qk")
                for k, name in enumerate("QK"):
                    a = SEG[name][0]
                    for i, w in enumerate((whi, wlo)):
                        for b in (0, 1):
                            last = fmm(bk[64 * b:64 * b + 64, 256 * k:256 * k + 256], w[:, a:a + D], xs[:, :, b, :],
                                       start=(i == 0), stop=(i == 1))
                last.then_inc(ring_full, 1)
                ring.wait_free(pe, ck, "soft", "v")
                bk = bank_of(ck, "soft", "v")
                a = SEG["V"][0]
                for th in (0, 1):
                    for b in (0, 1):
                        for i, w in enumerate((whi, wlo)):
                            for t2 in (0, 1):
                                at = 128 * th + 64 * b
                                last = fmm(bk[64 * t2:64 * t2 + 64, at:at + 64], xs[:, 2 * th + t2, b, :],
                                           w[:, a:a + D], start=(i == 0), stop=(i == 1))
                last.then_inc(ring_full, 1)

            def soft_scores(ck):
                ring.wait_emptied(pe, ck, "soft", "qk")
                ring.wait_free(pe, ck, "soft", "s", wait_apart)
                bk = bank_of(ck, "soft", "s")
                for t in range(CT):
                    for b in (0, 1):
                        half = slice(64 * b, 64 * b + 64)
                        last = fmm(bk[half, 64 * t:64 * t + 64], qk[half, ck.u, 0, 64 * t:64 * t + 64],
                                   qk[half, ck.u, 1, 64 * t:64 * t + 64])
                last.then_inc(ring_full, 1)

            def soft_turn_p(ck):
                pe.wait_ge(sm_exp, ck.c + 1)
                ring.wait_free(pe, ck, "soft", "pt")
                for th in (0, 1):
                    last = nc.tensor.transpose(bank_of(ck, "soft", "pt")[:, P * th:P * th + P],
                                               pr[:, ck.u, P * th:P * th + P], ident)
                last.then_inc(ring_full, 1)

            def soft_out(ck, t2):
                bk = bank_of(ck, "soft", "o")
                if t2 == 0:
                    ring.wait_emptied(pe, ck, "soft", "pt")
                    ring.wait_emptied(pe, ck, "soft", "v")
                    ring.wait_free(pe, ck, "soft", "o", wait_apart)
                else:
                    wait_apart(pe, out_even, ck.c + 1)
                half = slice(64 * t2, 64 * t2 + 64)
                for th in (0, 1):
                    for b in (0, 1):
                        at = 128 * th + 64 * b
                        t = 2 * th + t2
                        last = fmm(bk[64 * b:64 * b + 64, 64 * t:64 * t + 64], pT[half, at:at + 64],
                                   vv[half, ck.u, at:at + 64])
                last.then_inc(out_even if t2 == 0 else ring_full, 1)

            def bn_accumulate(ck, src, done):
                mm(bank[7][:, 0:CT * D], ones[:, :], src, start=False, stop=False,
                   skip_group_check=True).then_inc(done, 1)

            def ao_flat(ck):
                return tiles_of(ao, ck).rearrange("p t d -> p (t d)")

            def bn_sum_chunk(ck):
                ring.wait_emptied(pe, ck, "soft", "o")
                bn_accumulate(ck, ao_flat(ck), bn_sum)

            def clear_bank7():
                mm(bank[7][:, :], ones[0:1, :], zero[:, :], start=True, stop=False, skip_group_check=True)

            def soft_body(ck):
                nx = Chunk(ck.c + 1, 1 - ck.u, ck.near + 1, ck.looped)
                more = ck.looped or ck.c + 1 < CHUNKS
                soft_turn_p(ck)
                if ck.looped or ck.c + 2 < CHUNKS:
                    soft_turn(Chunk(ck.c + 2, ck.u, ck.near + 2, ck.looped))
                if more:
                    soft_proj(nx)
                soft_out(ck, 0)
                if more:
                    soft_scores(nx)
                soft_out(ck, 1)
                bn_sum_chunk(ck)

            pe.wait_ge(b2_added, CHUNKS)
            clear_bank7()
            soft_turn(c0)
            soft_proj(c0)
            soft_scores(c0)
            soft_turn(Chunk(1, 1, 1, False))
            all_chunks(pe, soft_body)

            pe.wait_ge(bn_mean, 1)
            clear_bank7()

            def bn_squares(ck):
                pe.wait_ge(bn_sq, ck.c + 1)
                bn_accumulate(ck, sq[:, ck.u, 0:CT * D], bn_var)

            all_chunks(pe, bn_squares)
            pe.wait_ge(bn_coef, 1)
            clear_bank7()

            def dense_turn(ck):
                pe.wait_ge(x16_ready, ck.c + 3 * CHUNKS)
                turn16(bank[6], ck.c, ck.c + 3 * CHUNKS + 1).then_inc(x16_turned, 1)
                for t in range(CT):
                    last = mm(bank[7][0:D, 0:S], xn[:, t, 0, :], fold, start=False, stop=False, skip_group_check=True)
                last.then_inc(feat_done, 1)

            all_chunks(pe, dense_turn)
            pe.wait_ge(x16_ready, 4 * CHUNKS)
            pe.wait_ge(gate_step, 1)
            fmm(bank[6][0:S, 0:E], feat[:, :], wr1[:, :]).then_inc(gate_pe, 1)
            pe.wait_ge(gate_step, GATE_SHIFTED + 3)
            nc.tensor.transpose(bank[6][0:E, 256:256 + S], gl[:, 3, :], ident[0:S, 0:S])
            for a in range(4):
                last = fmm(bank[7][:, S * a:S * a + S], gwx[:, 2 * a:2 * a + 2, :].rearrange("f e n -> f (e n)"),
                           ident[0:S, 0:S])
            last.then_inc(gate_pe, 1)
            pe.wait_ge(gate_step, GATE_STEPS - 1)
            fmm(bank[6][:, 384:384 + D], gwT[:, :, :].rearrange("e c f -> e (c f)"), bo1[:, :]).then_inc(gate_pe, 1)

            def dense_one(ck, k):
                ring.wait_free(pe, ck, "one", f"p{k}")
                xs = x16all[:, ck.c * CN:ck.c * CN + CN] if not ck.looped else x16all[:, DS(ck.c * CN, CN)]
                two_pass(bank_of(ck, "one", f"p{k}")[:, :], xs, "U", P * k, P * k + P, True).then_inc(ring_full, 1)

            def dense_two(ck, k):
                ring.wait_emptied(pe, ck, "one", f"p{k}")
                ring.wait_free(pe, ck, "two", f"p{k}", wait_apart)
                for e2 in (0, 1):
                    half = slice(64 * e2, 64 * e2 + 64)
                    last = fmm(bank_of(ck, "two", f"p{k}")[half, :], u2[half, k, :], h1[half, ck.u, k, :])
                last.then_inc(ring_full, 1)

            def dense_three(ck):
                pe.wait_ge(weighed, ck.c * 4 + 4)
                ring.wait_free(pe, ck, "three", "y")
                for t in range(CT):
                    for k in range(4):
                        last = fmm(bank_of(ck, "three", "y")[:, D * t:D * t + D], h2w[:, ck.u, k, P * t:P * t + P],
                                   uo[:, k, :], start=(k == 0), stop=(k == 3))
                last.then_inc(ring_full, 1)

            def dense_body(ck):
                nx = Chunk(ck.c + 1, 1 - ck.u, ck.near + 1, ck.looped)
                for k in range(4):
                    if ck.looped or ck.c + 1 < CHUNKS:
                        dense_one(nx, k)
                    dense_two(ck, k)
                    if k == 1 and (ck.looped or ck.c >= 1):
                        dense_three(three_chunk(ck))

            for k in range(4):
                dense_one(c0, k)
            all_chunks(pe, dense_body)
            dense_three(Chunk(CHUNKS - 1, 1, CHUNKS - 1, False))


_INS = ["x", "L0_tok_W", "L0_tok_b", "L0_attn_Wq", "L0_attn_Wk", "L0_attn_Wv", "L0_attn_Wo",
        "L0_ffn_gamma", "L0_ffn_beta", "L0_ffn_Wr", "L0_ffn_br", "L0_ffn_W1", "L0_ffn_b1", "L0_ffn_W2", "L0_ffn_b2",
        "L1_attn_Wq", "L1_attn_bq", "L1_attn_Wk", "L1_attn_bk", "L1_attn_Wv", "L1_attn_bv", "L1_attn_Wl", "L1_attn_bl",
        "L1_attn_gamma", "L1_attn_beta",
        "L1_ffn_Wr", "L1_ffn_br", "L1_ffn_W1", "L1_ffn_b1", "L1_ffn_g1", "L1_ffn_be1", "L1_ffn_m1", "L1_ffn_v1",
        "L1_ffn_W2", "L1_ffn_b2", "L1_ffn_g2", "L1_ffn_be2", "L1_ffn_m2", "L1_ffn_v2", "L1_ffn_Wo", "L1_ffn_bo"]


def shape_constants():
    import numpy as np

    r2 = 0.5 ** 0.5

    def haar(n, sign):
        m = np.zeros((n // 2, n))
        m[np.arange(n // 2), 2 * np.arange(n // 2)] = r2
        m[np.arange(n // 2), 2 * np.arange(n // 2) + 1] = sign * r2
        return m

    def resize(n, to=8):
        scale = n / to
        at = (np.arange(to) + 0.5) * scale - 0.5
        w = np.maximum(0, 1 - np.abs(at[:, None] - np.arange(n)[None, :]) / scale)
        return w / w.sum(1, keepdims=True)

    lo = haar(R, 1)
    ops = [resize(R // 4) @ haar(R // 2, 1) @ lo, resize(R // 4) @ haar(R // 2, -1) @ lo,
           resize(R // 2) @ lo, resize(R // 2) @ haar(R, -1)]
    c = np.zeros((P, 32 + P + S), np.float32)
    c[:R, :32] = np.concatenate(ops).T
    c[:, 32:32 + P] = np.eye(P)
    c[:, 32 + P:] = np.concatenate([np.eye(S), np.eye(S)])
    return c


def kernel(**inputs):
    import numpy as _np
    import concourse.bacc as _bacc
    from concourse import mybir as _mybir
    from concourse.bass_utils import run_bass_kernel_spmd as _run

    nc = _bacc.Bacc("TRN2", target_bir_lowering=False, num_devices=1)
    arrays, args = {}, []
    for name in _INS:
        a = _np.ascontiguousarray(inputs[name])
        arrays[f"in_{name}_dram"] = a
        args.append(nc.dram_tensor(f"in_{name}_dram", a.shape, _mybir.dt.from_np(a.dtype), kind="ExternalInput").ap())
    consts = shape_constants()
    arrays["shape_constants_dram"] = consts
    args.append(nc.dram_tensor("shape_constants_dram", consts.shape, _mybir.dt.float32, kind="ExternalInput").ap())
    args.append(nc.dram_tensor("out_0_dram", (B, S, D), _mybir.dt.float32, kind="ExternalOutput").ap())
    vit_tower(nc, *args)
    r = _run(nc, [arrays], core_ids=[0])
    return r.results[0]["out_0_dram"]
```

```python
from contextlib import ExitStack

import concourse.bass as bass
from concourse import mybir

F32 = mybir.dt.float32
F16 = mybir.dt.float16
I32 = mybir.dt.int32
ALU = mybir.AluOpType
ACT = mybir.ActivationFunctionType
AX = mybir.AxisListType
DS = bass.ds

P = 128
B = 128
S = 64
D = 64
R = 96
TILES = B // 2
CT = 4
CHUNKS = TILES // CT
CN = CT * P
HEADS = 8
E = 8
H0 = 128
NMAPS = 7
GROUP = 16
GROUPS = B // GROUP
EPS = 1e-5
BN_EPS_ATT = 1e-5
BN_EPS_FFN = 1e-3
RING = 6

SEG = {}
_at = 0
for _name, _width in (("M", HEADS * D), ("N", HEADS * D), ("W1", E * H0), ("R", E),
                      ("Q", D), ("K", D), ("V", D), ("U", E * D)):
    SEG[_name] = (_at, _at + _width)
    _at += _width
WCOLS = _at
SEGS = list(SEG)

POOL_CONSTS = 5 + E
FTOK_ONES = 1
PERMUTED = 5
TURNED_READY = 16
EPS_ADDED = 22
PRODUCTS_READY = 24
WMAX_READY = 52
SPLIT_READY = 69
PREP_AT = (2, 3, 4, 5)
LN_STEPS = (2, 7, 2, 2)
RT_TANH = 13
RT_STEPS = 18
GATE_SHIFTED = 4
GATE_STEPS = 11


class Chunk:

    def __init__(self, c, u, near, looped):
        self.c, self.u, self.near, self.looped = c, u, near, looped


def all_chunks(eng, body, tail=2):
    for c in (0, 1):
        body(Chunk(c, c, c, False))
    with eng.Fori(1, (CHUNKS - tail) // 2) as i:
        for u in (0, 1):
            body(Chunk(i * 2 + u, u, 2 + u, True))
    for c in range(CHUNKS - tail, CHUNKS):
        body(Chunk(c, c % 2, c, False))


def later(ck, n):
    return Chunk(ck.c + n, (ck.u + n) % 2, ck.near + n, ck.looped)


def has(ck, n, tail=2):
    assert not ck.looped or n <= tail and n >= -2
    return ck.looped or 0 <= ck.c + n < CHUNKS


def wait_if(eng, sem, value):
    if isinstance(value, int) and value <= 0:
        return
    eng.wait_ge(sem, value)


class BankRing:

    def __init__(self, full, emptied):
        self.full, self.emptied, self.order, self.index = full, emptied, [], {}

    def plan(self, stage, chunk, names):
        for name, engine in names:
            self.index[stage, chunk, name] = len(self.order)
            self.order.append(engine)

    def fills(self, n):
        return n + 1 - self.order[:n + 1].count("-")

    def _value(self, ck, at):
        v0 = at(ck.near)
        if not ck.looped:
            return v0
        slope = (at(ck.near + 2) - v0) // 2
        for j in range(0, CHUNKS - 4, 2):
            assert at(ck.near + j) == v0 + slope * j
        return ck.c * slope + (v0 - slope * ck.near)

    def slot(self, ck, stage, name):
        n = self.index[stage, ck.near, name] % RING
        assert not ck.looped or self.index[stage, ck.near + 2, name] % RING == n
        return n

    def filled(self, ck, stage, name, back=0):
        return self._value(ck, lambda c: self.fills(self.index[stage, c - back, name]))

    def _emptied(self, ck, stage, name, uses_back):
        def place(c):
            n = self.index[stage, c, name] - uses_back
            while n >= 0 and self.order[n] == "-":
                n -= RING
            return n

        if place(ck.near) < 0:
            return None, 0
        e = self.order[place(ck.near)]

        def at(c):
            n = place(c)
            assert self.order[n] == e
            return self.order[:n + 1].count(e)

        return self.emptied[e], self._value(ck, at)

    def wait_free(self, pe, ck, stage, name, wait=wait_if):
        sem, value = self._emptied(ck, stage, name, RING)
        wait(pe, sem, value)

    def wait_emptied(self, eng, ck, stage, name, wait=wait_if):
        sem, value = self._emptied(ck, stage, name, 0)
        wait(eng, sem, value)


ATT_Q = [("q0", "V"), ("q1", "A"), ("q2", "V"), ("q3", "A")]
ATT_V = [("v0", "V"), ("v1", "V"), ("v2", "A"), ("v3", "V")]
ATT_S = [("s0", "A"), ("s1", "A"), ("s2", "A"), ("s3", "A")]


def plan_ring(ring):
    for c in range(CHUNKS):
        ring.plan("att", c, ATT_Q + ATT_V + ATT_S)
    ring.plan("up", 0, [(f"e{e}", "A") for e in range(E)])
    for c in range(CHUNKS):
        for t in range(CT):
            if c + 1 < CHUNKS:
                ring.plan("up", c + 1, [(f"e{e}", "A") for e in (2 * t, 2 * t + 1)])
            ring.plan("down", c, [(f"t{t}", "V")])
    ring.plan("soft", 0, [("q", "V"), ("k", "A"), ("v", "V"), ("s", "V")])
    for c in range(CHUNKS):
        if c + 1 < CHUNKS:
            ring.plan("soft", c + 1, [("q", "V"), ("k", "A"), ("v", "V")])
        ring.plan("soft", c, [("pt", "A")])
        if c + 1 < CHUNKS:
            ring.plan("soft", c + 1, [("s", "V")])
        ring.plan("soft", c, [("o", "V")])
    ring.plan("one", 0, [(f"p{k}", "AV"[k % 2]) for k in range(4)])
    for c in range(CHUNKS):
        for k in range(4):
            if c + 1 < CHUNKS:
                ring.plan("one", c + 1, [(f"p{k}", "AV"[k % 2])])
            ring.plan("two", c, [(f"p{k}", "AV"[k % 2 if k != 3 else 0])])
            if k == 1 and c >= 1:
                ring.plan("three", c - 1, [("y", "V")])
    ring.plan("three", CHUNKS - 1, [("y", "V")])


def vit_tower(nc, x, tok_W, tok_b, a_Wq, a_Wk, a_Wv, a_Wo, f_gamma, f_beta, f_Wr, f_br, f_W1, f_b1, f_W2, f_b2,
              s_Wq, s_bq, s_Wk, s_bk, s_Wv, s_bv, s_Wl, s_bl, s_gamma, s_beta,
              g_Wr, g_br, g_W1, g_b1, g_g1, g_be1, g_m1, g_v1, g_W2, g_b2, g_g2, g_be2, g_m2, g_v2, g_Wo, g_bo,
              shape_consts, out):
    with ExitStack() as ctx:
        def sb(name, shape, dt=F32):
            return ctx.enter_context(nc.sbuf_tensor(name, shape, dt))

        def sem(name):
            return ctx.enter_context(nc.semaphore(name))

        bank = [ctx.enter_context(nc.psum_tensor(f"bank{i}", [P, 512], F32)) for i in range(8)]

        h = sb("h", [P, TILES, D])
        consts = sb("consts", [P, 32 + P + S])
        resize = consts[0:R, 0:32]
        ident = consts[:, 32:32 + P]
        fold = consts[:, 32 + P:32 + P + S]
        ident16 = sb("ident16", [P, P], F16)
        ones = sb("ones", [P, P])

        wcat = sb("wcat", [P, WCOLS])
        whi = sb("whi", [P, WCOLS], F16)
        wlo = sb("wlo", [P, WCOLS], F16)
        wscale = sb("wscale", [P, len(SEGS)])
        winv = sb("winv", [P, len(SEGS)])
        wmax = sb("wmax", [P, 2, len(SEGS)])

        def seg(t, name):
            a, b = SEG[name]
            return t[:, a:b]

        def scale_of(t, name):
            k = SEGS.index(name)
            return t[:, k:k + 1]

        arena = sb("arena", [P, 8192])
        wb = sb("wb", [NMAPS + 1, D])
        rawqkv = arena[0:D, 0:1536].rearrange("g (w n) -> g w n", w=3)
        permqkv = arena[0:D, 1536:3072].rearrange("g (w a n) -> g w a n", w=3, a=4)
        wo_a = sb("wo_a", [P, HEADS, D])
        wT = arena[:, 3072:4608].rearrange("p (w a c g) -> p w a c g", w=3, a=4, c=2)
        w1raw = arena[:, 4608:5632]
        wrraw = sb("wrraw", [P, E])
        gamma0 = sb("gamma0", [P, 1])
        beta0 = sb("beta0", [D, 1])
        beta0_b = sb("beta0_b", [D, P])
        br_b = sb("br_b", [P, E])
        w2 = sb("w2", [P, E, D])
        b2blk = sb("b2blk", [CT * E, CT * D])
        rows = sb("rows", [48, P])
        cols = sb("cols", [P, 48])
        b1c = sb("b1c", [P, E])
        sig_scale = sb("sig_scale", [P, 1])
        wv1raw = sb("wv1raw", [D, D])
        wl1 = sb("wl1", [D, D])
        wv1T = sb("wv1T", [D, 2, D])
        bqk = sb("bqk", [P, 2])
        bv_c = sb("bv_c", [D, 1])
        bv_b = sb("bv_b", [D, P])
        vbias = sb("vbias", [P, D])
        bl_b = sb("bl_b", [P, D])
        bn_g = sb("bn_g", [P, D])
        bn_b = sb("bn_b", [P, D])
        u1raw = arena[:, 5632:6144].rearrange("p (e n) -> p e n", e=E)
        bnrow = arena[:, 6144:7168].rearrange("p (c n) -> p c n", c=2)
        bnrow2 = sb("bnrow2", [P, 2, 4, D])
        u2raw = sb("u2raw", [P, 4, D])
        u2 = sb("u2", [P, 4, D])
        uo = sb("uo", [P, 4, D])
        t12 = sb("t12", [P, 2, 4])
        NV = (E + 4) * D + 8
        var_all = arena[:, 7168:7168 + NV]
        roots = sb("roots", [P, NV])
        s1row, s2row = roots[:, 0:E * D], roots[:, E * D:(E + 4) * D].rearrange("p (a n) -> p a n", a=4)
        s12 = roots[:, (E + 4) * D:NV].rearrange("p (l a) -> p l a", l=2)
        tmp4 = sb("tmp4", [P, 4])
        wr1 = sb("wr1", [D, E])
        br1_b = sb("br1_b", [S, E])
        bo1 = sb("bo1", [E, D])

        late = sb("late", [P, TILES * D])

        stage = sb("stage", [P, 4 * GROUP * R])
        img = stage[0:R, :].rearrange("r (g b c) -> r g b c", g=4, b=GROUP)
        zbuf = sb("zbuf", [R, 2, 4, P])
        fbuf = sb("fbuf", [P, 2, 56])
        ftok = late[0:NMAPS + 1, 0:2 * GROUP * S].rearrange("m (u n) -> m u n", u=2)

        st = sb("st", [P, CT, 6])
        mv = sb("mv", [P, CT, 2])
        rstd = sb("rstd", [P, 4, CT])
        cent = sb("cent", [P, CT, D])
        xn = sb("xn", [P, CT, 2, D])
        xcat = sb("xcat", [P, CT, 2 * D], F16)
        x16 = sb("x16", [P, 2, CN], F16)
        x32 = sb("x32", [P, 2, CN])
        qbuf = arena[:, 0:2048].rearrange("p (a n) -> p a n", a=4)
        vbuf = arena[:, 2048:4096].rearrange("p (t n) -> p t n", t=CT)
        abuf = arena[:, 4096:6144].rearrange("p (t n) -> p t n", t=CT)
        gbuf = arena[:, 0:8192].rearrange("p (u e n) -> p u e n", u=2, e=E)
        resid = sb("resid", [P, 2, CT, D])
        lg = sb("lg", [P, 10, CT, E])
        top = sb("top", [P, 8, CT])
        iota = sb("iota", [P, CT, E])
        wtT = sb("wtT", [CT * E, P])
        prod = late.rearrange("p (u t e d) -> p u t e d", u=2, t=CT, e=E)
        qk = sb("qk", [P, 2, 2, 256])
        vv = sb("vv", [P, 2, 256])
        sc = sb("sc", [P, 256])
        pr = sb("pr", [P, 2, 256])
        mx = sb("mx", [P, 2, CT])
        rs = sb("rs", [P, 2, CT])
        pT = sb("pT", [P, 256])
        ao = late[:, :].rearrange("p (t d) -> p t d", t=TILES)
        mean_b = sb("mean_b", [P, D])
        bnA = sb("bnA", [P, D])
        sq = sb("sq", [P, 2, CT * D])
        x16all = sb("x16all", [P, TILES * P], F16)
        feat = sb("feat", [D, S])
        gl = sb("gl", [S, 4, E])
        gs = sb("gs", [S, 4])
        gwb = sb("gwb", [P, 4, S])
        gwx = sb("gwx", [S, E, D])
        gwT = sb("gwT", [E, 2, S])
        bow = sb("bow", [P, D])
        h1 = arena[:, 0:4096].rearrange("p (u a n) -> p u a n", u=2, a=4)
        h2 = arena[:, 4096:8192].rearrange("p (u a n) -> p u a n", u=2, a=4)
        h2w = stage[:, 0:8 * CN].rearrange("p (u a n) -> p u a n", u=2, a=4)
        zero = sb("zero", [1, 512])
        minus_half = sb("minus_half", [P, 1])
        ln_eps = sb("ln_eps", [P, CT])

        s_const, s_wa, s_wf = sem("consts_loaded"), sem("attention_weights_loaded"), sem("other_weights_loaded")
        s_b2 = sem("b2_blocks_loaded")
        s_img = [sem(f"images_loaded{i}") for i in range(4)]
        prep_pe, prep_dve, prep_pool = sem("prep_pe"), sem("prep_dve"), sem("prep_pool")
        roots_ready = sem("roots_ready")
        rows_done, z_copied, maps_done, maps_copied = (sem("rows_resized"), sem("rows_copied"), sem("maps_done"),
                                                       sem("maps_copied"))
        ft_done, ft_copied, tok_done, h_ready = (sem("maps_turned"), sem("turned_copied"), sem("tokens_done"),
                                                 sem("tokens_copied"))
        ring_full = sem("ring_full")
        act_emptied, dve_emptied = sem("act_emptied"), sem("dve_emptied")
        ln_stats, ln_aggr, ln_step = sem("ln_stats"), sem("ln_aggr"), sem("ln_step")
        n_cent, n_scaled, n_hi, n_split = sem("norm_centred"), sem("norm_scaled"), sem("norm_hi"), sem("norm_split")
        x16_turned, x16_ready = sem("x16_turned"), sem("x16_ready")
        x32_turned, x32_ready = sem("x32_turned"), sem("x32_ready")
        av_done, av_relu, att_added = sem("av_done"), sem("av_relu"), sem("attention_added")
        rt_done, rt_step, rt_tanh = sem("router_done"), sem("router_step"), sem("router_tanh")
        wt_turned, wt_ready, b2_done, b2_added = (sem("weights_turned"), sem("weights_turned_copied"),
                                                  sem("b2_done"), sem("b2_added"))
        tree_step, moe_added = sem("expert_sum_step"), sem("experts_added")
        hx_added = sem("hx_added")
        sm_max, sm_exp, sm_sum = sem("score_max"), sem("score_exp"), sem("score_sum")
        sm_inv, out_even = sem("score_inverse"), sem("even_tiles_done")
        bn_sum, bn_mean, bn_cent, bn_sq, bn_var, bn_coef = (sem("bn_sum"), sem("bn_mean"), sem("bn_centred"),
                                                            sem("bn_squared"), sem("bn_var"), sem("bn_coef"))
        bn_app, bn_step, bn_eps, bn_root = sem("bn_applied"), sem("bn_step"), sem("bn_eps"), sem("bn_root")
        feat_done, gate_step, gate_pe = sem("feat_done"), sem("gate_step"), sem("gate_pe")
        gate_exp = sem("gate_exp")
        bow_added, weighed, stored = sem("bo_added"), sem("hidden_weighed"), sem("stored")

        ring = BankRing(ring_full, {"A": act_emptied, "V": dve_emptied})
        plan_ring(ring)

        def ln_base(n, stage):
            extra = LN_STEPS[1] - LN_STEPS[0]
            return n * LN_STEPS[stage] + (0, -extra * CHUNKS, extra * CHUNKS, extra * CHUNKS)[stage]

        def wait_apart(eng, sem, value):
            if not isinstance(value, int):
                value = eng.to_reg(value)
                eng.wait_ge(s_const, 16)
            wait_if(eng, sem, value)

        def bank_of(ck, stage, name):
            return bank[ring.slot(ck, stage, name)]

        def tiles_of(t, ck):
            return t[:, ck.c * CT:ck.c * CT + CT, :] if isinstance(ck.c, int) else t[:, DS(ck.c * CT, CT), :]

        def bc(ap, shape):
            return ap.to_broadcast(shape)

        def minus_half_like(ap):
            half = minus_half[:, 0:1] if len(ap.shape) == 2 else minus_half[:, 0:1].unsqueeze(2)
            return bc(half, list(ap.shape))

        def ring_who(stage, k):
            return ring.order[ring.index[stage, 2, f"p{k}"]]

        def three_chunk(ck):
            if not ck.looped:
                return Chunk(ck.c - 1, 1 - ck.u, ck.near - 1, False)
            return Chunk(ck.c - 1, 1 - ck.u, ck.near - 1, True)

        block = ctx.enter_context(nc.Block())

        ATT_LOADS, TOKEN_W_LOADS = [], []
        for i, w in enumerate((a_Wq, a_Wk, a_Wv)):
            ATT_LOADS.append((rawqkv[:, i, :], w))
        for q in (0, D):
            ATT_LOADS.append((wo_a[q:q + D], a_Wo.rearrange("(k h) d -> k h d", h=HEADS)))
        for i, m in enumerate((0, 2, 1, 3, 5, 4, 6)):
            TOKEN_W_LOADS.append((wb[i:i + 1, :], tok_W[m:m + 1, :]))
        TOKEN_W_LOADS.append((wb[NMAPS:NMAPS + 1, :], tok_b.rearrange("(a d) -> a d", a=1)))
        for q in (0, D):
            ATT_LOADS += [(w1raw[q:q + D, :].rearrange("p (e n) -> p e n", e=E), f_W1.rearrange("e d n -> d e n")),
                          (wrraw[q:q + D, :], f_Wr),
                          (gamma0[q:q + D, :], f_gamma.rearrange("(d a) -> d a", a=1)),
                          (seg(wcat, "Q")[q:q + D, :], s_Wq), (seg(wcat, "K")[q:q + D, :], s_Wk),
                          (u1raw[q:q + D], g_W1.rearrange("e d n -> d e n"))]
        ATT_LOADS += [(beta0[:, :], f_beta.rearrange("(d a) -> d a", a=1)),
                      (wv1raw[:, :], s_Wv), (wl1[:, :], s_Wl),
                      (bv_c[:, :], s_bv.rearrange("(d a) -> d a", a=1)),
                      (br_b[:, :], f_br.partition_broadcast(P)),
                      (bl_b[:, :], s_bl.partition_broadcast(P)),
                      (bn_g[:, :], s_gamma.partition_broadcast(P)),
                      (bn_b[:, :], s_beta.partition_broadcast(P)),
                      (bnrow[:, 0, :], g_g1.rearrange("e n -> (e n)").partition_broadcast(P)),
                      (bnrow[:, 1, :], g_v1.rearrange("e n -> (e n)").partition_broadcast(P)),
                      (w2[:, :, :], f_W2.rearrange("e n d -> n e d")),
                      (u2raw[:, :, :], g_W2.rearrange("(a e) n k -> (e n) a k", e=2)),
                      (uo[:, :, :], g_Wo.rearrange("(a e) n k -> (e n) a k", e=2)),
                      (rows[40:48, :], f_b1),
                      (wr1[:, :], g_Wr), (br1_b[:, :], g_br.partition_broadcast(S)), (bo1[:, :], g_bo)]
        for e2 in (0, 1):
            for k, v in enumerate((g_g2, g_v2)):
                ATT_LOADS.append((bnrow2[e2 * D:e2 * D + D, k], v.rearrange("(a e) n -> e a n", e=2)[e2]
                                  .partition_broadcast(D)))
            for k, v in enumerate((s_bq, s_bk)):
                ATT_LOADS.append((bqk[e2 * D:e2 * D + D, k:k + 1], v.rearrange("(d a) -> d a", a=1)))
        for k, v in enumerate((g_b1, g_g1, g_be1, g_m1, g_v1, g_b2, g_g2, g_be2, g_m2, g_v2)):
            ATT_LOADS.append((rows[4 * k:4 * k + 4, :], v.rearrange("(a e) n -> a (e n)", e=2)))
        B2_LOADS = [(b2blk[E * t:E * t + E, D * t:D * t + D], f_b2) for t in range(CT)]

        LOADS = 16 * len(ATT_LOADS)

        @block.sync
        def _(sp):
            sp.dma_start(consts[:, :], shape_consts).then_inc(s_const, 16)
            for g in range(4):
                sp.dma_start(img[:, g], x[g * GROUP:(g + 1) * GROUP, 0].rearrange("b r c -> r b c")
                             ).then_inc(s_img[g], 16)
            for dst, src in TOKEN_W_LOADS:
                sp.dma_start(dst, src).then_inc(s_wa, 16)
            for dst, src in ATT_LOADS[:12]:
                sp.dma_start(dst, src).then_inc(s_wf, 16)
            for g in range(4, GROUPS):
                sp.wait_ge(rows_done, g - 3)
                sp.dma_start(img[:, g % 4], x[g * GROUP:(g + 1) * GROUP, 0].rearrange("b r c -> r b c")
                             ).then_inc(s_img[g % 4], 16)

            out_v = out.rearrange("(n p) t d -> (p t) n d", p=2)

            def store(ck):
                ring.wait_emptied(sp, ck, "three", "y")
                sp.dma_start(tiles_of(out_v, ck), tiles_of(h, ck)).then_inc(stored, 16)

            all_chunks(sp, store)
            sp.wait_ge(stored, 16 * CHUNKS)

        @block.gpsimd
        def _(pool):
            nc.gpsimd.memset(b2blk[:, :], 0.0).then_inc(prep_pool, 1)
            nc.gpsimd.memset(ones[:, :], 1.0).then_inc(prep_pool, 1)
            nc.gpsimd.memset(zero[:, :], 0.0).then_inc(prep_pool, 1)
            for e in range(E):
                nc.gpsimd.memset(iota[:, :, e:e + 1], float(e)).then_inc(prep_pool, 1)
            nc.gpsimd.memset(minus_half[:, :], -0.5).then_inc(prep_pool, 1)
            nc.gpsimd.memset(ln_eps[:, :], EPS).then_inc(prep_pool, 1)
            pool.wait_ge(prep_pool, POOL_CONSTS)
            for dst, src in B2_LOADS:
                pool.dma_start(dst, src).then_inc(s_b2, 16)
            def inverse_root(dst, src):
                return nc.gpsimd.tensor_tensor(dst, src, minus_half_like(src), ALU.pow)

            pool.wait_ge(prep_dve, WMAX_READY)
            nc.gpsimd.partition_all_reduce(wmax[:, 1, :], wmax[:, 0, :], P, bass.bass_isa.ReduceOp.max
                                           ).then_inc(prep_pool, 1)

            def roots_of(n, stage):
                base, k = ln_base(n, stage), [0]

                def ln(ins):
                    k[0] += 1
                    ins.then_inc(ln_step, 1)

                def ln_wait():
                    pool.wait_ge(ln_step, base + k[0])

                double = stage == 1
                var = mv[:, :, 1]
                pool.wait_ge(ln_aggr, n + 1)
                wait_if(pool, n_scaled, n)
                ln(nc.gpsimd.tensor_tensor(rstd[:, 1, :], var, ln_eps[:, :], ALU.add))
                ln_wait()
                ln(inverse_root(rstd[:, 2 if double else 0, :], rstd[:, 1, :]))
                if double:
                    ln_wait()
                    ln(nc.gpsimd.tensor_tensor(rstd[:, 3, :], rstd[:, 2, :], var, ALU.mult))
                    ln_wait()
                    ln(nc.gpsimd.tensor_tensor(rstd[:, 1, :], rstd[:, 3, :], rstd[:, 2, :], ALU.mult))
                    ln_wait()
                    ln(nc.gpsimd.tensor_tensor(rstd[:, 3, :], rstd[:, 1, :], ln_eps[:, :], ALU.add))
                    ln_wait()
                    ln(inverse_root(rstd[:, 1, :], rstd[:, 3, :]))
                    ln_wait()
                    ln(nc.gpsimd.tensor_tensor(rstd[:, 0, :], rstd[:, 1, :], rstd[:, 2, :], ALU.mult))
                assert k[0] == LN_STEPS[stage]

            def low_part(ck, n, stage):
                pool.wait_ge(n_hi, n + 1)
                nc.gpsimd.tensor_tensor(xcat[:, :, D:2 * D], xn[:, :, ck.u if stage else 0, :], xcat[:, :, 0:D],
                                        ALU.subtract).then_inc(n_split, 1)

            def attention_body(ck):
                if has(ck, 2):
                    roots_of(ck.c + 2, 0)
                pool.wait_ge(av_relu, ck.c + 1)
                nc.gpsimd.tensor_tensor(tiles_of(h, ck), tiles_of(h, ck), resid[:, ck.u], ALU.add
                                        ).then_inc(att_added, 1)
                if has(ck, 2):
                    low_part(later(ck, 2), ck.c + 2, 0)

            for c in (0, 1):
                roots_of(c, 0)
                low_part(Chunk(c, c, c, False), c, 0)
            all_chunks(pool, attention_body)

            def expert_sum(ck):
                y = prod[:, ck.u]
                ring.wait_emptied(pool, ck, "down", f"t{CT - 1}")
                nc.gpsimd.tensor_tensor(y[:, :, 0:4, :], y[:, :, 0:4, :], y[:, :, 4:8, :], ALU.add
                                        ).then_inc(tree_step, 1)
                pool.wait_ge(tree_step, ck.c * 3 + 1)
                nc.gpsimd.tensor_tensor(y[:, :, 0:2, :], y[:, :, 0:2, :], y[:, :, 2:4, :], ALU.add
                                        ).then_inc(tree_step, 1)
                pool.wait_ge(tree_step, ck.c * 3 + 2)
                nc.gpsimd.tensor_tensor(y[:, :, 0, :], y[:, :, 0, :], y[:, :, 1, :], ALU.add
                                        ).then_inc(tree_step, 1)
                pool.wait_ge(tree_step, ck.c * 3 + 3)
                pool.wait_ge(b2_added, ck.c + 1)
                nc.gpsimd.tensor_tensor(tiles_of(h, ck), tiles_of(h, ck), y[:, :, 0, :], ALU.add
                                        ).then_inc(moe_added, 1)

            def moe_body(ck):
                if has(ck, 3, 4):
                    roots_of(ck.c + CHUNKS + 3, 1)
                if has(ck, -1):
                    expert_sum(later(ck, -1))
                if has(ck, 3, 4):
                    low_part(later(ck, 3), ck.c + CHUNKS + 3, 1)

            for c in range(3):
                roots_of(c + CHUNKS, 1)
                low_part(Chunk(c, c % 2, c, False), c + CHUNKS, 1)
            all_chunks(pool, moe_body, 4)
            expert_sum(Chunk(CHUNKS - 1, 1, CHUNKS - 1, False))

            def norm_soft(ck):
                n = ck.c + 2 * CHUNKS
                roots_of(n, 2)
                low_part(ck, n, 2)
                nc.gpsimd.tensor_tensor(tiles_of(h, ck), tiles_of(h, ck), xn[:, :, ck.u, :], ALU.add
                                        ).then_inc(hx_added, 1)

            def soft_body(ck):
                if has(ck, 3, 4):
                    norm_soft(later(ck, 3))

            for c in range(3):
                norm_soft(Chunk(c, c % 2, c, False))
            all_chunks(pool, soft_body, 4)

            pool.wait_ge(bn_eps, 1)
            inverse_root(bnA[:, :], bnA[:, :]).then_inc(bn_root, 1)

            def bn_apply(ck):
                pool.wait_ge(bn_coef, 1)
                nc.gpsimd.tensor_tensor(tiles_of(ao, ck), tiles_of(ao, ck), bc(bnA[:, :].unsqueeze(1), [P, CT, D]),
                                        ALU.mult).then_inc(bn_app, 1)

            def apply_body(ck):
                if has(ck, 1):
                    bn_apply(later(ck, 1))
                roots_of(ck.c + 3 * CHUNKS, 3)
                if has(ck, -1):
                    low_part(later(ck, -1), ck.c + 3 * CHUNKS - 1, 3)

            bn_apply(Chunk(0, 0, 0, False))
            all_chunks(pool, apply_body)
            low_part(Chunk(CHUNKS - 1, 1, CHUNKS - 1, False), 4 * CHUNKS - 1, 3)

            def add_bo(ck):
                pool.wait_ge(gate_step, GATE_STEPS)
                nc.gpsimd.tensor_tensor(tiles_of(h, ck), tiles_of(h, ck), bc(bow[:, :].unsqueeze(1), [P, CT, D]),
                                        ALU.add).then_inc(bow_added, 1)

            def dense_body(ck):
                add_bo(ck)
                for k in range(4):
                    ring.wait_emptied(pool, ck, "two", f"p{k}")
                    if k == 0 and (ck.looped or ck.c >= 2):
                        pool.wait_ge(ring_full, ring.filled(ck, "three", "y", 2))
                    nc.gpsimd.tensor_tensor(h2w[:, ck.u, k, :].rearrange("p (b f) -> p b f", f=S),
                                            h2[:, ck.u, k, :].rearrange("p (b f) -> p b f", f=S),
                                            bc(gwb[:, k, :].unsqueeze(1), [P, 2 * CT, S]), ALU.mult
                                            ).then_inc(weighed, 1)

            all_chunks(pool, dense_body)

        @block.scalar
        def _(act):
            def copy(dst, src):
                return nc.scalar.activation(dst, src, ACT.Copy)

            for dst, src in ATT_LOADS[12:]:
                act.dma_start(dst, src).then_inc(s_wf, 16)

            def tok_copies(g):
                u = g % 2
                act.wait_ge(rows_done, g + 1)
                if g >= 2:
                    act.wait_ge(maps_done, g - 1)
                copy(zbuf[:, u].rearrange("c o (b i) -> c o b i", b=GROUP),
                     bank[u][0:R, :].rearrange("c (b o i) -> c o b i", b=GROUP, o=4)).then_inc(z_copied, 1)
                act.wait_ge(ft_done, g + 1)
                if g >= 2:
                    act.wait_ge(tok_done, g - 1)
                else:
                    act.wait_ge(prep_dve, FTOK_ONES)
                for q in (0, 1):
                    last = copy(ftok[0:NMAPS, u].rearrange("m (b j) -> m b j", j=8)[:, :, 4 * q:4 * q + 4],
                                bank[4 + q][0:NMAPS, :].rearrange("m (j b) -> m b j", j=4))
                last.then_inc(ft_copied, 1)

            for g in range(GROUPS):
                tok_copies(g)
                if g == PREP_AT[0] + 1:
                    act.wait_ge(prep_dve, EPS_ADDED)
                    nc.scalar.activation(roots[:, :], var_all, ACT.Sqrt).then_inc(roots_ready, 1)

            def high_part(ck, n, stage):
                act.wait_ge(n_scaled, n + 1)
                wait_if(act, x16_turned, n)
                copy(xcat[:, :, 0:D], xn[:, :, ck.u if stage else 0, :]).then_inc(n_hi, 1)

            def att_x16(ck):
                act.wait_ge(x16_turned, ck.c + 1)
                if ck.looped or ck.c >= 2:
                    act.wait_ge(av_done, ck.c - 1)
                copy(x16[:, ck.u, :], bank[6][:, :].bitcast(F16)[:, 0:CN]).then_inc(x16_ready, 1)

            def att_empty(ck, name, dst, func=None):
                act.wait_ge(ring_full, ring.filled(ck, "att", name))
                if func is None:
                    copy(dst, bank_of(ck, "att", name)[:, :]).then_inc(act_emptied, 1)
                else:
                    nc.scalar.activation(dst, bank_of(ck, "att", name)[:, :], func, scale=sig_scale[:, 0:1]
                                         ).then_inc(act_emptied, 1)

            def attention_body(ck):
                wait_if(act, av_done, ck.c)
                for k, (name, who) in enumerate(ATT_Q):
                    if who == "A":
                        att_empty(ck, name, qbuf[:, k, :])
                if ck.looped or ck.c + 1 < CHUNKS:
                    att_x16(Chunk(ck.c + 1, 1 - ck.u, ck.near + 1, ck.looped))
                for t, (name, who) in enumerate(ATT_V):
                    if who == "A":
                        att_empty(ck, name, vbuf[:, t, :])
                for t in range(CT):
                    att_empty(ck, f"s{t}", abuf[:, t, :], ACT.Sigmoid)
                if has(ck, 2):
                    high_part(later(ck, 2), ck.c + 2, 0)
                act.wait_ge(av_done, ck.c + 1)
                if ck.looped or ck.c >= 2:
                    act.wait_ge(att_added, ck.c - 1)
                nc.scalar.activation(resid[:, ck.u].rearrange("p t d -> p (t d)"), bank[7][:, 0:CT * D], ACT.Relu,
                                     scale=scale_of(wscale, "N")).then_inc(av_relu, 1)

            high_part(Chunk(0, 0, 0, False), 0, 0)
            act.wait_ge(prep_dve, SPLIT_READY)
            att_x16(Chunk(0, 0, 0, False))
            high_part(Chunk(1, 1, 1, False), 1, 0)
            all_chunks(act, attention_body)

            def moe_x16(ck):
                act.wait_ge(x16_turned, ck.c + CHUNKS + 1)
                if ck.looped or ck.c >= 2:
                    act.wait_ge(ring_full, ring.filled(ck, "up", f"e{E - 1}", 2))
                copy(x16[:, ck.u, :], bank[6][:, :].bitcast(F16)[:, 0:CN]).then_inc(x16_ready, 1)

            def gelu(ck, e):
                act.wait_ge(ring_full, ring.filled(ck, "up", f"e{e}"))
                nc.scalar.activation(gbuf[:, ck.u, e, :], bank_of(ck, "up", f"e{e}")[:, :], ACT.Gelu,
                                     bias=b1c[:, e:e + 1], scale=scale_of(wscale, "W1")).then_inc(act_emptied, 1)

            def router_tanh(ck):
                act.wait_ge(rt_step, ck.c * RT_STEPS + RT_TANH)
                nc.scalar.activation(top[:, 3, :], top[:, 2, :], ACT.Tanh, scale=0.5).then_inc(rt_tanh, 1)

            def moe_body(ck):
                nx = later(ck, 1)
                if has(ck, 2):
                    moe_x16(later(ck, 2))
                for t in range(CT):
                    if has(ck, 1):
                        for e in (2 * t, 2 * t + 1):
                            if e == 0 and has(ck, -1):
                                act.wait_ge(ring_full, ring.filled(ck, "down", f"t{CT - 1}", 1))
                            gelu(nx, e)
                        if t == 2:
                            router_tanh(nx)
                    if t == 3 and has(ck, 3, 4):
                        high_part(later(ck, 3), ck.c + CHUNKS + 3, 1)

            for c in range(2):
                high_part(Chunk(c, c % 2, c, False), c + CHUNKS, 1)
                moe_x16(Chunk(c, c % 2, c, False))
            high_part(Chunk(2, 0, 2, False), 2 + CHUNKS, 1)
            act.wait_ge(av_done, CHUNKS)
            for e in range(E):
                gelu(Chunk(0, 0, 0, False), e)
                if e == 5:
                    router_tanh(Chunk(0, 0, 0, False))
            all_chunks(act, moe_body, 4)

            def soft_x16(ck):
                act.wait_ge(x16_turned, ck.c + 2 * CHUNKS + 1)
                if ck.looped or ck.c >= 2:
                    act.wait_ge(ring_full, ring.filled(ck, "soft", "v", 2))
                copy(x16[:, ck.u, :], bank[6][:, :].bitcast(F16)[:, 0:CN]).then_inc(x16_ready, 1)

            def soft_k(ck):
                act.wait_ge(ring_full, ring.filled(ck, "soft", "k"))
                if ck.looped or ck.c >= 2:
                    act.wait_ge(ring_full, ring.filled(ck, "soft", "s", 2))
                nc.scalar.activation(qk[:, ck.u, 1, :], bank_of(ck, "soft", "k")[:, 0:256], ACT.Identity,
                                     bias=bqk[:, 1:2], scale=scale_of(wscale, "K")).then_inc(act_emptied, 1)

            def soft_exp(ck):
                ring.wait_emptied(act, ck, "soft", "s")
                if ck.looped or ck.c >= 2:
                    act.wait_ge(ring_full, ring.filled(ck, "soft", "pt", 2))
                    act.wait_ge(sm_sum, ck.c - 1)
                nc.scalar.activation(pr[:, ck.u, :], sc[:, :], ACT.Exp, scale=1.0 / D).then_inc(sm_exp, 1)

            def soft_body(ck):
                if has(ck, 2):
                    soft_x16(later(ck, 2))
                if has(ck, 1):
                    soft_k(later(ck, 1))
                act.wait_ge(ring_full, ring.filled(ck, "soft", "pt"))
                if has(ck, -1):
                    act.wait_ge(ring_full, ring.filled(ck, "soft", "o", 1))
                copy(pT[:, :], bank_of(ck, "soft", "pt")[:, 0:256]).then_inc(act_emptied, 1)
                if has(ck, 1):
                    soft_exp(later(ck, 1))
                if has(ck, 3, 4):
                    high_part(later(ck, 3), ck.c + 2 * CHUNKS + 3, 2)

            act.wait_ge(ring_full, ring.fills(ring.index["up", CHUNKS - 1, "e7"]))
            for c in range(2):
                high_part(Chunk(c, c % 2, c, False), c + 2 * CHUNKS, 2)
                soft_x16(Chunk(c, c % 2, c, False))
            high_part(Chunk(2, 0, 2, False), 2 + 2 * CHUNKS, 2)
            soft_k(Chunk(0, 0, 0, False))
            soft_exp(Chunk(0, 0, 0, False))
            all_chunks(act, soft_body, 4)

            def bn_square(ck):
                act.wait_ge(bn_cent, ck.c + 1)
                if ck.looped or ck.c >= 2:
                    act.wait_ge(bn_var, ck.c - 1)
                nc.scalar.activation(sq[:, ck.u, 0:CT * D].rearrange("p (t d) -> p t d", t=CT), tiles_of(ao, ck),
                                     ACT.Square).then_inc(bn_sq, 1)

            all_chunks(act, bn_square)

            def dense_x16(ck):
                act.wait_ge(x16_turned, ck.c + 3 * CHUNKS + 1)
                dst = x16all[:, ck.c * CN:ck.c * CN + CN] if not ck.looped else x16all[:, DS(ck.c * CN, CN)]
                copy(dst, bank[6][:, :].bitcast(F16)[:, 0:CN]).then_inc(x16_ready, 1)

            def turn_body(ck):
                high_part(ck, ck.c + 3 * CHUNKS, 3)
                dense_x16(ck)

            all_chunks(act, turn_body)

            act.wait_ge(gate_step, GATE_SHIFTED)
            nc.scalar.activation(gl[:, 2, :], gl[:, 1, :], ACT.Exp, accum_out=gs[:, 1:2]).then_inc(gate_exp, 1)

            def dense_relu(ck, stage, k, dst, bias):
                act.wait_ge(ring_full, ring.filled(ck, stage, f"p{k}"))
                nc.scalar.activation(dst, bank_of(ck, stage, f"p{k}")[:, :], ACT.Relu, bias=bias
                                     ).then_inc(act_emptied, 1)

            def dense_body(ck):
                if ck.looped or ck.c >= 2:
                    act.wait_ge(weighed, ck.c * 4 - 4)
                for k in range(4):
                    if ring_who("one", k) == "A" and (ck.looped or ck.c + 1 < CHUNKS):
                        dense_relu(Chunk(ck.c + 1, 1 - ck.u, ck.near + 1, ck.looped), "one", k,
                                   h1[:, 1 - ck.u, k, :], t12[:, 0, k:k + 1])
                    if ring_who("two", k) == "A":
                        dense_relu(ck, "two", k, h2[:, ck.u, k, :], t12[:, 1, k:k + 1])

            for k in range(4):
                if ring_who("one", k) == "A":
                    dense_relu(Chunk(0, 0, 0, False), "one", k, h1[:, 0, k, :], t12[:, 0, k:k + 1])
            all_chunks(act, dense_body)

        @block.vector
        def _(dve):
            v = nc.vector
            step = [0]

            def link(ins):
                step[0] += 1
                ins.then_inc(prep_dve, 1)
                dve.wait_ge(prep_dve, step[0])

            link(v.memset(ftok[:, :, :], 1.0))
            assert step[0] == FTOK_ONES
            dve.wait_ge(s_const, 16)
            link(v.tensor_copy(ident16[:, :], ident))

            def prep_turned():
                dve.wait_ge(s_wf, LOADS)
                for w in range(3):
                    link(v.tensor_copy(permqkv[:, w].rearrange("g a (e k) -> g a e k", e=2),
                                       rawqkv[:, w, :].rearrange("g (k a e) -> g a e k", a=4, e=2)))
                assert step[0] == PERMUTED
                dve.wait_ge(prep_pe, 1)
                for w in (0, 1):
                    for c in (0, 1):
                        link(v.tensor_copy(wT[:, w, :, c, :],
                                           bank[6][:, 256 * w:256 * w + 256].rearrange("p (a g) -> p a g", a=4)))
                dve.wait_ge(prep_pe, 2)
                for c in (0, 1):
                    link(v.tensor_copy(wT[:, 2, :, c, :], bank[7][:, 0:256].rearrange("p (a g) -> p a g", a=4)))
                    link(v.tensor_copy(wv1T[:, c, :], bank[7][0:D, 256:320]))
                link(v.tensor_copy(cols[:, :], bank[7][:, 320:368]))
                link(v.tensor_copy(bv_b[:, :], bc(bv_c[:, 0:1], [D, P])))
                link(v.tensor_copy(beta0_b[:, :], bc(beta0[:, 0:1], [D, P])))
                assert step[0] == TURNED_READY
                link(v.tensor_scalar(seg(wcat, "W1"), w1raw[:, :], gamma0[:, 0:1], None, ALU.mult))
                link(v.tensor_scalar(seg(wcat, "R"), wrraw[:, :], gamma0[:, 0:1], None, ALU.mult))
                link(v.tensor_scalar(var_all[:, 0:E * D], bnrow[:, 1, :], BN_EPS_FFN, None, ALU.add))
                link(v.tensor_scalar(var_all[:, E * D:(E + 4) * D].rearrange("p (a n) -> p a n", a=4), bnrow2[:, 1],
                                     BN_EPS_FFN, None, ALU.add))
                for l in (0, 1):
                    link(v.tensor_scalar(var_all[:, (E + 4) * D + 4 * l:(E + 4) * D + 4 * l + 4],
                                         cols[:, 20 * l + 16:20 * l + 20], BN_EPS_FFN, None, ALU.add))
                assert step[0] == EPS_ADDED

            def prep_products():
                dve.wait_ge(prep_pe, 4)
                link(v.tensor_copy(seg(wcat, "M"), bank[6][:, :]))
                link(v.tensor_copy(seg(wcat, "N"), bank[7][:, :]))
                assert step[0] == PRODUCTS_READY

            def prep_small():
                dve.wait_ge(roots_ready, 1)
                newton = x32.rearrange("p u n -> p (u n)")[:, 0:NV]
                link(v.reciprocal(roots[:, :], roots[:, :]))
                link(v.tensor_tensor(newton, roots[:, :], roots[:, :], ALU.mult))
                link(v.tensor_tensor(newton, newton, var_all, ALU.mult))
                link(v.tensor_scalar(newton, newton, -0.5, 1.5, ALU.mult, ALU.add))
                link(v.tensor_tensor(roots[:, :], roots[:, :], newton, ALU.mult))
                link(v.tensor_tensor(s1row, s1row, bnrow[:, 0, :], ALU.mult))
                link(v.tensor_tensor(seg(wcat, "U"), u1raw[:, :, :].rearrange("p e n -> p (e n)"), s1row, ALU.mult))
                link(v.tensor_tensor(s2row, s2row, bnrow2[:, 0], ALU.mult))
                for l in (0, 1):
                    b_, g_, be_, m_ = (cols[:, 20 * l + 4 * k:20 * l + 4 * k + 4] for k in range(4))
                    link(v.tensor_tensor(s12[:, l, :], s12[:, l, :], g_, ALU.mult))
                    link(v.tensor_tensor(tmp4[:, :], b_, m_, ALU.subtract))
                    link(v.tensor_tensor(tmp4[:, :], tmp4[:, :], s12[:, l, :], ALU.mult))
                    link(v.tensor_tensor(t12[:, l, :], tmp4[:, :], be_, ALU.add))
                dve.wait_ge(prep_pe, 5)
                link(v.tensor_copy(seg(wcat, "V"), bank[7][:, 0:D]))
                link(v.tensor_tensor(vbias[:, :], bank[7][:, 64:128], bl_b[:, :], ALU.add))
                link(v.tensor_tensor(br_b[:, :], bank[7][:, 128:128 + E], br_b[:, :], ALU.add))
                link(v.tensor_tensor(b1c[:, :], bank[7][:, 192:192 + E], cols[:, 40:48], ALU.add))
                for k, name in enumerate(SEGS):
                    link(v.tensor_reduce(wmax[:, 0, k:k + 1], seg(wcat, name), AX.X, ALU.max, apply_absolute_value=True))
                assert step[0] == WMAX_READY

            def prep_split():
                dve.wait_ge(prep_pool, POOL_CONSTS + 1)
                link(v.tensor_scalar(wscale[:, :], wmax[:, 1, :], 2.0 ** -100, 2.0 ** 100, ALU.max, ALU.min))
                link(v.tensor_scalar(wscale[:, :].bitcast(I32), wscale[:, :].bitcast(I32), 0x7F800000, None,
                                     ALU.bitwise_and))
                link(v.reciprocal(winv[:, :], wscale[:, :]))
                for name in SEGS:
                    link(v.tensor_scalar(seg(wcat, name), seg(wcat, name), scale_of(winv, name), None, ALU.mult))
                link(v.tensor_copy(whi[:, :], wcat[:, :]))
                link(v.tensor_tensor(wlo[:, :], wcat[:, :], whi[:, :], ALU.subtract))
                link(v.tensor_scalar(sig_scale[:, :], scale_of(wscale, "M"), 8.0, None, ALU.mult))
                link(v.tensor_scalar(t12[:, 0, :], t12[:, 0, :], scale_of(winv, "U"), None, ALU.mult))
                link(v.tensor_scalar(s2row, s2row, scale_of(wscale, "U"), None, ALU.mult))
                link(v.tensor_tensor(u2[:, :, :], u2raw[:, :, :], s2row, ALU.mult))
                assert step[0] == SPLIT_READY

            def tok_maps(g):
                dve.wait_ge(maps_done, g + 1)
                if g >= 2:
                    dve.wait_ge(ft_done, g - 1)
                v.tensor_copy(fbuf[:, g % 2, :], bank[2][:, 0:56]).then_inc(maps_copied, 1)

            def tok_h(g):
                dve.wait_ge(tok_done, g + 1)
                n = GROUP // 2
                v.tensor_copy(h[:, g * n:(g + 1) * n, :].rearrange("p t d -> p (t d)"), bank[3][:, :]
                              ).then_inc(h_ready, 1)

            tok_maps(0)
            for g in range(GROUPS):
                if g + 1 < GROUPS:
                    tok_maps(g + 1)
                tok_h(g)
                if g in PREP_AT:
                    (prep_turned, prep_products, prep_small, prep_split)[PREP_AT.index(g)]()

            def statistics(ck, n, ready=None):
                if ready:
                    wait_apart(dve, *ready)
                for t in range(CT):
                    src = h[:, ck.c * CT + t, :] if not ck.looped else h[:, DS(ck.c * CT + t, 1), :]
                    v.bn_stats(st[:, t, :], src).then_inc(ln_stats, 1)
                wait_apart(dve, ln_stats, n * CT + CT)
                wait_apart(dve, n_scaled, n)
                for t in range(CT):
                    last = v.bn_aggr(mv[:, t, :], st[:, t, :])
                last.then_inc(ln_aggr, 1)

            def scale(ck, n, stage, *readers):
                dve.wait_ge(ln_step, ln_base(n, stage) + LN_STEPS[stage])
                wait_if(dve, n_split, n - 1 if stage else n)
                for sem_, value in readers:
                    wait_if(dve, sem_, value)
                for t in range(CT):
                    src = h[:, ck.c * CT + t:ck.c * CT + t + 1, :] if not ck.looped else h[:, DS(ck.c * CT + t, 1), :]
                    dst = xn[:, t, :, :] if stage == 0 else xn[:, t, ck.u:ck.u + 1, :]
                    last = v.tensor_scalar(dst, src if stage else bc(src, [P, 2, D]), mv[:, t, 0:1], rstd[:, 0, t:t + 1],
                                           ALU.subtract, ALU.mult)
                last.then_inc(n_scaled, 1)

            def att_empty(ck, name, dst):
                dve.wait_ge(ring_full, ring.filled(ck, "att", name))
                v.tensor_copy(dst, bank_of(ck, "att", name)[:, :]).then_inc(dve_emptied, 1)

            def att_x32(ck):
                dve.wait_ge(x32_turned, ck.c + 1)
                if ck.looped or ck.c >= 2:
                    dve.wait_ge(av_done, ck.c - 1)
                v.tensor_copy(x32[:, ck.u, :], bank[6][:, :]).then_inc(x32_ready, 1)

            def attention_body(ck):
                wait_if(dve, av_done, ck.c)
                for k, (name, who) in enumerate(ATT_Q):
                    if who == "V":
                        att_empty(ck, name, qbuf[:, k, :])
                if ck.looped or ck.c + 2 < CHUNKS:
                    statistics(Chunk(ck.c + 2, ck.u, ck.near + 2, ck.looped), ck.c + 2)
                for t, (name, who) in enumerate(ATT_V):
                    if who == "V":
                        att_empty(ck, name, vbuf[:, t, :])
                if has(ck, 1):
                    att_x32(later(ck, 1))
                if has(ck, 2):
                    scale(later(ck, 2), ck.c + 2, 0)

            dve.wait_ge(h_ready, GROUPS)
            statistics(Chunk(0, 0, 0, False), 0)
            scale(Chunk(0, 0, 0, False), 0, 0)
            statistics(Chunk(1, 1, 1, False), 1)
            att_x32(Chunk(0, 0, 0, False))
            scale(Chunk(1, 1, 1, False), 1, 0)
            all_chunks(dve, attention_body)

            def stats_moe(ck):
                statistics(ck, ck.c + CHUNKS, (att_added, ck.c + 1))

            def router(ck, *steps):
                L, Q, one, two = lg[:, 0], lg[:, 1], lg[:, 2], lg[:, 3]
                wide = [P, CT, E]

                def value(r):
                    return top[:, r, :]

                def spread(r):
                    return bc(top[:, r, :].unsqueeze(2), wide)

                for k in steps:
                    if k == 0:
                        dve.wait_ge(rt_done, ck.c + 1)
                        ins = v.scalar_tensor_tensor(out=L, in0=bank[6][:, 256:256 + CT * E].rearrange(
                            "p (t e) -> p t e", t=CT), scalar=scale_of(wscale, "R"),
                            in1=bc(br_b[:, :].unsqueeze(1), wide), op0=ALU.mult, op1=ALU.add)
                    else:
                        dve.wait_ge(rt_step, ck.c * RT_STEPS + k)
                    r, src, hot = (0, L, one) if k < 7 else (1, Q, two)
                    if k in (1, 7):
                        ins = v.tensor_reduce(value(r), src, AX.X, ALU.max)
                    elif k in (2, 8):
                        ins = v.tensor_tensor(lg[:, 4], src, spread(r), ALU.is_lt)
                    elif k in (3, 9):
                        ins = v.scalar_tensor_tensor(out=lg[:, 5], in0=lg[:, 4], scalar=float(E), in1=iota[:, :, :],
                                                     op0=ALU.mult, op1=ALU.add)
                    elif k in (4, 10):
                        ins = v.tensor_reduce(value(4 + r), lg[:, 5], AX.X, ALU.min)
                    elif k in (5, 11):
                        ins = v.tensor_tensor(hot, iota[:, :, :], spread(4 + r), ALU.is_equal)
                    elif k == 6:
                        ins = v.scalar_tensor_tensor(out=Q, in0=one, scalar=-3.0e38, in1=L, op0=ALU.mult, op1=ALU.add)
                    elif k == 12:
                        ins = v.tensor_tensor(value(2), value(0), value(1), ALU.subtract)
                    elif k == RT_TANH:
                        dve.wait_ge(rt_tanh, ck.c + 1)
                        ins = v.tensor_scalar(value(6), value(3), 0.5, 0.5, ALU.mult, ALU.add)
                    elif k == 14:
                        ins = v.tensor_scalar(value(7), value(3), -0.5, 0.5, ALU.mult, ALU.add)
                    elif k == 15:
                        ins = v.tensor_tensor(lg[:, 6], one, spread(6), ALU.mult)
                    elif k == 16:
                        ins = v.tensor_tensor(lg[:, 7], two, spread(7), ALU.mult)
                    elif k == 17:
                        ins = v.tensor_tensor(lg[:, 8 + ck.u], lg[:, 6], lg[:, 7], ALU.add)
                    ins.then_inc(rt_step, 1)

            def router_turned(ck):
                dve.wait_ge(wt_turned, ck.c + 1)
                v.tensor_copy(wtT[:, :], bank[7][0:CT * E, 128:256]).then_inc(wt_ready, 1)

            def router_b2(ck):
                dve.wait_ge(b2_done, ck.c + 1)
                v.tensor_tensor(tiles_of(h, ck), tiles_of(h, ck), bank[7][:, 256:512].rearrange("p (t d) -> p t d", t=CT),
                                ALU.add).then_inc(b2_added, 1)

            def weigh(ck, t):
                if t == 0 and has(ck, -2):
                    dve.wait_ge(moe_added, ck.c - 1)
                dve.wait_ge(ring_full, ring.filled(ck, "down", f"t{t}"))
                v.tensor_tensor(prod[:, ck.u, t], bank_of(ck, "down", f"t{t}")[:, :].rearrange("p (e d) -> p e d", e=E),
                                bc(lg[:, 8 + ck.u, t, :].unsqueeze(2), [P, E, D]), ALU.mult).then_inc(dve_emptied, 1)

            def moe_body(ck):
                nx, more, far = later(ck, 1), has(ck, 1), has(ck, 3, 4)
                router_turned(ck)
                if more:
                    router(nx, 0)
                if far:
                    stats_moe(later(ck, 3))
                if more:
                    router(nx, 1, 2, 3, 4)
                weigh(ck, 0)
                if more:
                    router(nx, 5, 6)
                router_b2(ck)
                if more:
                    router(nx, 7, 8, 9)
                weigh(ck, 1)
                if more:
                    router(nx, 10, 11, 12)
                if far:
                    scale(later(ck, 3), ck.c + CHUNKS + 3, 1)
                weigh(ck, 2)
                if more:
                    router(nx, *range(RT_TANH, RT_STEPS))
                weigh(ck, 3)

            for c in range(3):
                stats_moe(Chunk(c, c % 2, c, False))
                scale(Chunk(c, c % 2, c, False), c + CHUNKS, 1, (x32_turned, CHUNKS))
            router(Chunk(0, 0, 0, False), *range(RT_STEPS))
            all_chunks(dve, moe_body, 4)

            def stats_soft(ck):
                statistics(ck, ck.c + 2 * CHUNKS, (moe_added, ck.c + 1))

            def soft_proj(ck):
                dve.wait_ge(ring_full, ring.filled(ck, "soft", "q"))
                if ck.looped or ck.c >= 2:
                    dve.wait_ge(ring_full, ring.filled(ck, "soft", "s", 2))
                v.tensor_scalar(qk[:, ck.u, 0, :], bank_of(ck, "soft", "q")[:, 0:256], scale_of(wscale, "Q"),
                                bqk[:, 0:1], ALU.mult, ALU.add).then_inc(dve_emptied, 1)
                dve.wait_ge(ring_full, ring.filled(ck, "soft", "v"))
                if ck.looped or ck.c >= 2:
                    dve.wait_ge(ring_full, ring.filled(ck, "soft", "o", 2))
                v.scalar_tensor_tensor(out=vv[:, ck.u].rearrange("p (t d) -> p t d", d=D),
                                       in0=bank_of(ck, "soft", "v")[:, 0:256].rearrange("p (t d) -> p t d", d=D),
                                       scalar=scale_of(wscale, "V"), in1=bc(vbias[:, :].unsqueeze(1), [P, CT, D]),
                                       op0=ALU.mult, op1=ALU.add).then_inc(dve_emptied, 1)

            def soft_shift(ck):
                s = bank_of(ck, "soft", "s")[:, 0:256].rearrange("p (t j) -> p t j", t=CT)
                dve.wait_ge(ring_full, ring.filled(ck, "soft", "s"))
                v.tensor_reduce(mx[:, ck.u, :], s, AX.X, ALU.max).then_inc(sm_max, 1)
                dve.wait_ge(sm_max, ck.c + 1)
                wait_if(dve, sm_exp, ck.c)
                v.tensor_tensor(sc[:, :].rearrange("p (t j) -> p t j", t=CT), s,
                                bc(mx[:, ck.u, :].unsqueeze(2), [P, CT, S]), ALU.subtract).then_inc(dve_emptied, 1)

            def soft_sum(ck):
                dve.wait_ge(sm_exp, ck.c + 1)
                v.tensor_reduce(rs[:, 0, :], pr[:, ck.u, :].rearrange("p (t j) -> p t j", t=CT), AX.X, ALU.add
                                ).then_inc(sm_sum, 1)
                dve.wait_ge(sm_sum, ck.c + 1)
                v.reciprocal(rs[:, 1, :], rs[:, 0, :]).then_inc(sm_inv, 1)

            def soft_body(ck):
                if has(ck, 1):
                    soft_proj(later(ck, 1))
                soft_sum(ck)
                if has(ck, 3, 4):
                    stats_soft(later(ck, 3))
                if has(ck, 1):
                    soft_shift(later(ck, 1))
                if has(ck, 3, 4):
                    scale(later(ck, 3), ck.c + 2 * CHUNKS + 3, 2, (hx_added, ck.c + 2))
                dve.wait_ge(ring_full, ring.filled(ck, "soft", "o"))
                dve.wait_ge(sm_inv, ck.c + 1)
                v.tensor_tensor(tiles_of(ao, ck), bank_of(ck, "soft", "o")[:, 0:256].rearrange("p (t d) -> p t d", d=D),
                                bc(rs[:, 1, :].unsqueeze(2), [P, CT, D]), ALU.mult).then_inc(dve_emptied, 1)

            for c in range(3):
                stats_soft(Chunk(c, c % 2, c, False))
                scale(Chunk(c, c % 2, c, False), c + 2 * CHUNKS, 2, (hx_added, c - 1))
            dve.wait_ge(moe_added, CHUNKS)
            soft_proj(Chunk(0, 0, 0, False))
            soft_shift(Chunk(0, 0, 0, False))
            all_chunks(dve, soft_body, 4)

            N = float(B * S)
            s4 = bank[7][:, 0:CT * D].rearrange("p (t d) -> p d t", t=CT)
            k = step[0]
            dve.wait_ge(bn_sum, CHUNKS)
            link(v.tensor_reduce(mean_b[:, :], s4, AX.X, ALU.add))
            v.tensor_scalar(mean_b[:, :], mean_b[:, :], 1.0 / N, None, ALU.mult).then_inc(bn_mean, 1)
            dve.wait_ge(bn_mean, 1)

            def bn_centre(ck):
                v.tensor_tensor(tiles_of(ao, ck), tiles_of(ao, ck), bc(mean_b[:, :].unsqueeze(1), [P, CT, D]),
                                ALU.subtract).then_inc(bn_cent, 1)

            all_chunks(dve, bn_centre)
            dve.wait_ge(bn_var, CHUNKS)
            link(v.tensor_reduce(bnA[:, :], s4, AX.X, ALU.add))
            v.tensor_scalar(bnA[:, :], bnA[:, :], 1.0 / N, BN_EPS_ATT, ALU.mult, ALU.add).then_inc(bn_eps, 1)
            dve.wait_ge(bn_root, 1)
            v.tensor_tensor(bnA[:, :], bnA[:, :], bn_g[:, :], ALU.mult).then_inc(bn_coef, 1)

            def bn_add(ck):
                dve.wait_ge(bn_app, ck.c + 1)
                v.tensor_tensor(tiles_of(ao, ck), tiles_of(ao, ck), bc(bn_b[:, :].unsqueeze(1), [P, CT, D]), ALU.add
                                ).then_inc(bn_step, 1)
                dve.wait_ge(bn_step, ck.c * 2 + 1)
                v.scalar_tensor_tensor(out=tiles_of(h, ck), in0=tiles_of(ao, ck), scalar=0.0, in1=tiles_of(h, ck),
                                       op0=ALU.max, op1=ALU.add).then_inc(bn_step, 1)
                if has(ck, -1):
                    norm_dense(later(ck, -1))
                statistics(ck, ck.c + 3 * CHUNKS, (bn_step, ck.c * 2 + 2))

            def norm_dense(ck):
                scale(ck, ck.c + 3 * CHUNKS, 3, (feat_done, ck.c - 1), (hx_added, CHUNKS))

            dve.wait_ge(hx_added, CHUNKS)
            all_chunks(dve, bn_add)
            norm_dense(Chunk(CHUNKS - 1, 1, CHUNKS - 1, False))

            g = [0]

            def gate(ins):
                g[0] += 1
                ins.then_inc(gate_step, 1)
                dve.wait_ge(gate_step, g[0])

            dve.wait_ge(feat_done, CHUNKS)
            gate(v.tensor_scalar(feat[:, :], bank[7][0:D, 0:S], 1.0 / B, None, ALU.mult))
            dve.wait_ge(gate_pe, 1)
            gate(v.tensor_tensor(gl[:, 0, :], bank[6][0:S, 0:E], br1_b[:, :], ALU.add))
            gate(v.tensor_reduce(gs[:, 0:1], gl[:, 0, :], AX.X, ALU.max))
            gate(v.tensor_scalar(gl[:, 1, :], gl[:, 0, :], gs[:, 0:1], None, ALU.subtract))
            assert g[0] == GATE_SHIFTED
            dve.wait_ge(gate_exp, 1)
            gate(v.reciprocal(gs[:, 2:3], gs[:, 1:2]))
            gate(v.tensor_scalar(gl[:, 3, :], gl[:, 2, :], gs[:, 2:3], None, ALU.mult))
            gate(v.tensor_copy(gwx[:, :, :], bc(gl[:, 3, :].unsqueeze(2), [S, E, D])))
            dve.wait_ge(gate_pe, 2)
            gate(v.tensor_copy(gwT[:, 0, :], bank[6][0:E, 256:256 + S]))
            gate(v.tensor_copy(gwT[:, 1, :], bank[6][0:E, 256:256 + S]))
            gate(v.tensor_copy(gwb[:, :, :], bank[7][:, 0:4 * S].rearrange("p (a f) -> p a f", a=4)))
            dve.wait_ge(gate_pe, 3)
            gate(v.tensor_copy(bow[:, :], bank[6][:, 384:384 + D]))
            assert g[0] == GATE_STEPS

            def dense_relu(ck, stage, k, dst, bias):
                dve.wait_ge(ring_full, ring.filled(ck, stage, f"p{k}"))
                v.tensor_scalar(dst, bank_of(ck, stage, f"p{k}")[:, :], bias, 0.0, ALU.add, ALU.max
                                ).then_inc(dve_emptied, 1)

            def third(ck):
                dve.wait_ge(ring_full, ring.filled(ck, "three", "y"))
                dve.wait_ge(bow_added, ck.c + 1)
                v.tensor_tensor(tiles_of(h, ck), tiles_of(h, ck),
                                bank_of(ck, "three", "y")[:, 0:CT * D].rearrange("p (t d) -> p t d", t=CT), ALU.add
                                ).then_inc(dve_emptied, 1)

            def dense_body(ck):
                if ck.looped or ck.c >= 2:
                    dve.wait_ge(weighed, ck.c * 4 - 4)
                for k in range(4):
                    if ring_who("one", k) == "V" and (ck.looped or ck.c + 1 < CHUNKS):
                        dense_relu(Chunk(ck.c + 1, 1 - ck.u, ck.near + 1, ck.looped), "one", k,
                                   h1[:, 1 - ck.u, k, :], t12[:, 0, k:k + 1])
                    if ring_who("two", k) == "V":
                        dense_relu(ck, "two", k, h2[:, ck.u, k, :], t12[:, 1, k:k + 1])
                    if k == 1 and (ck.looped or ck.c >= 1):
                        third(three_chunk(ck))

            for k in range(4):
                if ring_who("one", k) == "V":
                    dense_relu(Chunk(0, 0, 0, False), "one", k, h1[:, 0, k, :], t12[:, 0, k:k + 1])
            all_chunks(dve, dense_body)
            third(Chunk(CHUNKS - 1, 1, CHUNKS - 1, False))

        @block.tensor
        def _(pe):
            mm = nc.tensor.matmul

            def fmm(out, lhsT, rhs, start=True, stop=True):
                return mm(out, lhsT, rhs, start=start, stop=stop)

            def two_pass(out, xs, name, lo, hi, x_moving):
                a = SEG[name][0]
                for i, w in enumerate((whi, wlo)):
                    wp = w[:, a + lo:a + hi]
                    last = fmm(out, wp if x_moving else xs, xs if x_moving else wp, start=(i == 0), stop=(i == 1))
                return last

            pe.wait_ge(s_const, 16)

            def prep_turn():
                pe.wait_ge(s_wf, LOADS)
                pe.wait_ge(prep_pool, POOL_CONSTS)

                pe.wait_ge(prep_dve, PERMUTED)

                for w in (0, 1):
                    for a in range(4):
                        last = nc.tensor.transpose(bank[6][:, 256 * w + 64 * a:256 * w + 64 * a + 64], permqkv[:, w, a, :],
                                                   ident[0:D, 0:D])
                last.then_inc(prep_pe, 1)
                for a in range(4):
                    nc.tensor.transpose(bank[7][:, 64 * a:64 * a + 64], permqkv[:, 2, a, :], ident[0:D, 0:D])
                nc.tensor.transpose(bank[7][0:D, 256:320], wv1raw[:, :], ident[0:D, 0:D])
                nc.tensor.transpose(bank[7][:, 320:368], rows[:, :], ident[0:48, 0:48]).then_inc(prep_pe, 1)

            def prep_products():
                pe.wait_ge(prep_dve, TURNED_READY)
                for e2 in (0, 1):
                    if e2 == 1:
                        pe.wait_ge(prep_pe, 3)
                    half = slice(64 * e2, 64 * e2 + 64)
                    for a in range(4):
                        hd = 2 * a + e2
                        fmm(bank[6][:, 64 * hd:64 * hd + 64], wT[half, 0, a].rearrange("p c g -> p (c g)"),
                            wT[half, 1, a, 0, :])
                        last = fmm(bank[7][:, (4 * e2 + a) * 64:(4 * e2 + a) * 64 + 64],
                                   wT[half, 2, a].rearrange("p c g -> p (c g)"), wo_a[half, hd, :])
                    last.then_inc(prep_pe, 1)

            def prep_small():
                pe.wait_ge(prep_dve, PRODUCTS_READY)
                fmm(bank[7][:, 0:D], wv1T[:, :, :].rearrange("p c g -> p (c g)"), wl1[:, :])
                fmm(bank[7][:, 64:128], bv_b[:, :], wl1[:, :])
                fmm(bank[7][:, 128:128 + E], beta0_b[:, :], wrraw[0:D, :])
                for e in range(E):
                    last = fmm(bank[7][:, 192 + e:193 + e], w1raw[0:D, H0 * e:H0 * e + H0], beta0[:, 0:1])
                last.then_inc(prep_pe, 1)

            def tok_rows(g):
                u = g % 2
                pe.wait_ge(s_img[g % 4], 16 * (g // 4 + 1))
                if g >= 2:
                    pe.wait_ge(z_copied, g - 1)
                for b in range(GROUP):
                    last = fmm(bank[u][0:R, 32 * b:32 * b + 32], img[:, g % 4, b, :], resize)
                last.then_inc(rows_done, 1)

            MAPS = ((0, 16, 0), (0, 16, 16), (24, 32, 32), (16, 32, 40))

            def tok_maps(g):
                u = g % 2
                pe.wait_ge(z_copied, g + 1)
                wait_if(pe, maps_copied, g)
                for o, (lo, hi, at) in enumerate(MAPS):
                    last = fmm(bank[2][:, at:at + hi - lo], zbuf[:, u, o, :], resize[:, lo:hi])
                last.then_inc(maps_done, 1)

            def tok_turn(g):
                u = g % 2
                pe.wait_ge(maps_copied, g + 1)
                if g >= 1:
                    pe.wait_ge(ft_copied, g)
                for j in range(8):
                    last = nc.tensor.transpose(bank[4 + j // 4][0:NMAPS, 128 * (j % 4):128 * (j % 4) + 128],
                                               fbuf[:, u, :].rearrange("p (m j) -> p j m", j=8)[:, j, :], ident)
                last.then_inc(ft_done, 1)

            def tok_project(g):
                u = g % 2
                pe.wait_ge(ft_copied, g + 1)
                if g >= 1:
                    pe.wait_ge(h_ready, g)
                for t in range(GROUP // 2):
                    last = fmm(bank[3][:, 64 * t:64 * t + 64], ftok[:, u, P * t:P * t + P], wb[:, :])
                last.then_inc(tok_done, 1)

            pe.wait_ge(s_wa, 16 * len(TOKEN_W_LOADS))
            tok_rows(0)
            tok_maps(0)
            for g in range(GROUPS):
                if g + 1 < GROUPS:
                    tok_rows(g + 1)
                tok_turn(g)
                tok_project(g)
                if g + 1 < GROUPS:
                    tok_maps(g + 1)
                if g in PREP_AT[:3]:
                    (prep_turn, prep_products, prep_small)[PREP_AT.index(g)]()

            def turn16(dst, n, split_value):
                pe.wait_ge(n_split, split_value)
                d = dst[:, :].bitcast(F16)
                for t in range(CT):
                    last = nc.tensor.transpose(d[:, P * t:P * t + P], xcat[:, t, :], ident16[:, :])
                return last

            def att_turn16(ck):
                wait_if(pe, x32_ready, ck.c)
                turn16(bank[6], ck.c, ck.c + 1).then_inc(x16_turned, 1)

            def att_turn32(ck):
                pe.wait_ge(x16_ready, ck.c + 1)
                for t in range(CT):
                    last = nc.tensor.transpose(bank[6][:, P * t:P * t + P],
                                               xn[:, t, :, :].rearrange("p c d -> p (c d)"), ident)
                last.then_inc(x32_turned, 1)

            def attention_body(ck):
                more = ck.looped or ck.c + 1 < CHUNKS
                nx = Chunk(ck.c + 1, 1 - ck.u, ck.near + 1, ck.looped)
                xs = x16[:, ck.u, :]
                pe.wait_ge(x16_ready, ck.c + 1)
                for a in range(4):
                    ring.wait_free(pe, ck, "att", f"q{a}")
                    two_pass(bank_of(ck, "att", f"q{a}")[:, :], xs, "M", P * a, P * a + P, True
                             ).then_inc(ring_full, 1)
                if more:
                    att_turn16(nx)
                for t in range(CT):
                    ring.wait_free(pe, ck, "att", f"v{t}")
                    bk = bank_of(ck, "att", f"v{t}")
                    for b in (0, 1):
                        xb = xs[:, P * t + S * b:P * t + S * b + S]
                        for i, w in enumerate((whi, wlo)):
                            for e2 in (0, 1):
                                a0 = SEG["N"][0] + 256 * e2
                                last = fmm(bk[64 * e2:64 * e2 + 64, 256 * b:256 * b + 256], xb, w[:, a0:a0 + 256],
                                           start=(i == 0), stop=(i == 1))
                    last.then_inc(ring_full, 1)
                if more:
                    att_turn32(nx)
                pe.wait_ge(x32_ready, ck.c + 1)
                for a in range(4):
                    ring.wait_emptied(pe, ck, "att", f"q{a}", wait_apart)
                for t in range(CT):
                    ring.wait_free(pe, ck, "att", f"s{t}", wait_apart)
                    bk = bank_of(ck, "att", f"s{t}")
                    for b in (0, 1):
                        at = P * t + S * b
                        for e2 in (0, 1):
                            half = slice(64 * e2, 64 * e2 + 64)
                            last = fmm(bk[half, 256 * b:256 * b + 256], x32[half, ck.u, at:at + S],
                                       qbuf[half, :, at:at + S])
                    last.then_inc(ring_full, 1)
                wait_if(pe, av_relu, ck.c)
                for t in range(CT):
                    ring.wait_emptied(pe, ck, "att", f"v{t}")
                    ring.wait_emptied(pe, ck, "att", f"s{t}")
                    for a in range(4):
                        for b in (0, 1):
                            cs = slice(256 * b + 64 * a, 256 * b + 64 * a + 64)
                            last = fmm(bank[7][64 * b:64 * b + 64, D * t:D * t + D], abuf[:, t, cs], vbuf[:, t, cs],
                                       start=(a == 0), stop=(a == 3))
                last.then_inc(av_done, 1)

            pe.wait_ge(prep_dve, SPLIT_READY)
            pe.wait_ge(h_ready, GROUPS)
            att_turn16(Chunk(0, 0, 0, False))
            att_turn32(Chunk(0, 0, 0, False))
            all_chunks(pe, attention_body)

            def moe_turn(ck):
                if not ck.looped and ck.c == 0:
                    pe.wait_ge(x32_ready, CHUNKS)
                else:
                    pe.wait_ge(rt_step, (ck.c - 1) * RT_STEPS + 1)
                pe.wait_ge(x16_ready, ck.c + CHUNKS)
                turn16(bank[6], ck.c, ck.c + CHUNKS + 1).then_inc(x16_turned, 1)

            def moe_router(ck):
                pe.wait_ge(x16_ready, ck.c + CHUNKS + 1)
                for t in range(CT):
                    last = two_pass(bank[6][:, 256 + E * t:256 + E * t + E], x16[:, ck.u, P * t:P * t + P], "R", 0, E, False)
                last.then_inc(rt_done, 1)

            def moe_up(ck, e):
                ring.wait_free(pe, ck, "up", f"e{e}")
                two_pass(bank_of(ck, "up", f"e{e}")[:, :], x16[:, ck.u, :], "W1", H0 * e, H0 * e + H0, True
                         ).then_inc(ring_full, 1)

            def moe_b2_turn(ck):
                pe.wait_ge(rt_step, ck.c * RT_STEPS + RT_STEPS)
                wait_if(pe, b2_added, ck.c)
                nc.tensor.transpose(bank[7][0:CT * E, 128:256], lg[:, 8 + ck.u].rearrange("p t e -> p (t e)"), ident
                                    ).then_inc(wt_turned, 1)

            def moe_b2(ck):
                pe.wait_ge(wt_ready, ck.c + 1)
                fmm(bank[7][:, 256:512], wtT[:, :], b2blk[:, :]).then_inc(b2_done, 1)

            def moe_down(ck, t):
                ring.wait_free(pe, ck, "down", f"t{t}")
                for e in range(E):
                    last = fmm(bank_of(ck, "down", f"t{t}")[:, D * e:D * e + D], gbuf[:, ck.u, e, P * t:P * t + P],
                               w2[:, e, :])
                last.then_inc(ring_full, 1)

            def moe_body(ck):
                nx, more = later(ck, 1), has(ck, 1)
                if more:
                    moe_router(nx)
                moe_b2_turn(ck)
                for t in range(CT):
                    if more:
                        moe_up(nx, 2 * t)
                        moe_up(nx, 2 * t + 1)
                    if t == 0 and has(ck, 2):
                        moe_turn(later(ck, 2))
                    if t == 0:
                        ring.wait_emptied(pe, ck, "up", f"e{E - 1}")
                    moe_down(ck, t)
                    if t == 0:
                        moe_b2(ck)

            c0 = Chunk(0, 0, 0, False)
            pe.wait_ge(av_relu, CHUNKS)
            moe_turn(c0)
            moe_router(c0)
            for e in range(E):
                moe_up(c0, e)
                if e == 1:
                    moe_turn(Chunk(1, 1, 1, False))
            pe.wait_ge(s_b2, 16 * len(B2_LOADS))
            all_chunks(pe, moe_body, 4)

            def soft_turn(ck):
                pe.wait_ge(x16_ready, ck.c + 2 * CHUNKS)
                turn16(bank[6], ck.c, ck.c + 2 * CHUNKS + 1).then_inc(x16_turned, 1)

            def soft_proj(ck):
                pe.wait_ge(x16_ready, ck.c + 2 * CHUNKS + 1)
                xs = x16[:, ck.u, :].rearrange("p (t b i) -> p t b i", t=CT, b=2)
                for name in "QK":
                    ring.wait_free(pe, ck, "soft", name.lower())
                    bk = bank_of(ck, "soft", name.lower())
                    a = SEG[name][0]
                    for i, w in enumerate((whi, wlo)):
                        for b in (0, 1):
                            last = fmm(bk[64 * b:64 * b + 64, 0:256], w[:, a:a + D], xs[:, :, b, :],
                                       start=(i == 0), stop=(i == 1))
                    last.then_inc(ring_full, 1)
                ring.wait_free(pe, ck, "soft", "v")
                bk = bank_of(ck, "soft", "v")
                a = SEG["V"][0]
                for th in (0, 1):
                    for b in (0, 1):
                        for i, w in enumerate((whi, wlo)):
                            for t2 in (0, 1):
                                at = 128 * th + 64 * b
                                last = fmm(bk[64 * t2:64 * t2 + 64, at:at + 64], xs[:, 2 * th + t2, b, :],
                                           w[:, a:a + D], start=(i == 0), stop=(i == 1))
                last.then_inc(ring_full, 1)

            def soft_scores(ck):
                ring.wait_emptied(pe, ck, "soft", "q")
                ring.wait_emptied(pe, ck, "soft", "k")
                ring.wait_free(pe, ck, "soft", "s", wait_apart)
                bk = bank_of(ck, "soft", "s")
                for t in range(CT):
                    for b in (0, 1):
                        half = slice(64 * b, 64 * b + 64)
                        last = fmm(bk[half, 64 * t:64 * t + 64], qk[half, ck.u, 0, 64 * t:64 * t + 64],
                                   qk[half, ck.u, 1, 64 * t:64 * t + 64])
                last.then_inc(ring_full, 1)

            def soft_turn_p(ck):
                pe.wait_ge(sm_exp, ck.c + 1)
                ring.wait_free(pe, ck, "soft", "pt")
                for th in (0, 1):
                    last = nc.tensor.transpose(bank_of(ck, "soft", "pt")[:, P * th:P * th + P],
                                               pr[:, ck.u, P * th:P * th + P], ident)
                last.then_inc(ring_full, 1)

            def soft_out(ck, t2):
                bk = bank_of(ck, "soft", "o")
                if t2 == 0:
                    ring.wait_emptied(pe, ck, "soft", "pt")
                    ring.wait_emptied(pe, ck, "soft", "v")
                    ring.wait_free(pe, ck, "soft", "o", wait_apart)
                else:
                    wait_apart(pe, out_even, ck.c + 1)
                half = slice(64 * t2, 64 * t2 + 64)
                for th in (0, 1):
                    for b in (0, 1):
                        at = 128 * th + 64 * b
                        t = 2 * th + t2
                        last = fmm(bk[64 * b:64 * b + 64, 64 * t:64 * t + 64], pT[half, at:at + 64],
                                   vv[half, ck.u, at:at + 64])
                last.then_inc(out_even if t2 == 0 else ring_full, 1)

            def bn_accumulate(ck, src, done):
                mm(bank[7][:, 0:CT * D], ones[:, :], src, start=False, stop=False,
                   skip_group_check=True).then_inc(done, 1)

            def ao_flat(ck):
                return tiles_of(ao, ck).rearrange("p t d -> p (t d)")

            def bn_sum_chunk(ck):
                ring.wait_emptied(pe, ck, "soft", "o")
                bn_accumulate(ck, ao_flat(ck), bn_sum)

            def clear_bank7():
                mm(bank[7][:, :], ones[0:1, :], zero[:, :], start=True, stop=False, skip_group_check=True)

            def soft_body(ck):
                if has(ck, 2):
                    soft_turn(later(ck, 2))
                if has(ck, 1):
                    soft_proj(later(ck, 1))
                soft_turn_p(ck)
                if has(ck, 1):
                    soft_scores(later(ck, 1))
                soft_out(ck, 0)
                if has(ck, -1):
                    bn_sum_chunk(later(ck, -1))
                soft_out(ck, 1)

            pe.wait_ge(b2_added, CHUNKS)
            clear_bank7()
            soft_turn(c0)
            soft_turn(Chunk(1, 1, 1, False))
            soft_proj(c0)
            soft_scores(c0)
            all_chunks(pe, soft_body, 4)
            bn_sum_chunk(Chunk(CHUNKS - 1, 1, CHUNKS - 1, False))

            pe.wait_ge(bn_mean, 1)
            clear_bank7()

            def bn_squares(ck):
                pe.wait_ge(bn_sq, ck.c + 1)
                bn_accumulate(ck, sq[:, ck.u, 0:CT * D], bn_var)

            all_chunks(pe, bn_squares)
            pe.wait_ge(bn_coef, 1)
            clear_bank7()

            def dense_turn(ck):
                pe.wait_ge(x16_ready, ck.c + 3 * CHUNKS)
                turn16(bank[6], ck.c, ck.c + 3 * CHUNKS + 1).then_inc(x16_turned, 1)
                for t in range(CT):
                    last = mm(bank[7][0:D, 0:S], xn[:, t, ck.u, :], fold, start=False, stop=False, skip_group_check=True)
                last.then_inc(feat_done, 1)

            all_chunks(pe, dense_turn)
            pe.wait_ge(x16_ready, 4 * CHUNKS)
            pe.wait_ge(gate_step, 1)
            fmm(bank[6][0:S, 0:E], feat[:, :], wr1[:, :]).then_inc(gate_pe, 1)
            pe.wait_ge(gate_step, GATE_SHIFTED + 3)
            nc.tensor.transpose(bank[6][0:E, 256:256 + S], gl[:, 3, :], ident[0:S, 0:S])
            for a in range(4):
                last = fmm(bank[7][:, S * a:S * a + S], gwx[:, 2 * a:2 * a + 2, :].rearrange("f e n -> f (e n)"),
                           ident[0:S, 0:S])
            last.then_inc(gate_pe, 1)
            pe.wait_ge(gate_step, GATE_STEPS - 1)
            fmm(bank[6][:, 384:384 + D], gwT[:, :, :].rearrange("e c f -> e (c f)"), bo1[:, :]).then_inc(gate_pe, 1)

            def dense_one(ck, k):
                ring.wait_free(pe, ck, "one", f"p{k}")
                xs = x16all[:, ck.c * CN:ck.c * CN + CN] if not ck.looped else x16all[:, DS(ck.c * CN, CN)]
                two_pass(bank_of(ck, "one", f"p{k}")[:, :], xs, "U", P * k, P * k + P, True).then_inc(ring_full, 1)

            def dense_two(ck, k):
                ring.wait_emptied(pe, ck, "one", f"p{k}")
                ring.wait_free(pe, ck, "two", f"p{k}", wait_apart)
                for e2 in (0, 1):
                    half = slice(64 * e2, 64 * e2 + 64)
                    last = fmm(bank_of(ck, "two", f"p{k}")[half, :], u2[half, k, :], h1[half, ck.u, k, :])
                last.then_inc(ring_full, 1)

            def dense_three(ck):
                pe.wait_ge(weighed, ck.c * 4 + 4)
                ring.wait_free(pe, ck, "three", "y")
                for t in range(CT):
                    for k in range(4):
                        last = fmm(bank_of(ck, "three", "y")[:, D * t:D * t + D], h2w[:, ck.u, k, P * t:P * t + P],
                                   uo[:, k, :], start=(k == 0), stop=(k == 3))
                last.then_inc(ring_full, 1)

            def dense_body(ck):
                nx = Chunk(ck.c + 1, 1 - ck.u, ck.near + 1, ck.looped)
                for k in range(4):
                    if ck.looped or ck.c + 1 < CHUNKS:
                        dense_one(nx, k)
                    dense_two(ck, k)
                    if k == 1 and (ck.looped or ck.c >= 1):
                        dense_three(three_chunk(ck))

            for k in range(4):
                dense_one(c0, k)
            all_chunks(pe, dense_body)
            dense_three(Chunk(CHUNKS - 1, 1, CHUNKS - 1, False))


_INS = ["x", "L0_tok_W", "L0_tok_b", "L0_attn_Wq", "L0_attn_Wk", "L0_attn_Wv", "L0_attn_Wo",
        "L0_ffn_gamma", "L0_ffn_beta", "L0_ffn_Wr", "L0_ffn_br", "L0_ffn_W1", "L0_ffn_b1", "L0_ffn_W2", "L0_ffn_b2",
        "L1_attn_Wq", "L1_attn_bq", "L1_attn_Wk", "L1_attn_bk", "L1_attn_Wv", "L1_attn_bv", "L1_attn_Wl", "L1_attn_bl",
        "L1_attn_gamma", "L1_attn_beta",
        "L1_ffn_Wr", "L1_ffn_br", "L1_ffn_W1", "L1_ffn_b1", "L1_ffn_g1", "L1_ffn_be1", "L1_ffn_m1", "L1_ffn_v1",
        "L1_ffn_W2", "L1_ffn_b2", "L1_ffn_g2", "L1_ffn_be2", "L1_ffn_m2", "L1_ffn_v2", "L1_ffn_Wo", "L1_ffn_bo"]


def shape_constants():
    import numpy as np

    r2 = 0.5 ** 0.5

    def haar(n, sign):
        m = np.zeros((n // 2, n))
        m[np.arange(n // 2), 2 * np.arange(n // 2)] = r2
        m[np.arange(n // 2), 2 * np.arange(n // 2) + 1] = sign * r2
        return m

    def resize(n, to=8):
        scale = n / to
        at = (np.arange(to) + 0.5) * scale - 0.5
        w = np.maximum(0, 1 - np.abs(at[:, None] - np.arange(n)[None, :]) / scale)
        return w / w.sum(1, keepdims=True)

    lo = haar(R, 1)
    ops = [resize(R // 4) @ haar(R // 2, 1) @ lo, resize(R // 4) @ haar(R // 2, -1) @ lo,
           resize(R // 2) @ lo, resize(R // 2) @ haar(R, -1)]
    c = np.zeros((P, 32 + P + S), np.float32)
    c[:R, :32] = np.concatenate(ops).T
    c[:, 32:32 + P] = np.eye(P)
    c[:, 32 + P:] = np.concatenate([np.eye(S), np.eye(S)])
    return c


def kernel(**inputs):
    import numpy as _np
    import concourse.bacc as _bacc
    from concourse import mybir as _mybir
    from concourse.bass_utils import run_bass_kernel_spmd as _run

    nc = _bacc.Bacc("TRN2", target_bir_lowering=False, num_devices=1)
    arrays, args = {}, []
    for name in _INS:
        a = _np.ascontiguousarray(inputs[name])
        arrays[f"in_{name}_dram"] = a
        args.append(nc.dram_tensor(f"in_{name}_dram", a.shape, _mybir.dt.from_np(a.dtype), kind="ExternalInput").ap())
    consts = shape_constants()
    arrays["shape_constants_dram"] = consts
    args.append(nc.dram_tensor("shape_constants_dram", consts.shape, _mybir.dt.float32, kind="ExternalInput").ap())
    args.append(nc.dram_tensor("out_0_dram", (B, S, D), _mybir.dt.float32, kind="ExternalOutput").ap())
    vit_tower(nc, *args)
    r = _run(nc, [arrays], core_ids=[0])
    return r.results[0]["out_0_dram"]
```

```python
from contextlib import ExitStack

import concourse.bass as bass
from concourse import mybir

F32 = mybir.dt.float32
F16 = mybir.dt.float16
I32 = mybir.dt.int32
ALU = mybir.AluOpType
ACT = mybir.ActivationFunctionType
AX = mybir.AxisListType
DS = bass.ds

P = 128
B = 128
S = 64
D = 64
R = 96
TILES = B // 2
CT = 4
CHUNKS = TILES // CT
CN = CT * P
HEADS = 8
E = 8
H0 = 128
NMAPS = 7
GROUP = 16
GROUPS = B // GROUP
EPS = 1e-5
BN_EPS_ATT = 1e-5
BN_EPS_FFN = 1e-3
BN_PARTS = (0, 16, 32, 46)
RING = 6

SEG = {}
_at = 0
for _name, _width in (("M", HEADS * D), ("N", HEADS * D), ("W1", E * H0), ("R", E),
                      ("Q", D), ("K", D), ("V", D), ("U", E * D)):
    SEG[_name] = (_at, _at + _width)
    _at += _width
WCOLS = _at
SEGS = list(SEG)

POOL_CONSTS = 5 + E
FTOK_ONES = 1
PERMUTED = 5
TURNED_READY = 8
PRODUCTS_MAX = 12
PRODUCTS_SPLIT = 20
EPS_ADDED = 28
FACTORS_READY = 38
WMAX_READY = 50
SPLIT_READY = 65
PREP_AT = (1, 2, 3, 4, 5, 6)
LN_STEPS = (2, 7, 2, 2)
RT_TANH = 13
RT_STEPS = 18
GATE_SHIFTED = 4
GATE_STEPS = 11


class Chunk:

    def __init__(self, c, u, near, looped):
        self.c, self.u, self.near, self.looped = c, u, near, looped


def all_chunks(eng, body, tail=2):
    for c in (0, 1):
        body(Chunk(c, c, c, False))
    with eng.Fori(1, (CHUNKS - tail) // 2) as i:
        for u in (0, 1):
            body(Chunk(i * 2 + u, u, 2 + u, True))
    for c in range(CHUNKS - tail, CHUNKS):
        body(Chunk(c, c % 2, c, False))


def later(ck, n):
    return Chunk(ck.c + n, (ck.u + n) % 2, ck.near + n, ck.looped)


def has(ck, n, tail=2):
    assert not ck.looped or n <= tail and n >= -2
    return ck.looped or 0 <= ck.c + n < CHUNKS


def wait_if(eng, sem, value):
    if isinstance(value, int) and value <= 0:
        return
    eng.wait_ge(sem, value)


class BankRing:

    def __init__(self, full, emptied):
        self.full, self.emptied, self.order, self.index = full, emptied, [], {}

    def plan(self, stage, chunk, names):
        for name, engine in names:
            self.index[stage, chunk, name] = len(self.order)
            self.order.append(engine)

    def fills(self, n):
        return n + 1 - self.order[:n + 1].count("-")

    def _value(self, ck, at):
        v0 = at(ck.near)
        if not ck.looped:
            return v0
        slope = (at(ck.near + 2) - v0) // 2
        for j in range(0, CHUNKS - 4, 2):
            assert at(ck.near + j) == v0 + slope * j
        return ck.c * slope + (v0 - slope * ck.near)

    def slot(self, ck, stage, name):
        n = self.index[stage, ck.near, name] % RING
        assert not ck.looped or self.index[stage, ck.near + 2, name] % RING == n
        return n

    def filled(self, ck, stage, name, back=0):
        return self._value(ck, lambda c: self.fills(self.index[stage, c - back, name]))

    def _emptied(self, ck, stage, name, uses_back):
        def place(c):
            n = self.index[stage, c, name] - uses_back
            while n >= 0 and self.order[n] == "-":
                n -= RING
            return n

        if place(ck.near) < 0:
            return None, 0
        e = self.order[place(ck.near)]

        def at(c):
            n = place(c)
            assert self.order[n] == e
            return self.order[:n + 1].count(e)

        return self.emptied[e], self._value(ck, at)

    def wait_free(self, pe, ck, stage, name, wait=wait_if):
        sem, value = self._emptied(ck, stage, name, RING)
        wait(pe, sem, value)

    def wait_emptied(self, eng, ck, stage, name, wait=wait_if):
        sem, value = self._emptied(ck, stage, name, 0)
        wait(eng, sem, value)


ATT_Q = [("q0", "V"), ("q1", "A"), ("q2", "V"), ("q3", "A")]
ATT_V = [("v0", "V"), ("v1", "V"), ("v2", "A"), ("v3", "V")]
ATT_S = [("s0", "A"), ("s1", "A"), ("s2", "A"), ("s3", "A")]


def plan_ring(ring):
    for c in range(CHUNKS):
        ring.plan("att", c, ATT_Q + ATT_V + ATT_S)
    ring.plan("up", 0, [(f"e{e}", "A") for e in range(E)])
    for c in range(CHUNKS):
        for t in range(CT):
            if c + 1 < CHUNKS:
                ring.plan("up", c + 1, [(f"e{e}", "A") for e in (2 * t, 2 * t + 1)])
            ring.plan("down", c, [(f"t{t}", "V")])
    ring.plan("soft", 0, [("q", "V"), ("k", "A"), ("v", "V"), ("s", "V")])
    for c in range(CHUNKS):
        if c + 1 < CHUNKS:
            ring.plan("soft", c + 1, [("q", "V"), ("k", "A"), ("v", "V")])
        ring.plan("soft", c, [("pt", "A")])
        if c + 1 < CHUNKS:
            ring.plan("soft", c + 1, [("s", "V")])
        ring.plan("soft", c, [("o", "V")])
    ring.plan("one", 0, [(f"p{k}", "AV"[k % 2]) for k in range(4)])
    for c in range(CHUNKS):
        for k in range(4):
            if c + 1 < CHUNKS:
                ring.plan("one", c + 1, [(f"p{k}", "AV"[k % 2])])
            ring.plan("two", c, [(f"p{k}", "AV"[k % 2])])
            if k == 1 and c >= 1:
                ring.plan("three", c - 1, [("z", "A")])
            if k == 2 and c >= 1:
                ring.plan("three", c - 1, [("y", "V"), ("skip", "-"), ("skip", "-")])
    ring.plan("three", CHUNKS - 1, [("z", "A"), ("y", "V")])


def vit_tower(nc, x, tok_W, tok_b, a_Wq, a_Wk, a_Wv, a_Wo, f_gamma, f_beta, f_Wr, f_br, f_W1, f_b1, f_W2, f_b2,
              s_Wq, s_bq, s_Wk, s_bk, s_Wv, s_bv, s_Wl, s_bl, s_gamma, s_beta,
              g_Wr, g_br, g_W1, g_b1, g_g1, g_be1, g_m1, g_v1, g_W2, g_b2, g_g2, g_be2, g_m2, g_v2, g_Wo, g_bo,
              shape_consts, out):
    with ExitStack() as ctx:
        def sb(name, shape, dt=F32):
            return ctx.enter_context(nc.sbuf_tensor(name, shape, dt))

        def sem(name):
            return ctx.enter_context(nc.semaphore(name))

        bank = [ctx.enter_context(nc.psum_tensor(f"bank{i}", [P, 512], F32)) for i in range(8)]

        h = sb("h", [P, TILES, D])
        consts = sb("consts", [P, 32 + P + S])
        resize = consts[0:R, 0:32]
        ident = consts[:, 32:32 + P]
        fold = consts[:, 32 + P:32 + P + S]
        ident16 = sb("ident16", [P, P], F16)
        ones = sb("ones", [P, P])

        wcat = sb("wcat", [P, WCOLS])
        whi = sb("whi", [P, WCOLS], F16)
        wlo = sb("wlo", [P, WCOLS], F16)
        wscale = sb("wscale", [P, len(SEGS)])
        winv = sb("winv", [P, len(SEGS)])
        wmax = sb("wmax", [P, 2, len(SEGS)])

        def seg(t, name):
            a, b = SEG[name]
            return t[:, a:b]

        def scale_of(t, name):
            k = SEGS.index(name)
            return t[:, k:k + 1]

        arena = sb("arena", [P, 8192])
        wb = sb("wb", [NMAPS + 1, D])
        rawqkv = arena[0:D, 0:1536].rearrange("g (w n) -> g w n", w=3)
        permqkv = arena[0:D, 1536:3072].rearrange("g (w a n) -> g w a n", w=3, a=4)
        wo_a = sb("wo_a", [P, HEADS, D])
        wT = arena[:, 3072:4608].rearrange("p (w a c g) -> p w a c g", w=3, a=4, c=2)
        w1raw = arena[:, 4608:5632]
        wrraw = sb("wrraw", [P, E])
        gamma0 = sb("gamma0", [P, 1])
        beta0 = sb("beta0", [D, 1])
        beta0_b = sb("beta0_b", [D, P])
        br_b = sb("br_b", [P, E])
        w2 = sb("w2", [P, E, D])
        b2blk = sb("b2blk", [CT * E, CT * D])
        rows = sb("rows", [48, P])
        cols = sb("cols", [P, 48])
        b1c = sb("b1c", [P, E])
        sig_scale = sb("sig_scale", [P, 1])
        wv1raw = sb("wv1raw", [D, D])
        wl1 = sb("wl1", [D, D])
        wv1T = sb("wv1T", [D, 2, D])
        bqk = sb("bqk", [P, 2])
        bv_c = sb("bv_c", [D, 1])
        bv_b = sb("bv_b", [D, P])
        vbias = sb("vbias", [P, D])
        bl_b = sb("bl_b", [P, D])
        bn_g = sb("bn_g", [P, D])
        bn_b = sb("bn_b", [P, D])
        u1raw = arena[:, 5632:6144].rearrange("p (e n) -> p e n", e=E)
        u2raw = sb("u2raw", [P, 4, D])
        u2 = sb("u2", [P, 4, D])
        uo = sb("uo", [P, 4, D])
        t12 = sb("t12", [P, 2, 4])
        s12 = sb("s12", [P, 2, 4])
        s1wide = sb("s1wide", [P, 4, P])
        s2wide = sb("s2wide", [P, 4, D])
        tmp4 = sb("tmp4", [P, 4])
        wr1 = sb("wr1", [D, E])
        br1_b = sb("br1_b", [S, E])
        bo1 = sb("bo1", [E, D])

        late = sb("late", [P, TILES * D])

        stage = sb("stage", [P, 4 * GROUP * R])
        img = stage[0:R, :].rearrange("r (g b c) -> r g b c", g=4, b=GROUP)
        zbuf = sb("zbuf", [R, 2, 4, P])
        fbuf = sb("fbuf", [P, 2, 56])
        ybuf = late[:, 2048:2048 + 4 * R]
        ftok = late[0:NMAPS + 1, 0:2 * GROUP * S].rearrange("m (u n) -> m u n", u=2)

        st = sb("st", [P, CT, 6])
        mv = sb("mv", [P, 2, CT, 2])
        rstd = sb("rstd", [P, 5, CT])
        xn = sb("xn", [P, CT, 2, D])
        xcat = sb("xcat", [P, CT, 2 * D], F16)
        x16 = sb("x16", [P, 2, CN], F16)
        x32 = sb("x32", [P, 2, CN])
        qbuf = arena[:, 0:2048].rearrange("p (a n) -> p a n", a=4)
        vbuf = arena[:, 2048:4096].rearrange("p (t n) -> p t n", t=CT)
        abuf = arena[:, 4096:6144].rearrange("p (t n) -> p t n", t=CT)
        gbuf = arena[:, 0:8192].rearrange("p (u e n) -> p u e n", u=2, e=E)
        resid = sb("resid", [P, 2, CT, D])
        lg = sb("lg", [P, 10, CT, E])
        top = sb("top", [P, 8, CT])
        iota = sb("iota", [P, CT, E])
        wtT = sb("wtT", [CT * E, P])
        prod = late.rearrange("p (u t e d) -> p u t e d", u=2, t=CT, e=E)
        qk = sb("qk", [P, 2, 2, 256])
        vv = sb("vv", [P, 2, 256])
        sc = sb("sc", [P, 256])
        pr = sb("pr", [P, 2, 256])
        mx = sb("mx", [P, 2, CT])
        rs = sb("rs", [P, 2, CT])
        pT = sb("pT", [P, 256])
        ao = late[:, :].rearrange("p (t d) -> p t d", t=TILES)
        mean_b = sb("mean_b", [P, D])
        bnA = sb("bnA", [P, D])
        bn_y = sb("bn_y", [P, D])
        bn_n = sb("bn_n", [P, D])
        zs = x32.rearrange("p u n -> p (u n)")[:, 0:CN]
        shift = sb("shift", [P, 2, CT])
        bn_acc = sb("bn_acc", [P, CT, D])
        sq_half = sb("sq_half", [P, 2, D])
        squares = stage[:, 0:TILES * D].rearrange("p (t d) -> p t d", t=TILES)
        x16all = sb("x16all", [P, TILES * P], F16)
        feat = sb("feat", [D, S])
        gl = sb("gl", [S, 4, E])
        gs = sb("gs", [S, 4])
        gwb = sb("gwb", [P, 4, S])
        gwx = sb("gwx", [S, E, D])
        gwT = sb("gwT", [E, 2, S])
        bow = sb("bow", [P, D])
        h1 = arena[:, 0:4096].rearrange("p (u a n) -> p u a n", u=2, a=4)
        h2 = arena[:, 4096:8192].rearrange("p (u a n) -> p u a n", u=2, a=4)
        h2w = stage[:, 0:8 * CN].rearrange("p (u a n) -> p u a n", u=2, a=4)
        zero = sb("zero", [1, 512])
        minus_half = sb("minus_half", [P, 1])
        ln_eps = sb("ln_eps", [P, CT])

        s_const, s_wa, s_wf = sem("consts_loaded"), sem("attention_weights_loaded"), sem("other_weights_loaded")
        s_wqkv, s_wp = sem("attention_weights"), sem("gpsimd_weights_loaded")
        s_img = [sem(f"images_loaded{i}") for i in range(4)]
        prep_pe, prep_dve, prep_pool = sem("prep_pe"), sem("prep_dve"), sem("prep_pool")
        rows_copied, rows_turned = sem("rows_copied_out"), sem("rows_turned")
        rows_done, z_copied, maps_done, maps_copied = (sem("rows_resized"), sem("rows_copied"), sem("maps_done"),
                                                       sem("maps_copied"))
        ft_done, ft_copied, tok_done, h_ready = (sem("maps_turned"), sem("turned_copied"), sem("tokens_done"),
                                                 sem("tokens_copied"))
        ring_full = sem("ring_full")
        act_emptied, dve_emptied = sem("act_emptied"), sem("dve_emptied")
        ln_stats, ln_aggr, ln_step = sem("ln_stats"), sem("ln_aggr"), sem("ln_step")
        n_shift = sem("norm_shift")
        n_scaled, n_hi, n_split = sem("norm_scaled"), sem("norm_hi"), sem("norm_split")
        x16_turned, x16_ready = sem("x16_turned"), sem("x16_ready")
        x32_turned, x32_ready = sem("x32_turned"), sem("x32_ready")
        av_done, av_relu, att_added = sem("av_done"), sem("av_relu"), sem("attention_added")
        rt_done, rt_step, rt_tanh = sem("router_done"), sem("router_step"), sem("router_tanh")
        wt_turned, wt_ready, b2_done, b2_added = (sem("weights_turned"), sem("weights_turned_copied"),
                                                  sem("b2_done"), sem("b2_added"))
        tree_step, moe_added = sem("expert_sum_step"), sem("experts_added")
        hx_added = sem("hx_added")
        sm_max, sm_exp, sm_sum = sem("score_max"), sem("score_exp"), sem("score_sum")
        sm_inv, out_even = sem("score_inverse"), sem("even_tiles_done")
        bn_sum, bn_mean, bn_cent, bn_sq, bn_var, bn_coef = (sem("bn_sum"), sem("bn_mean"), sem("bn_centred"),
                                                            sem("bn_squared"), sem("bn_var"), sem("bn_coef"))
        bn_total, bn_cent_pool = sem("bn_total"), sem("bn_centred_by_pool")
        bn_app, bn_step, bn_eps, bn_root = sem("bn_applied"), sem("bn_step"), sem("bn_eps"), sem("bn_root")
        feat_done, gate_step, gate_pe = sem("feat_done"), sem("gate_step"), sem("gate_pe")
        gate_exp = sem("gate_exp")
        bow_added, weighed, stored = sem("bo_added"), sem("hidden_weighed"), sem("stored")

        ring = BankRing(ring_full, {"A": act_emptied, "V": dve_emptied})
        plan_ring(ring)

        def ln_base(n, stage):
            extra = LN_STEPS[1] - LN_STEPS[0]
            return n * LN_STEPS[stage] + (0, -extra * CHUNKS, extra * CHUNKS, extra * CHUNKS)[stage]

        def wait_apart(eng, sem, value):
            if not isinstance(value, int):
                value = eng.to_reg(value)
                eng.wait_ge(s_const, 16)
            wait_if(eng, sem, value)

        def bank_of(ck, stage, name):
            return bank[ring.slot(ck, stage, name)]

        def tiles_of(t, ck):
            return t[:, ck.c * CT:ck.c * CT + CT, :] if isinstance(ck.c, int) else t[:, DS(ck.c * CT, CT), :]

        def bc(ap, shape):
            return ap.to_broadcast(shape)

        def minus_half_like(ap):
            half = minus_half[:, 0:1] if len(ap.shape) == 2 else minus_half[:, 0:1].unsqueeze(2)
            return bc(half, list(ap.shape))

        def ring_who(stage, k):
            return ring.order[ring.index[stage, 2, f"p{k}"]]

        block = ctx.enter_context(nc.Block())

        ATT_LOADS, TOKEN_W_LOADS, LATE_LOADS, POOL_LOADS = [], [], [], []
        for i, w in enumerate((a_Wq, a_Wk, a_Wv)):
            ATT_LOADS.append((rawqkv[:, i, :], w))
        for q in (0, D):
            ATT_LOADS.append((wo_a[q:q + D], a_Wo.rearrange("(k h) d -> k h d", h=HEADS)))
        for i, m in enumerate((0, 2, 1, 3, 5, 4, 6)):
            TOKEN_W_LOADS.append((wb[i:i + 1, :], tok_W[m:m + 1, :]))
        TOKEN_W_LOADS.append((wb[NMAPS:NMAPS + 1, :], tok_b.rearrange("(a d) -> a d", a=1)))
        for k, v in enumerate((g_b1, g_g1, g_be1, g_m1, g_v1, g_b2, g_g2, g_be2, g_m2, g_v2)):
            LATE_LOADS.append((rows[4 * k:4 * k + 4, :], v.rearrange("(a e) n -> a (e n)", e=2)))
        LATE_LOADS += [(rows[40:48, :], f_b1), (wv1raw[:, :], s_Wv), (wl1[:, :], s_Wl)]
        for q in (0, D):
            LATE_LOADS += [(w1raw[q:q + D, :].rearrange("p (e n) -> p e n", e=E), f_W1.rearrange("e d n -> d e n")),
                           (wrraw[q:q + D, :], f_Wr),
                           (gamma0[q:q + D, :], f_gamma.rearrange("(d a) -> d a", a=1)),
                           (u1raw[q:q + D], g_W1.rearrange("e d n -> d e n"))]
            POOL_LOADS += [(seg(wcat, "Q")[q:q + D, :], s_Wq), (seg(wcat, "K")[q:q + D, :], s_Wk)]
        LATE_LOADS += [(beta0[:, :], f_beta.rearrange("(d a) -> d a", a=1)),
                       (bv_c[:, :], s_bv.rearrange("(d a) -> d a", a=1))]
        POOL_LOADS += [(br_b[:, :], f_br.partition_broadcast(P)),
                       (bl_b[:, :], s_bl.partition_broadcast(P)),
                       (u2raw[:, :, :], g_W2.rearrange("(a e) n k -> (e n) a k", e=2)),
                       (w2[:, :, :], f_W2.rearrange("e n d -> n e d")),
                       (bn_g[:, :], s_gamma.partition_broadcast(P)),
                       (bn_b[:, :], s_beta.partition_broadcast(P)),
                       (uo[:, :, :], g_Wo.rearrange("(a e) n k -> (e n) a k", e=2)),
                       (wr1[:, :], g_Wr), (br1_b[:, :], g_br.partition_broadcast(S)), (bo1[:, :], g_bo)]
        for e2 in (0, 1):
            for k, v in enumerate((s_bq, s_bk)):
                POOL_LOADS.append((bqk[e2 * D:e2 * D + D, k:k + 1], v.rearrange("(d a) -> d a", a=1)))
        POOL_LOADS += [(b2blk[E * t:E * t + E, D * t:D * t + D], f_b2) for t in range(CT)]


        @block.sync
        def _(sp):
            sp.dma_start(consts[:, :], shape_consts).then_inc(s_const, 16)
            def load_images(g):
                sp.dma_start(img[:, g % 4], x[g * GROUP:(g + 1) * GROUP, 0].rearrange("b r c -> r b c")
                             ).then_inc(s_img[g % 4], 16)

            load_images(0)
            load_images(1)
            for dst, src in TOKEN_W_LOADS:
                sp.dma_start(dst, src).then_inc(s_wa, 16)
            load_images(2)
            for dst, src in ATT_LOADS:
                sp.dma_start(dst, src).then_inc(s_wqkv, 16)
            load_images(3)
            assert len(LATE_LOADS) <= 6 * (GROUPS - 4)
            for g in range(4, GROUPS):
                sp.wait_ge(rows_done, g - 3)
                load_images(g)
                for dst, src in LATE_LOADS[(g - 4) * 6:(g - 3) * 6]:
                    sp.dma_start(dst, src).then_inc(s_wf, 16)

            out_v = out.rearrange("(n p) t d -> (p t) n d", p=2)

            def store(ck):
                ring.wait_emptied(sp, ck, "three", "y")
                sp.dma_start(tiles_of(out_v, ck), tiles_of(h, ck)).then_inc(stored, 16)

            all_chunks(sp, store)
            sp.wait_ge(stored, 16 * CHUNKS)

        @block.gpsimd
        def _(pool):
            nc.gpsimd.memset(b2blk[:, :], 0.0).then_inc(prep_pool, 1)
            nc.gpsimd.memset(ones[:, :], 1.0).then_inc(prep_pool, 1)
            nc.gpsimd.memset(zero[:, :], 0.0).then_inc(prep_pool, 1)
            for e in range(E):
                nc.gpsimd.memset(iota[:, :, e:e + 1], float(e)).then_inc(prep_pool, 1)
            nc.gpsimd.memset(minus_half[:, :], -0.5).then_inc(prep_pool, 1)
            nc.gpsimd.memset(ln_eps[:, :], EPS).then_inc(prep_pool, 1)
            pool.wait_ge(prep_pool, POOL_CONSTS)
            for dst, src in POOL_LOADS:
                pool.dma_start(dst, src).then_inc(s_wp, 16)
            def inverse_root(dst, src):
                return nc.gpsimd.tensor_tensor(dst, src, minus_half_like(src), ALU.pow)

            def max_over_partitions(a, b):
                nc.gpsimd.partition_all_reduce(wmax[:, 1, a:b], wmax[:, 0, a:b], P, bass.bass_isa.ReduceOp.max
                                               ).then_inc(prep_pool, 1)

            pool.wait_ge(prep_dve, PRODUCTS_MAX)
            max_over_partitions(0, 2)
            pool.wait_ge(prep_dve, EPS_ADDED)
            inverse_root(s12[:, :, :], s12[:, :, :]).then_inc(prep_pool, 1)

            def roots_of(n, u, stage):
                base, k = ln_base(n, stage), [0]

                def ln(ins):
                    k[0] += 1
                    ins.then_inc(ln_step, 1)

                def ln_wait():
                    pool.wait_ge(ln_step, base + k[0])

                double = stage == 1
                var = mv[:, u, :, 1]
                pool.wait_ge(ln_aggr, n + 1)
                wait_if(pool, n_scaled, n - 1)
                ln(nc.gpsimd.tensor_tensor(rstd[:, 2, :], var, ln_eps[:, :], ALU.add))
                ln_wait()
                ln(inverse_root(rstd[:, 3 if double else u, :], rstd[:, 2, :]))
                if double:
                    ln_wait()
                    ln(nc.gpsimd.tensor_tensor(rstd[:, 4, :], rstd[:, 3, :], var, ALU.mult))
                    ln_wait()
                    ln(nc.gpsimd.tensor_tensor(rstd[:, 2, :], rstd[:, 4, :], rstd[:, 3, :], ALU.mult))
                    ln_wait()
                    ln(nc.gpsimd.tensor_tensor(rstd[:, 4, :], rstd[:, 2, :], ln_eps[:, :], ALU.add))
                    ln_wait()
                    ln(inverse_root(rstd[:, 2, :], rstd[:, 4, :]))
                    ln_wait()
                    ln(nc.gpsimd.tensor_tensor(rstd[:, u, :], rstd[:, 2, :], rstd[:, 3, :], ALU.mult))
                assert k[0] == LN_STEPS[stage]

            def low_part(ck, n, stage):
                pool.wait_ge(n_hi, n + 1)
                nc.gpsimd.tensor_tensor(xcat[:, :, D:2 * D], xn[:, :, ck.u if stage else 0, :], xcat[:, :, 0:D],
                                        ALU.subtract).then_inc(n_split, 1)

            def attention_body(ck):
                roots_of(ck.c + 2, ck.u, 0 if has(ck, 2) else 1)
                pool.wait_ge(av_relu, ck.c + 1)
                nc.gpsimd.tensor_tensor(tiles_of(h, ck), tiles_of(h, ck), resid[:, ck.u], ALU.add
                                        ).then_inc(att_added, 1)
                low_part(later(ck, 2), ck.c + 2, 0 if has(ck, 2) else 1)

            for c in (0, 1):
                roots_of(c, c % 2, 0)
                low_part(Chunk(c, c, c, False), c, 0)
            def attention_and_prep(ck):
                attention_body(ck)
                if not ck.looped and ck.c == 0:
                    pool.wait_ge(prep_dve, WMAX_READY)
                    max_over_partitions(2, len(SEGS))

            all_chunks(pool, attention_and_prep)

            def expert_sum(ck):
                y = prod[:, ck.u]
                ring.wait_emptied(pool, ck, "down", f"t{CT - 1}")
                nc.gpsimd.tensor_tensor(y[:, :, 0:4, :], y[:, :, 0:4, :], y[:, :, 4:8, :], ALU.add
                                        ).then_inc(tree_step, 1)
                pool.wait_ge(tree_step, ck.c * 3 + 1)
                nc.gpsimd.tensor_tensor(y[:, :, 0:2, :], y[:, :, 0:2, :], y[:, :, 2:4, :], ALU.add
                                        ).then_inc(tree_step, 1)
                pool.wait_ge(tree_step, ck.c * 3 + 2)
                nc.gpsimd.tensor_tensor(y[:, :, 0, :], y[:, :, 0, :], y[:, :, 1, :], ALU.add
                                        ).then_inc(tree_step, 1)
                pool.wait_ge(tree_step, ck.c * 3 + 3)
                pool.wait_ge(b2_added, ck.c + 1)
                nc.gpsimd.tensor_tensor(tiles_of(h, ck), tiles_of(h, ck), y[:, :, 0, :], ALU.add
                                        ).then_inc(moe_added, 1)

            def moe_body(ck):
                roots_of(ck.c + CHUNKS + 3, 1 - ck.u, 1 if has(ck, 3, 4) else 2)
                if has(ck, -1):
                    expert_sum(later(ck, -1))
                if has(ck, 3, 4):
                    low_part(later(ck, 3), ck.c + CHUNKS + 3, 1)
                else:
                    add_x(later(ck, 3 - CHUNKS))

            def add_x(ck):
                low_part(ck, ck.c + 2 * CHUNKS, 2)
                nc.gpsimd.tensor_tensor(tiles_of(h, ck), tiles_of(h, ck), xn[:, :, ck.u, :], ALU.add
                                        ).then_inc(hx_added, 1)

            for c in (2,):
                roots_of(c + CHUNKS, c % 2, 1)
                low_part(Chunk(c, c % 2, c, False), c + CHUNKS, 1)
            all_chunks(pool, moe_body, 4)
            expert_sum(Chunk(CHUNKS - 1, 1, CHUNKS - 1, False))

            def soft_body(ck):
                if has(ck, 3, 4):
                    roots_of(ck.c + 2 * CHUNKS + 3, 1 - ck.u, 2)
                if has(ck, -1):
                    accumulate(later(ck, -1))
                if has(ck, 3, 4):
                    add_x(later(ck, 3))

            def accumulate(ck):
                ring.wait_emptied(pool, ck, "soft", "o")
                if not ck.looped and ck.c == 0:
                    nc.gpsimd.tensor_copy(bn_acc[:, :, :], tiles_of(ao, ck)).then_inc(bn_sum, 1)
                    return
                pool.wait_ge(bn_sum, ck.c)
                nc.gpsimd.tensor_tensor(bn_acc[:, :, :], bn_acc[:, :, :], tiles_of(ao, ck), ALU.add
                                        ).then_inc(bn_sum, 1)

            all_chunks(pool, soft_body, 4)

            accumulate(Chunk(CHUNKS - 1, 1, CHUNKS - 1, False))

            pool.wait_ge(bn_mean, 1)
            a = BN_PARTS[-1]
            nc.gpsimd.tensor_tensor(ao[:, a:, :], ao[:, a:, :], bc(mean_b[:, :].unsqueeze(1), [P, TILES - a, D]),
                                    ALU.subtract).then_inc(bn_cent_pool, 1)

            def bn_apply(ck):
                pool.wait_ge(bn_coef, 1)
                nc.gpsimd.tensor_tensor(tiles_of(ao, ck), tiles_of(ao, ck), bc(bnA[:, :].unsqueeze(1), [P, CT, D]),
                                        ALU.mult).then_inc(bn_app, 1)

            def apply_body(ck):
                if has(ck, 1):
                    bn_apply(later(ck, 1))
                roots_of(ck.c + 3 * CHUNKS, ck.u, 3)
                if has(ck, -1):
                    low_part(later(ck, -1), ck.c + 3 * CHUNKS - 1, 3)

            bn_apply(Chunk(0, 0, 0, False))
            all_chunks(pool, apply_body)
            low_part(Chunk(CHUNKS - 1, 1, CHUNKS - 1, False), 4 * CHUNKS - 1, 3)

            def add_bo(ck):
                pool.wait_ge(gate_step, GATE_STEPS)
                nc.gpsimd.tensor_tensor(tiles_of(h, ck), tiles_of(h, ck), bc(bow[:, :].unsqueeze(1), [P, CT, D]),
                                        ALU.add).then_inc(bow_added, 1)

            def dense_body(ck):
                if not ck.looped and ck.c == 0:
                    pool.wait_ge(gate_step, GATE_STEPS - 1)
                for k in range(4):
                    ring.wait_emptied(pool, ck, "two", f"p{k}")
                    if k == 0 and (ck.looped or ck.c >= 2):
                        pool.wait_ge(ring_full, ring.filled(ck, "three", "z", 2))
                    nc.gpsimd.tensor_tensor(h2w[:, ck.u, k, :].rearrange("p (b f) -> p b f", f=S),
                                            h2[:, ck.u, k, :].rearrange("p (b f) -> p b f", f=S),
                                            bc(gwb[:, k, :].unsqueeze(1), [P, 2 * CT, S]), ALU.mult
                                            ).then_inc(weighed, 1)
                add_bo(ck)

            all_chunks(pool, dense_body)

        @block.scalar
        def _(act):
            def copy(dst, src):
                return nc.scalar.activation(dst, src, ACT.Copy)

            def copy_rows(g):
                act.wait_ge(rows_done, g + 1)
                wait_if(act, rows_turned, g)
                copy(ybuf, bank[0][:, 0:4 * R]).then_inc(rows_copied, 1)

            def copy_z(g):
                act.wait_ge(rows_turned, g + 1)
                if g >= 2:
                    act.wait_ge(maps_done, g - 1)
                copy(zbuf[:, g % 2].rearrange("c o (b i) -> c o b i", b=GROUP),
                     bank[1][0:R, :].rearrange("c (b o i) -> c o b i", b=GROUP, o=4)).then_inc(z_copied, 1)

            def copy_turned_maps(g):
                u = g % 2
                act.wait_ge(ft_done, g + 1)
                if g >= 2:
                    act.wait_ge(tok_done, g - 1)
                else:
                    act.wait_ge(prep_dve, FTOK_ONES)
                for q in (0, 1):
                    last = copy(ftok[0:NMAPS, u].rearrange("m (b j) -> m b j", j=8)[:, :, 4 * q:4 * q + 4],
                                bank[4 + q][0:NMAPS, :].rearrange("m (j b) -> m b j", j=4))
                last.then_inc(ft_copied, 1)

            copy_rows(0)
            copy_z(0)
            copy_rows(1)
            for g in range(GROUPS):
                copy_turned_maps(g)
                if g + 1 < GROUPS:
                    copy_z(g + 1)
                if g + 2 < GROUPS:
                    copy_rows(g + 2)

            def high_part(ck, n, stage):
                act.wait_ge(n_scaled, n + 1)
                wait_if(act, x16_turned, n)
                copy(xcat[:, :, 0:D], xn[:, :, ck.u if stage else 0, :]).then_inc(n_hi, 1)

            def att_x16(ck):
                act.wait_ge(x16_turned, ck.c + 1)
                if ck.looped or ck.c >= 2:
                    act.wait_ge(av_done, ck.c - 1)
                copy(x16[:, ck.u, :], bank[6][:, :].bitcast(F16)[:, 0:CN]).then_inc(x16_ready, 1)

            def att_empty(ck, name, dst, func=None):
                act.wait_ge(ring_full, ring.filled(ck, "att", name))
                if func is None:
                    copy(dst, bank_of(ck, "att", name)[:, :]).then_inc(act_emptied, 1)
                else:
                    nc.scalar.activation(dst, bank_of(ck, "att", name)[:, :], func, scale=sig_scale[:, 0:1]
                                         ).then_inc(act_emptied, 1)

            def attention_body(ck):
                wait_if(act, av_done, ck.c)
                for k, (name, who) in enumerate(ATT_Q):
                    if who == "A":
                        att_empty(ck, name, qbuf[:, k, :])
                if ck.looped or ck.c + 1 < CHUNKS:
                    att_x16(Chunk(ck.c + 1, 1 - ck.u, ck.near + 1, ck.looped))
                for t, (name, who) in enumerate(ATT_V):
                    if who == "A":
                        att_empty(ck, name, vbuf[:, t, :])
                for t in range(CT):
                    att_empty(ck, f"s{t}", abuf[:, t, :], ACT.Sigmoid)
                high_part(later(ck, 2), ck.c + 2, 0 if has(ck, 2) else 1)
                act.wait_ge(av_done, ck.c + 1)
                if ck.looped or ck.c >= 2:
                    act.wait_ge(att_added, ck.c - 1)
                nc.scalar.activation(resid[:, ck.u].rearrange("p t d -> p (t d)"), bank[7][:, 0:CT * D], ACT.Relu,
                                     scale=scale_of(wscale, "N")).then_inc(av_relu, 1)

            high_part(Chunk(0, 0, 0, False), 0, 0)
            act.wait_ge(prep_dve, PRODUCTS_SPLIT)
            att_x16(Chunk(0, 0, 0, False))
            high_part(Chunk(1, 1, 1, False), 1, 0)
            all_chunks(act, attention_body)

            def moe_x16(ck):
                act.wait_ge(x16_turned, ck.c + CHUNKS + 1)
                if ck.looped or ck.c >= 2:
                    act.wait_ge(ring_full, ring.filled(ck, "up", f"e{E - 1}", 2))
                copy(x16[:, ck.u, :], bank[6][:, :].bitcast(F16)[:, 0:CN]).then_inc(x16_ready, 1)

            def soft_x16(ck):
                act.wait_ge(x16_turned, ck.c + 2 * CHUNKS + 1)
                if ck.looped or ck.c >= 2:
                    act.wait_ge(ring_full, ring.filled(ck, "soft", "v", 2))
                else:
                    act.wait_ge(ring_full, ring.fills(ring.index["up", CHUNKS - 2 + ck.c, f"e{E - 1}"]))
                copy(x16[:, ck.u, :], bank[6][:, :].bitcast(F16)[:, 0:CN]).then_inc(x16_ready, 1)

            def gelu(ck, e):
                act.wait_ge(ring_full, ring.filled(ck, "up", f"e{e}"))
                nc.scalar.activation(gbuf[:, ck.u, e, :], bank_of(ck, "up", f"e{e}")[:, :], ACT.Gelu,
                                     bias=b1c[:, e:e + 1], scale=scale_of(wscale, "W1")).then_inc(act_emptied, 1)

            def router_tanh(ck):
                act.wait_ge(rt_step, ck.c * RT_STEPS + RT_TANH)
                nc.scalar.activation(top[:, 3, :], top[:, 2, :], ACT.Tanh, scale=0.5).then_inc(rt_tanh, 1)

            def moe_body(ck):
                nx = later(ck, 1)
                if has(ck, 2):
                    moe_x16(later(ck, 2))
                else:
                    soft_x16(later(ck, 2 - CHUNKS))
                for t in range(CT):
                    if has(ck, 1):
                        for e in (2 * t, 2 * t + 1):
                            if e == 0 and has(ck, -1):
                                act.wait_ge(ring_full, ring.filled(ck, "down", f"t{CT - 1}", 1))
                            gelu(nx, e)
                        if t == 2:
                            router_tanh(nx)
                    if t == 3:
                        high_part(later(ck, 3), ck.c + CHUNKS + 3, 1)

            for c in range(2):
                moe_x16(Chunk(c, c % 2, c, False))
            high_part(Chunk(2, 0, 2, False), 2 + CHUNKS, 1)
            act.wait_ge(av_done, CHUNKS)
            act.wait_ge(prep_dve, SPLIT_READY)
            for e in range(E):
                gelu(Chunk(0, 0, 0, False), e)
                if e == 2:
                    router_tanh(Chunk(0, 0, 0, False))
            all_chunks(act, moe_body, 4)

            def soft_k(ck):
                act.wait_ge(ring_full, ring.filled(ck, "soft", "k"))
                if ck.looped or ck.c >= 2:
                    act.wait_ge(ring_full, ring.filled(ck, "soft", "s", 2))
                nc.scalar.activation(qk[:, ck.u, 1, :], bank_of(ck, "soft", "k")[:, 0:256], ACT.Identity,
                                     bias=bqk[:, 1:2], scale=scale_of(wscale, "K")).then_inc(act_emptied, 1)

            def soft_exp(ck):
                ring.wait_emptied(act, ck, "soft", "s")
                if ck.looped or ck.c >= 2:
                    act.wait_ge(ring_full, ring.filled(ck, "soft", "pt", 2))
                    act.wait_ge(sm_sum, ck.c - 1)
                nc.scalar.activation(pr[:, ck.u, :], sc[:, :], ACT.Exp, scale=1.0 / D).then_inc(sm_exp, 1)

            def soft_body(ck):
                if has(ck, 2):
                    soft_x16(later(ck, 2))
                if has(ck, 1):
                    soft_k(later(ck, 1))
                act.wait_ge(ring_full, ring.filled(ck, "soft", "pt"))
                if has(ck, -1):
                    act.wait_ge(ring_full, ring.filled(ck, "soft", "o", 1))
                copy(pT[:, :], bank_of(ck, "soft", "pt")[:, 0:256]).then_inc(act_emptied, 1)
                if has(ck, 3, 4):
                    high_part(later(ck, 3), ck.c + 2 * CHUNKS + 3, 2)
                if has(ck, 1):
                    soft_exp(later(ck, 1))

            soft_k(Chunk(0, 0, 0, False))
            soft_exp(Chunk(0, 0, 0, False))
            all_chunks(act, soft_body, 4)

            for i, (a, b) in enumerate(zip(BN_PARTS, BN_PARTS[1:] + (TILES,))):
                if b < TILES:
                    act.wait_ge(bn_cent, i + 1)
                else:
                    act.wait_ge(bn_cent_pool, 1)
                nc.scalar.activation(squares[:, a:b, :], ao[:, a:b, :], ACT.Square).then_inc(bn_sq, 1)
            act.wait_ge(bn_eps, 1)
            nc.scalar.activation(bn_y[:, :], bnA[:, :], ACT.Sqrt).then_inc(bn_root, 1)

            def dense_x16(ck):
                act.wait_ge(x16_turned, ck.c + 3 * CHUNKS + 1)
                dst = x16all[:, ck.c * CN:ck.c * CN + CN] if not ck.looped else x16all[:, DS(ck.c * CN, CN)]
                copy(dst, bank[6][:, :].bitcast(F16)[:, 0:CN]).then_inc(x16_ready, 1)

            def scale_dense(ck):
                n = ck.c + 3 * CHUNKS
                act.wait_ge(n_shift, ck.c + 1)
                if has(ck, -2):
                    act.wait_ge(n_split, n - 1)
                    act.wait_ge(feat_done, ck.c - 1)
                for t in range(CT):
                    src = h[:, ck.c * CT + t, :] if not ck.looped else h[:, DS(ck.c * CT + t, 1), :]
                    last = nc.scalar.activation(xn[:, t, ck.u, :], src, ACT.Identity, bias=shift[:, ck.u, t:t + 1],
                                                scale=rstd[:, ck.u, t:t + 1])
                last.then_inc(n_scaled, 1)

            def turn_body(ck):
                scale_dense(ck)
                high_part(ck, ck.c + 3 * CHUNKS, 3)
                if has(ck, -1):
                    dense_x16(later(ck, -1))

            all_chunks(act, turn_body)
            dense_x16(Chunk(CHUNKS - 1, 1, CHUNKS - 1, False))

            def dense_relu(ck, stage, k, dst, bias):
                act.wait_ge(ring_full, ring.filled(ck, stage, f"p{k}"))
                nc.scalar.activation(dst, bank_of(ck, stage, f"p{k}")[:, :], ACT.Relu, bias=bias
                                     ).then_inc(act_emptied, 1)

            for k in range(4):
                if ring_who("one", k) == "A":
                    dense_relu(Chunk(0, 0, 0, False), "one", k, h1[:, 0, k, :], t12[:, 0, k:k + 1])

            act.wait_ge(gate_step, GATE_SHIFTED)
            nc.scalar.activation(gl[:, 2, :], gl[:, 1, :], ACT.Exp, accum_out=gs[:, 1:2]).then_inc(gate_exp, 1)

            def dense_body(ck):
                if ck.looped or ck.c >= 2:
                    act.wait_ge(weighed, ck.c * 4 - 4)
                for k in range(4):
                    if ring_who("one", k) == "A" and (ck.looped or ck.c + 1 < CHUNKS):
                        dense_relu(Chunk(ck.c + 1, 1 - ck.u, ck.near + 1, ck.looped), "one", k,
                                   h1[:, 1 - ck.u, k, :], t12[:, 0, k:k + 1])
                    if ring_who("two", k) == "A":
                        dense_relu(ck, "two", k, h2[:, ck.u, k, :], t12[:, 1, k:k + 1])
                    if k == 1 and has(ck, -1):
                        copy_z(later(ck, -1))

            def copy_z(ck):
                act.wait_ge(ring_full, ring.filled(ck, "three", "z"))
                if has(ck, -1):
                    act.wait_ge(ring_full, ring.filled(ck, "three", "y", 1))
                copy(zs[:, :], bank_of(ck, "three", "z")[:, :]).then_inc(act_emptied, 1)

            all_chunks(act, dense_body)
            copy_z(Chunk(CHUNKS - 1, 1, CHUNKS - 1, False))

        @block.vector
        def _(dve):
            v = nc.vector
            step = [0]

            def link(ins):
                step[0] += 1
                ins.then_inc(prep_dve, 1)
                dve.wait_ge(prep_dve, step[0])

            link(v.memset(ftok[:, :, :], 1.0))
            assert step[0] == FTOK_ONES
            dve.wait_ge(s_const, 16)
            link(v.tensor_copy(ident16[:, :], ident))

            def prep_turned():
                dve.wait_ge(s_wqkv, 16 * len(ATT_LOADS))
                for w in range(3):
                    link(v.tensor_copy(permqkv[:, w].rearrange("g a (e k) -> g a e k", e=2),
                                       rawqkv[:, w, :].rearrange("g (k a e) -> g a e k", a=4, e=2)))
                assert step[0] == PERMUTED
                for w in range(3):
                    dve.wait_ge(prep_pe, 1 if w < 2 else 2)
                    src = bank[6][:, 256 * w:256 * w + 256] if w < 2 else bank[7][:, 0:256]
                    link(v.tensor_copy(wT[:, w], bc(src.rearrange("p (a g) -> p a g", a=4).unsqueeze(2), [P, 4, 2, D])))
                assert step[0] == TURNED_READY

            def magnitudes(names):
                for name in names:
                    k = SEGS.index(name)
                    link(v.tensor_reduce(wmax[:, 0, k:k + 1], seg(wcat, name), AX.X, ALU.max, apply_absolute_value=True))

            def scales(a, b):
                link(v.tensor_scalar(wscale[:, a:b], wmax[:, 1, a:b], 2.0 ** -100, 2.0 ** 100, ALU.max, ALU.min))
                link(v.tensor_scalar(wscale[:, a:b].bitcast(I32), wscale[:, a:b].bitcast(I32), 0x7F800000, None,
                                     ALU.bitwise_and))
                link(v.reciprocal(winv[:, a:b], wscale[:, a:b]))
                for name in SEGS[a:b]:
                    link(v.tensor_scalar(seg(wcat, name), seg(wcat, name), scale_of(winv, name), None, ALU.mult))

            def parts(a, b):
                link(v.tensor_copy(whi[:, a:b], wcat[:, a:b]))
                link(v.tensor_tensor(wlo[:, a:b], wcat[:, a:b], whi[:, a:b], ALU.subtract))

            def prep_products():
                dve.wait_ge(prep_pe, 4)
                link(v.tensor_copy(seg(wcat, "M"), bank[6][:, :]))
                link(v.tensor_copy(seg(wcat, "N"), bank[7][:, :]))
                magnitudes(("M", "N"))
                assert step[0] == PRODUCTS_MAX

            def prep_products_split():
                dve.wait_ge(prep_pool, POOL_CONSTS + 1)
                scales(0, 2)
                parts(0, 2 * HEADS * D)
                link(v.tensor_scalar(sig_scale[:, :], scale_of(wscale, "M"), 8.0, None, ALU.mult))
                assert step[0] == PRODUCTS_SPLIT

            def prep_vectors():
                dve.wait_ge(s_wf, 16 * len(LATE_LOADS))
                link(v.tensor_scalar(seg(wcat, "W1"), w1raw[:, :], gamma0[:, 0:1], None, ALU.mult))
                link(v.tensor_scalar(seg(wcat, "R"), wrraw[:, :], gamma0[:, 0:1], None, ALU.mult))
                link(v.tensor_copy(bv_b[:, :], bc(bv_c[:, 0:1], [D, P])))
                link(v.tensor_copy(beta0_b[:, :], bc(beta0[:, 0:1], [D, P])))
                dve.wait_ge(prep_pe, 5)
                link(v.tensor_copy(wv1T[:, :, :], bc(bank[7][0:D, 256:320].unsqueeze(1), [D, 2, D])))
                link(v.tensor_copy(cols[:, :], bank[7][:, 320:368]))
                for l in (0, 1):
                    link(v.tensor_scalar(s12[:, l, :], cols[:, 20 * l + 16:20 * l + 20], BN_EPS_FFN, None, ALU.add))
                assert step[0] == EPS_ADDED

            def prep_factors():
                dve.wait_ge(prep_pool, POOL_CONSTS + 2)
                for l in (0, 1):
                    b_, g_, be_, m_ = (cols[:, 20 * l + 4 * k:20 * l + 4 * k + 4] for k in range(4))
                    link(v.tensor_tensor(s12[:, l, :], s12[:, l, :], g_, ALU.mult))
                    link(v.tensor_tensor(tmp4[:, :], b_, m_, ALU.subtract))
                    link(v.tensor_tensor(tmp4[:, :], tmp4[:, :], s12[:, l, :], ALU.mult))
                    link(v.tensor_tensor(t12[:, l, :], tmp4[:, :], be_, ALU.add))
                link(v.tensor_copy(s1wide[:, :, :], bc(s12[:, 0, :].unsqueeze(2), [P, 4, P])))
                link(v.tensor_copy(s2wide[:, :, :], bc(s12[:, 1, :].unsqueeze(2), [P, 4, D])))
                assert step[0] == FACTORS_READY

            def prep_small():
                dve.wait_ge(s_wp, 16 * len(POOL_LOADS))
                dve.wait_ge(prep_pe, 6)
                link(v.tensor_tensor(seg(wcat, "U"), u1raw[:, :, :].rearrange("p e n -> p (e n)"), bank[6][:, :], ALU.mult))
                link(v.tensor_tensor(u2[:, :, :], u2raw[:, :, :], bank[7][:, 256:512].rearrange("p (a n) -> p a n", a=4),
                                     ALU.mult))
                link(v.tensor_copy(seg(wcat, "V"), bank[7][:, 0:D]))
                link(v.tensor_tensor(vbias[:, :], bank[7][:, 64:128], bl_b[:, :], ALU.add))
                link(v.tensor_tensor(br_b[:, :], bank[7][:, 128:128 + E], br_b[:, :], ALU.add))
                link(v.tensor_tensor(b1c[:, :], bank[7][:, 192:192 + E], cols[:, 40:48], ALU.add))

            def prep_rest(c):
                if c == 0:
                    magnitudes(SEGS[2:])
                    assert step[0] == WMAX_READY
                elif c == 1:
                    dve.wait_ge(prep_pool, POOL_CONSTS + 3)
                    scales(2, len(SEGS))
                elif c == CHUNKS - 2:
                    parts(SEG["W1"][0], SEG["R"][1])
                    link(v.tensor_scalar(t12[:, 0, :], t12[:, 0, :], scale_of(winv, "U"), None, ALU.mult))
                    link(v.tensor_scalar(u2[:, :, :], u2[:, :, :], scale_of(wscale, "U"), None, ALU.mult))
                elif c == CHUNKS - 1:
                    parts(SEG["Q"][0], WCOLS)
                    assert step[0] == SPLIT_READY

            def tok_maps(g):
                dve.wait_ge(maps_done, g + 1)
                if g >= 2:
                    dve.wait_ge(ft_done, g - 1)
                v.tensor_copy(fbuf[:, g % 2, :], bank[2][:, 0:56]).then_inc(maps_copied, 1)

            def tok_h(g):
                dve.wait_ge(tok_done, g + 1)
                n = GROUP // 2
                v.tensor_copy(h[:, g * n:(g + 1) * n, :].rearrange("p t d -> p (t d)"), bank[3][:, :]
                              ).then_inc(h_ready, 1)

            tok_maps(0)
            for g in range(GROUPS):
                if g + 1 < GROUPS:
                    tok_maps(g + 1)
                tok_h(g)
                if g in PREP_AT:
                    (prep_turned, prep_products, prep_products_split, prep_vectors, prep_factors,
                     prep_small)[PREP_AT.index(g)]()

            def statistics(ck, n, ready=None):
                if ready:
                    wait_apart(dve, *ready)
                for t in range(CT):
                    src = h[:, ck.c * CT + t, :] if not ck.looped else h[:, DS(ck.c * CT + t, 1), :]
                    v.bn_stats(st[:, t, :], src).then_inc(ln_stats, 1)
                wait_apart(dve, ln_stats, n * CT + CT)
                wait_apart(dve, n_scaled, n - 1)
                for t in range(CT):
                    last = v.bn_aggr(mv[:, ck.u, t, :], st[:, t, :])
                last.then_inc(ln_aggr, 1)

            def scale(ck, n, stage, *readers):
                dve.wait_ge(ln_step, ln_base(n, stage) + LN_STEPS[stage])
                wait_if(dve, n_split, n - 1 if stage else n)
                for sem_, value in readers:
                    wait_if(dve, sem_, value)
                for t in range(CT):
                    src = h[:, ck.c * CT + t:ck.c * CT + t + 1, :] if not ck.looped else h[:, DS(ck.c * CT + t, 1), :]
                    dst = xn[:, t, :, :] if stage == 0 else xn[:, t, ck.u:ck.u + 1, :]
                    last = v.tensor_scalar(dst, src if stage else bc(src, [P, 2, D]), mv[:, ck.u, t, 0:1],
                                           rstd[:, ck.u, t:t + 1],
                                           ALU.subtract, ALU.mult)
                last.then_inc(n_scaled, 1)

            def att_empty(ck, name, dst):
                dve.wait_ge(ring_full, ring.filled(ck, "att", name))
                v.tensor_copy(dst, bank_of(ck, "att", name)[:, :]).then_inc(dve_emptied, 1)

            def att_x32(ck):
                dve.wait_ge(x32_turned, ck.c + 1)
                if ck.looped or ck.c >= 2:
                    dve.wait_ge(av_done, ck.c - 1)
                v.tensor_copy(x32[:, ck.u, :], bank[6][:, :]).then_inc(x32_ready, 1)

            def attention_body(ck):
                wait_if(dve, av_done, ck.c)
                for k, (name, who) in enumerate(ATT_Q):
                    if who == "V":
                        att_empty(ck, name, qbuf[:, k, :])
                if has(ck, 2):
                    statistics(later(ck, 2), ck.c + 2)
                else:
                    stats_moe(later(ck, 2 - CHUNKS))
                for t, (name, who) in enumerate(ATT_V):
                    if who == "V":
                        att_empty(ck, name, vbuf[:, t, :])
                if has(ck, 1):
                    att_x32(later(ck, 1))
                if has(ck, 2):
                    scale(later(ck, 2), ck.c + 2, 0)
                else:
                    scale(later(ck, 2 - CHUNKS), ck.c + 2, 1, (x32_turned, CHUNKS))
                if not ck.looped:
                    prep_rest(ck.c)

            def stats_moe(ck):
                statistics(ck, ck.c + CHUNKS, (att_added, ck.c + 1))

            dve.wait_ge(h_ready, GROUPS)
            statistics(Chunk(0, 0, 0, False), 0)
            scale(Chunk(0, 0, 0, False), 0, 0)
            statistics(Chunk(1, 1, 1, False), 1)
            att_x32(Chunk(0, 0, 0, False))
            scale(Chunk(1, 1, 1, False), 1, 0)
            all_chunks(dve, attention_body)

            def router(ck, *steps):
                L, Q, one, two = lg[:, 0], lg[:, 1], lg[:, 2], lg[:, 3]
                wide = [P, CT, E]

                def value(r):
                    return top[:, r, :]

                def spread(r):
                    return bc(top[:, r, :].unsqueeze(2), wide)

                for k in steps:
                    if k == 0:
                        dve.wait_ge(rt_done, ck.c + 1)
                        ins = v.scalar_tensor_tensor(out=L, in0=bank[6][:, 256:256 + CT * E].rearrange(
                            "p (t e) -> p t e", t=CT), scalar=scale_of(wscale, "R"),
                            in1=bc(br_b[:, :].unsqueeze(1), wide), op0=ALU.mult, op1=ALU.add)
                    else:
                        dve.wait_ge(rt_step, ck.c * RT_STEPS + k)
                    r, src, hot = (0, L, one) if k < 7 else (1, Q, two)
                    if k in (1, 7):
                        ins = v.tensor_reduce(value(r), src, AX.X, ALU.max)
                    elif k in (2, 8):
                        ins = v.tensor_tensor(lg[:, 4], src, spread(r), ALU.is_lt)
                    elif k in (3, 9):
                        ins = v.scalar_tensor_tensor(out=lg[:, 5], in0=lg[:, 4], scalar=float(E), in1=iota[:, :, :],
                                                     op0=ALU.mult, op1=ALU.add)
                    elif k in (4, 10):
                        ins = v.tensor_reduce(value(4 + r), lg[:, 5], AX.X, ALU.min)
                    elif k in (5, 11):
                        ins = v.tensor_tensor(hot, iota[:, :, :], spread(4 + r), ALU.is_equal)
                    elif k == 6:
                        ins = v.scalar_tensor_tensor(out=Q, in0=one, scalar=-3.0e38, in1=L, op0=ALU.mult, op1=ALU.add)
                    elif k == 12:
                        ins = v.tensor_tensor(value(2), value(0), value(1), ALU.subtract)
                    elif k == RT_TANH:
                        dve.wait_ge(rt_tanh, ck.c + 1)
                        ins = v.tensor_scalar(value(6), value(3), 0.5, 0.5, ALU.mult, ALU.add)
                    elif k == 14:
                        ins = v.tensor_scalar(value(7), value(3), -0.5, 0.5, ALU.mult, ALU.add)
                    elif k == 15:
                        ins = v.tensor_tensor(lg[:, 6], one, spread(6), ALU.mult)
                    elif k == 16:
                        ins = v.tensor_tensor(lg[:, 7], two, spread(7), ALU.mult)
                    elif k == 17:
                        ins = v.tensor_tensor(lg[:, 8 + ck.u], lg[:, 6], lg[:, 7], ALU.add)
                    ins.then_inc(rt_step, 1)

            def router_turned(ck):
                dve.wait_ge(wt_turned, ck.c + 1)
                v.tensor_copy(wtT[:, :], bank[7][0:CT * E, 128:256]).then_inc(wt_ready, 1)

            def router_b2(ck):
                dve.wait_ge(b2_done, ck.c + 1)
                v.tensor_tensor(tiles_of(h, ck), tiles_of(h, ck), bank[7][:, 256:512].rearrange("p (t d) -> p t d", t=CT),
                                ALU.add).then_inc(b2_added, 1)

            def weigh(ck, t):
                if t == 0 and has(ck, -2):
                    dve.wait_ge(moe_added, ck.c - 1)
                dve.wait_ge(ring_full, ring.filled(ck, "down", f"t{t}"))
                v.tensor_tensor(prod[:, ck.u, t], bank_of(ck, "down", f"t{t}")[:, :].rearrange("p (e d) -> p e d", e=E),
                                bc(lg[:, 8 + ck.u, t, :].unsqueeze(2), [P, E, D]), ALU.mult).then_inc(dve_emptied, 1)

            def moe_body(ck):
                nx, more, far = later(ck, 1), has(ck, 1), has(ck, 3, 4)
                router_turned(ck)
                if more:
                    router(nx, 0)
                if far:
                    stats_moe(later(ck, 3))
                else:
                    stats_soft(later(ck, 3 - CHUNKS))
                if more:
                    router(nx, 1, 2, 3, 4)
                weigh(ck, 0)
                if more:
                    router(nx, 5, 6)
                router_b2(ck)
                if more:
                    router(nx, 7, 8, 9)
                weigh(ck, 1)
                if more:
                    router(nx, 10, 11, 12)
                if far:
                    scale(later(ck, 3), ck.c + CHUNKS + 3, 1)
                else:
                    scale(later(ck, 3 - CHUNKS), ck.c + CHUNKS + 3, 2, (hx_added, ck.c + 2 - CHUNKS))
                weigh(ck, 2)
                if more:
                    router(nx, *range(RT_TANH, RT_STEPS))
                weigh(ck, 3)

            def stats_soft(ck):
                statistics(ck, ck.c + 2 * CHUNKS, (moe_added, ck.c + 1))

            c2 = Chunk(2, 0, 2, False)
            stats_moe(c2)
            router(Chunk(0, 0, 0, False), *range(RT_TANH))
            scale(c2, 2 + CHUNKS, 1)
            router(Chunk(0, 0, 0, False), *range(RT_TANH, RT_STEPS))
            all_chunks(dve, moe_body, 4)

            def soft_proj(ck):
                dve.wait_ge(ring_full, ring.filled(ck, "soft", "q"))
                if ck.looped or ck.c >= 2:
                    dve.wait_ge(ring_full, ring.filled(ck, "soft", "s", 2))
                v.tensor_scalar(qk[:, ck.u, 0, :], bank_of(ck, "soft", "q")[:, 0:256], scale_of(wscale, "Q"),
                                bqk[:, 0:1], ALU.mult, ALU.add).then_inc(dve_emptied, 1)
                dve.wait_ge(ring_full, ring.filled(ck, "soft", "v"))
                if ck.looped or ck.c >= 2:
                    dve.wait_ge(ring_full, ring.filled(ck, "soft", "o", 2))
                v.scalar_tensor_tensor(out=vv[:, ck.u].rearrange("p (t d) -> p t d", d=D),
                                       in0=bank_of(ck, "soft", "v")[:, 0:256].rearrange("p (t d) -> p t d", d=D),
                                       scalar=scale_of(wscale, "V"), in1=bc(vbias[:, :].unsqueeze(1), [P, CT, D]),
                                       op0=ALU.mult, op1=ALU.add).then_inc(dve_emptied, 1)

            def soft_shift(ck):
                s = bank_of(ck, "soft", "s")[:, 0:256].rearrange("p (t j) -> p t j", t=CT)
                dve.wait_ge(ring_full, ring.filled(ck, "soft", "s"))
                v.tensor_reduce(mx[:, ck.u, :], s, AX.X, ALU.max).then_inc(sm_max, 1)
                dve.wait_ge(sm_max, ck.c + 1)
                wait_if(dve, sm_exp, ck.c)
                v.tensor_tensor(sc[:, :].rearrange("p (t j) -> p t j", t=CT), s,
                                bc(mx[:, ck.u, :].unsqueeze(2), [P, CT, S]), ALU.subtract).then_inc(dve_emptied, 1)

            def soft_sum(ck):
                dve.wait_ge(sm_exp, ck.c + 1)
                v.tensor_reduce(rs[:, 0, :], pr[:, ck.u, :].rearrange("p (t j) -> p t j", t=CT), AX.X, ALU.add
                                ).then_inc(sm_sum, 1)
                dve.wait_ge(sm_sum, ck.c + 1)
                v.reciprocal(rs[:, 1, :], rs[:, 0, :]).then_inc(sm_inv, 1)

            def soft_body(ck):
                if has(ck, 3, 4):
                    stats_soft(later(ck, 3))
                if has(ck, 1):
                    soft_proj(later(ck, 1))
                if has(ck, 3, 4):
                    scale(later(ck, 3), ck.c + 2 * CHUNKS + 3, 2, (hx_added, ck.c + 2))
                soft_sum(ck)
                if has(ck, 1):
                    soft_shift(later(ck, 1))
                if not ck.looped and ck.c == 0:
                    dve.wait_ge(moe_added, CHUNKS)
                dve.wait_ge(ring_full, ring.filled(ck, "soft", "o"))
                dve.wait_ge(sm_inv, ck.c + 1)
                v.tensor_tensor(tiles_of(ao, ck), bank_of(ck, "soft", "o")[:, 0:256].rearrange("p (t d) -> p t d", d=D),
                                bc(rs[:, 1, :].unsqueeze(2), [P, CT, D]), ALU.mult).then_inc(dve_emptied, 1)

            soft_proj(Chunk(0, 0, 0, False))
            soft_shift(Chunk(0, 0, 0, False))
            all_chunks(dve, soft_body, 4)

            N = float(B * S)
            s4 = bank[7][:, 0:CT * D].rearrange("p (t d) -> p d t", t=CT)
            dve.wait_ge(bn_total, 1)
            link(v.tensor_reduce(mean_b[:, :], s4, AX.X, ALU.add))
            v.tensor_scalar(mean_b[:, :], mean_b[:, :], 1.0 / N, None, ALU.mult).then_inc(bn_mean, 1)
            dve.wait_ge(bn_mean, 1)

            for a, b in zip(BN_PARTS, BN_PARTS[1:]):
                v.tensor_tensor(ao[:, a:b, :], ao[:, a:b, :], bc(mean_b[:, :].unsqueeze(1), [P, b - a, D]),
                                ALU.subtract).then_inc(bn_cent, 1)
            for q in range(2):
                dve.wait_ge(bn_sq, 2 * q + 2)
                last = v.tensor_reduce(sq_half[:, q, :], squares[:, q * TILES // 2:(q + 1) * TILES // 2, :].rearrange(
                    "p t d -> p d t"), AX.X, ALU.add)
            last.then_inc(bn_var, 1)
            dve.wait_ge(bn_total, 2)
            link(v.tensor_reduce(bnA[:, :], bank[7][:, 0:2 * D].rearrange("p (t d) -> p d t", t=2), AX.X, ALU.add))
            v.tensor_scalar(bnA[:, :], bnA[:, :], 1.0 / N, BN_EPS_ATT, ALU.mult, ALU.add).then_inc(bn_eps, 1)
            dve.wait_ge(bn_root, 1)
            link(v.reciprocal(bn_y[:, :], bn_y[:, :]))
            link(v.tensor_tensor(bn_n[:, :], bn_y[:, :], bn_y[:, :], ALU.mult))
            link(v.tensor_tensor(bn_n[:, :], bn_n[:, :], bnA[:, :], ALU.mult))
            link(v.tensor_scalar(bn_n[:, :], bn_n[:, :], -0.5, 1.5, ALU.mult, ALU.add))
            link(v.tensor_tensor(bn_y[:, :], bn_y[:, :], bn_g[:, :], ALU.mult))
            v.tensor_tensor(bnA[:, :], bn_n[:, :], bn_y[:, :], ALU.mult).then_inc(bn_coef, 1)

            def bn_add(ck):
                dve.wait_ge(bn_app, ck.c + 1)
                v.tensor_tensor(tiles_of(ao, ck), tiles_of(ao, ck), bc(bn_b[:, :].unsqueeze(1), [P, CT, D]), ALU.add
                                ).then_inc(bn_step, 1)
                dve.wait_ge(bn_step, ck.c * 2 + 1)
                v.scalar_tensor_tensor(out=tiles_of(h, ck), in0=tiles_of(ao, ck), scalar=0.0, in1=tiles_of(h, ck),
                                       op0=ALU.max, op1=ALU.add).then_inc(bn_step, 1)
                if has(ck, -1):
                    norm_dense(later(ck, -1))
                statistics(ck, ck.c + 3 * CHUNKS, (bn_step, ck.c * 2 + 2))

            def norm_dense(ck):
                n = ck.c + 3 * CHUNKS
                dve.wait_ge(ln_step, ln_base(n, 3) + LN_STEPS[3])
                dve.wait_ge(n_scaled, n - 1)
                v.scalar_tensor_tensor(out=shift[:, ck.u, :], in0=mv[:, ck.u, :, 0], scalar=-1.0, in1=rstd[:, ck.u, :], op0=ALU.mult,
                                       op1=ALU.mult).then_inc(n_shift, 1)

            dve.wait_ge(hx_added, CHUNKS)
            all_chunks(dve, bn_add)
            norm_dense(Chunk(CHUNKS - 1, 1, CHUNKS - 1, False))

            def dense_relu(ck, stage, k, dst, bias):
                dve.wait_ge(ring_full, ring.filled(ck, stage, f"p{k}"))
                v.tensor_scalar(dst, bank_of(ck, stage, f"p{k}")[:, :], bias, 0.0, ALU.add, ALU.max
                                ).then_inc(dve_emptied, 1)

            def first_relus(ks):
                for k in ks:
                    if ring_who("one", k) == "V":
                        dense_relu(Chunk(0, 0, 0, False), "one", k, h1[:, 0, k, :], t12[:, 0, k:k + 1])

            first_relus((0, 1, 2))

            g = [0]

            def gate(ins):
                g[0] += 1
                ins.then_inc(gate_step, 1)
                dve.wait_ge(gate_step, g[0])

            dve.wait_ge(feat_done, CHUNKS)
            gate(v.tensor_scalar(feat[:, :], bank[7][0:D, 0:S], 1.0 / B, None, ALU.mult))
            first_relus((3,))
            dve.wait_ge(gate_pe, 1)
            gate(v.tensor_tensor(gl[:, 0, :], bank[6][0:S, 0:E], br1_b[:, :], ALU.add))
            gate(v.tensor_reduce(gs[:, 0:1], gl[:, 0, :], AX.X, ALU.max))
            gate(v.tensor_scalar(gl[:, 1, :], gl[:, 0, :], gs[:, 0:1], None, ALU.subtract))
            assert g[0] == GATE_SHIFTED
            dve.wait_ge(gate_exp, 1)
            gate(v.reciprocal(gs[:, 2:3], gs[:, 1:2]))
            gate(v.tensor_scalar(gl[:, 3, :], gl[:, 2, :], gs[:, 2:3], None, ALU.mult))
            gate(v.tensor_copy(gwx[:, :, :], bc(gl[:, 3, :].unsqueeze(2), [S, E, D])))

            def gate_turned():
                dve.wait_ge(gate_pe, 2)
                gate(v.tensor_copy(gwT[:, 0, :], bank[6][0:E, 256:256 + S]))
                gate(v.tensor_copy(gwT[:, 1, :], bank[6][0:E, 256:256 + S]))
                gate(v.tensor_copy(gwb[:, :, :], bank[7][:, 0:4 * S].rearrange("p (a f) -> p a f", a=4)))

            def gate_bo():
                dve.wait_ge(gate_pe, 3)
                gate(v.tensor_copy(bow[:, :], bank[6][:, 384:384 + D]))
                assert g[0] == GATE_STEPS

            def third(ck):
                dve.wait_ge(ring_full, ring.filled(ck, "three", "y"))
                dve.wait_ge(bow_added, ck.c + 1)
                v.tensor_tensor(tiles_of(h, ck), tiles_of(h, ck),
                                bank_of(ck, "three", "y")[:, 0:CT * D].rearrange("p (t d) -> p t d", t=CT), ALU.add
                                ).then_inc(dve_emptied, 1)

            gate_part = {2: gate_turned, 3: gate_bo}

            def dense_body(ck):
                if ck.looped or ck.c >= 2:
                    dve.wait_ge(weighed, ck.c * 4 - 4)
                for k in range(4):
                    if not ck.looped and ck.c == 0 and k in gate_part:
                        gate_part[k]()
                    if ring_who("one", k) == "V" and (ck.looped or ck.c + 1 < CHUNKS):
                        dense_relu(Chunk(ck.c + 1, 1 - ck.u, ck.near + 1, ck.looped), "one", k,
                                   h1[:, 1 - ck.u, k, :], t12[:, 0, k:k + 1])
                    if ring_who("two", k) == "V":
                        dense_relu(ck, "two", k, h2[:, ck.u, k, :], t12[:, 1, k:k + 1])
                    if k == 2 and has(ck, -1):
                        third(later(ck, -1))

            all_chunks(dve, dense_body)
            third(Chunk(CHUNKS - 1, 1, CHUNKS - 1, False))

        @block.tensor
        def _(pe):
            mm = nc.tensor.matmul

            def fmm(out, lhsT, rhs, start=True, stop=True):
                return mm(out, lhsT, rhs, start=start, stop=stop)

            def two_pass(out, xs, name, lo, hi, x_moving):
                a = SEG[name][0]
                for i, w in enumerate((whi, wlo)):
                    wp = w[:, a + lo:a + hi]
                    last = fmm(out, wp if x_moving else xs, xs if x_moving else wp, start=(i == 0), stop=(i == 1))
                return last

            pe.wait_ge(s_const, 16)

            def prep_turn():
                pe.wait_ge(prep_dve, PERMUTED)
                for w in (0, 1):
                    for a in range(4):
                        last = nc.tensor.transpose(bank[6][:, 256 * w + 64 * a:256 * w + 64 * a + 64], permqkv[:, w, a, :],
                                                   ident[0:D, 0:D])
                last.then_inc(prep_pe, 1)
                for a in range(4):
                    last = nc.tensor.transpose(bank[7][:, 64 * a:64 * a + 64], permqkv[:, 2, a, :], ident[0:D, 0:D])
                last.then_inc(prep_pe, 1)

            def prep_products():
                pe.wait_ge(prep_dve, TURNED_READY)
                for e2 in (0, 1):
                    if e2 == 1:
                        pe.wait_ge(prep_pe, 3)
                    half = slice(64 * e2, 64 * e2 + 64)
                    for a in range(4):
                        hd = 2 * a + e2
                        fmm(bank[6][:, 64 * hd:64 * hd + 64], wT[half, 0, a].rearrange("p c g -> p (c g)"),
                            wT[half, 1, a, 0, :])
                        last = fmm(bank[7][:, (4 * e2 + a) * 64:(4 * e2 + a) * 64 + 64],
                                   wT[half, 2, a].rearrange("p c g -> p (c g)"), wo_a[half, hd, :])
                    last.then_inc(prep_pe, 1)

            def prep_vectors():
                pe.wait_ge(s_wf, 16 * len(LATE_LOADS))
                pe.wait_ge(prep_dve, PRODUCTS_MAX)
                nc.tensor.transpose(bank[7][0:D, 256:320], wv1raw[:, :], ident[0:D, 0:D])
                nc.tensor.transpose(bank[7][:, 320:368], rows[:, :], ident[0:48, 0:48]).then_inc(prep_pe, 1)

            def prep_small():
                pe.wait_ge(prep_dve, FACTORS_READY)
                for a in range(4):
                    fmm(bank[6][:, P * a:P * a + P], s1wide[:, a, :], ident)
                    for e2 in (0, 1):
                        half = slice(64 * e2, 64 * e2 + 64)
                        fmm(bank[7][half, 256 + D * a:256 + D * a + D], s2wide[half, a, :], fold[half, :])
                fmm(bank[7][:, 0:D], wv1T[:, :, :].rearrange("p c g -> p (c g)"), wl1[:, :])
                fmm(bank[7][:, 64:128], bv_b[:, :], wl1[:, :])
                fmm(bank[7][:, 128:128 + E], beta0_b[:, :], wrraw[0:D, :])
                for e in range(E):
                    last = fmm(bank[7][:, 192 + e:193 + e], w1raw[0:D, H0 * e:H0 * e + H0], beta0[:, 0:1])
                last.then_inc(prep_pe, 1)

            def tok_rows(g):
                pe.wait_ge(s_img[g % 4], 16 * (g // 4 + 1))
                wait_if(pe, rows_copied, g)
                for q in range(4):
                    last = fmm(bank[0][32 * q:32 * q + 32, 0:4 * R], resize,
                               img[:, g % 4].rearrange("r (k q) c -> r q k c", q=4)[:, q])
                last.then_inc(rows_done, 1)

            def tok_turn_rows(g):
                pe.wait_ge(rows_copied, g + 1)
                wait_if(pe, z_copied, g)
                for k in range(4):
                    last = nc.tensor.transpose(bank[1][0:R, P * k:P * k + P], ybuf[:, R * k:R * k + R], ident)
                last.then_inc(rows_turned, 1)

            MAPS = ((0, 16, 0), (0, 16, 16), (24, 32, 32), (16, 32, 40))

            def tok_maps(g):
                u = g % 2
                pe.wait_ge(z_copied, g + 1)
                wait_if(pe, maps_copied, g)
                for o, (lo, hi, at) in enumerate(MAPS):
                    last = fmm(bank[2][:, at:at + hi - lo], zbuf[:, u, o, :], resize[:, lo:hi])
                last.then_inc(maps_done, 1)

            def tok_turn(g):
                u = g % 2
                pe.wait_ge(maps_copied, g + 1)
                if g >= 1:
                    pe.wait_ge(ft_copied, g)
                for j in range(8):
                    last = nc.tensor.transpose(bank[4 + j // 4][0:NMAPS, 128 * (j % 4):128 * (j % 4) + 128],
                                               fbuf[:, u, :].rearrange("p (m j) -> p j m", j=8)[:, j, :], ident)
                last.then_inc(ft_done, 1)

            def tok_project(g):
                u = g % 2
                pe.wait_ge(ft_copied, g + 1)
                if g >= 1:
                    pe.wait_ge(h_ready, g)
                for t in range(GROUP // 2):
                    last = fmm(bank[3][:, 64 * t:64 * t + 64], ftok[:, u, P * t:P * t + P], wb[:, :])
                last.then_inc(tok_done, 1)

            pe.wait_ge(s_wa, 16 * len(TOKEN_W_LOADS))
            tok_rows(0)
            tok_turn_rows(0)
            tok_rows(1)
            tok_maps(0)
            for g in range(GROUPS):
                tok_turn(g)
                if g + 1 < GROUPS:
                    tok_turn_rows(g + 1)
                if g + 2 < GROUPS:
                    tok_rows(g + 2)
                tok_project(g)
                if g + 1 < GROUPS:
                    tok_maps(g + 1)
                if g in (PREP_AT[0], PREP_AT[1], PREP_AT[3], PREP_AT[5]):
                    {PREP_AT[0]: prep_turn, PREP_AT[1]: prep_products, PREP_AT[3]: prep_vectors,
                     PREP_AT[5]: prep_small}[g]()

            def turn16(dst, n, split_value):
                pe.wait_ge(n_split, split_value)
                d = dst[:, :].bitcast(F16)
                for t in range(CT):
                    last = nc.tensor.transpose(d[:, P * t:P * t + P], xcat[:, t, :], ident16[:, :])
                return last

            def att_turn16(ck):
                wait_if(pe, x32_ready, ck.c)
                turn16(bank[6], ck.c, ck.c + 1).then_inc(x16_turned, 1)

            def att_turn32(ck):
                pe.wait_ge(x16_ready, ck.c + 1)
                for t in range(CT):
                    last = nc.tensor.transpose(bank[6][:, P * t:P * t + P],
                                               xn[:, t, :, :].rearrange("p c d -> p (c d)"), ident)
                last.then_inc(x32_turned, 1)

            def moe_turn(ck):
                if not ck.looped and ck.c == 0:
                    pe.wait_ge(x32_ready, CHUNKS)
                else:
                    pe.wait_ge(rt_step, (ck.c - 1) * RT_STEPS + 1)
                pe.wait_ge(x16_ready, ck.c + CHUNKS)
                turn16(bank[6], ck.c, ck.c + CHUNKS + 1).then_inc(x16_turned, 1)

            def attention_body(ck):
                more = ck.looped or ck.c + 1 < CHUNKS
                nx = Chunk(ck.c + 1, 1 - ck.u, ck.near + 1, ck.looped)
                xs = x16[:, ck.u, :]
                pe.wait_ge(x16_ready, ck.c + 1)
                for a in range(4):
                    ring.wait_free(pe, ck, "att", f"q{a}")
                    two_pass(bank_of(ck, "att", f"q{a}")[:, :], xs, "M", P * a, P * a + P, True
                             ).then_inc(ring_full, 1)
                if more:
                    att_turn16(nx)
                else:
                    moe_turn(Chunk(0, 0, 0, False))
                for t in range(CT):
                    ring.wait_free(pe, ck, "att", f"v{t}")
                    bk = bank_of(ck, "att", f"v{t}")
                    for b in (0, 1):
                        xb = xs[:, P * t + S * b:P * t + S * b + S]
                        for i, w in enumerate((whi, wlo)):
                            for e2 in (0, 1):
                                a0 = SEG["N"][0] + 256 * e2
                                last = fmm(bk[64 * e2:64 * e2 + 64, 256 * b:256 * b + 256], xb, w[:, a0:a0 + 256],
                                           start=(i == 0), stop=(i == 1))
                    last.then_inc(ring_full, 1)
                if more:
                    att_turn32(nx)
                pe.wait_ge(x32_ready, ck.c + 1)
                for a in range(4):
                    ring.wait_emptied(pe, ck, "att", f"q{a}", wait_apart)
                for t in range(CT):
                    ring.wait_free(pe, ck, "att", f"s{t}", wait_apart)
                    bk = bank_of(ck, "att", f"s{t}")
                    for b in (0, 1):
                        at = P * t + S * b
                        for e2 in (0, 1):
                            half = slice(64 * e2, 64 * e2 + 64)
                            last = fmm(bk[half, 256 * b:256 * b + 256], x32[half, ck.u, at:at + S],
                                       qbuf[half, :, at:at + S])
                    last.then_inc(ring_full, 1)
                wait_if(pe, av_relu, ck.c)
                for t in range(CT):
                    ring.wait_emptied(pe, ck, "att", f"v{t}")
                    ring.wait_emptied(pe, ck, "att", f"s{t}")
                    for a in range(4):
                        for b in (0, 1):
                            cs = slice(256 * b + 64 * a, 256 * b + 64 * a + 64)
                            last = fmm(bank[7][64 * b:64 * b + 64, D * t:D * t + D], abuf[:, t, cs], vbuf[:, t, cs],
                                       start=(a == 0), stop=(a == 3))
                last.then_inc(av_done, 1)

            pe.wait_ge(prep_dve, FACTORS_READY + 6)
            pe.wait_ge(h_ready, GROUPS)
            att_turn16(Chunk(0, 0, 0, False))
            att_turn32(Chunk(0, 0, 0, False))
            all_chunks(pe, attention_body)

            def soft_turn(ck):
                if not ck.looped and ck.c == 0:
                    pe.wait_ge(rt_step, (CHUNKS - 1) * RT_STEPS + 1)
                pe.wait_ge(x16_ready, ck.c + 2 * CHUNKS)
                turn16(bank[6], ck.c, ck.c + 2 * CHUNKS + 1).then_inc(x16_turned, 1)

            def moe_router(ck):
                pe.wait_ge(x16_ready, ck.c + CHUNKS + 1)
                for t in range(CT):
                    last = two_pass(bank[6][:, 256 + E * t:256 + E * t + E], x16[:, ck.u, P * t:P * t + P], "R", 0, E, False)
                last.then_inc(rt_done, 1)

            def moe_up(ck, e):
                ring.wait_free(pe, ck, "up", f"e{e}")
                two_pass(bank_of(ck, "up", f"e{e}")[:, :], x16[:, ck.u, :], "W1", H0 * e, H0 * e + H0, True
                         ).then_inc(ring_full, 1)

            def moe_b2_turn(ck):
                if not ck.looped and ck.c == 0:
                    pe.wait_ge(av_relu, CHUNKS)
                pe.wait_ge(rt_step, ck.c * RT_STEPS + RT_STEPS)
                wait_if(pe, b2_added, ck.c)
                nc.tensor.transpose(bank[7][0:CT * E, 128:256], lg[:, 8 + ck.u].rearrange("p t e -> p (t e)"), ident
                                    ).then_inc(wt_turned, 1)

            def moe_b2(ck):
                pe.wait_ge(wt_ready, ck.c + 1)
                fmm(bank[7][:, 256:512], wtT[:, :], b2blk[:, :]).then_inc(b2_done, 1)

            def moe_down(ck, t):
                ring.wait_free(pe, ck, "down", f"t{t}")
                for e in range(E):
                    last = fmm(bank_of(ck, "down", f"t{t}")[:, D * e:D * e + D], gbuf[:, ck.u, e, P * t:P * t + P],
                               w2[:, e, :])
                last.then_inc(ring_full, 1)

            def moe_body(ck):
                nx, more = later(ck, 1), has(ck, 1)
                if more:
                    moe_router(nx)
                moe_b2_turn(ck)
                for t in range(CT):
                    if more:
                        moe_up(nx, 2 * t)
                        moe_up(nx, 2 * t + 1)
                    if t == 0:
                        if has(ck, 2):
                            moe_turn(later(ck, 2))
                        else:
                            soft_turn(later(ck, 2 - CHUNKS))
                    if t == 0:
                        ring.wait_emptied(pe, ck, "up", f"e{E - 1}")
                    moe_down(ck, t)
                    if t == 0:
                        moe_b2(ck)

            c0 = Chunk(0, 0, 0, False)
            pe.wait_ge(prep_dve, SPLIT_READY)
            moe_router(c0)
            for e in range(E):
                moe_up(c0, e)
                if e == 1:
                    moe_turn(Chunk(1, 1, 1, False))
            pe.wait_ge(s_wp, 16 * len(POOL_LOADS))
            all_chunks(pe, moe_body, 4)

            def soft_proj(ck):
                pe.wait_ge(x16_ready, ck.c + 2 * CHUNKS + 1)
                xs = x16[:, ck.u, :].rearrange("p (t b i) -> p t b i", t=CT, b=2)
                for name in "QK":
                    ring.wait_free(pe, ck, "soft", name.lower())
                    bk = bank_of(ck, "soft", name.lower())
                    a = SEG[name][0]
                    for i, w in enumerate((whi, wlo)):
                        for b in (0, 1):
                            last = fmm(bk[64 * b:64 * b + 64, 0:256], w[:, a:a + D], xs[:, :, b, :],
                                       start=(i == 0), stop=(i == 1))
                    last.then_inc(ring_full, 1)
                ring.wait_free(pe, ck, "soft", "v")
                bk = bank_of(ck, "soft", "v")
                a = SEG["V"][0]
                for th in (0, 1):
                    for b in (0, 1):
                        for i, w in enumerate((whi, wlo)):
                            for t2 in (0, 1):
                                at = 128 * th + 64 * b
                                last = fmm(bk[64 * t2:64 * t2 + 64, at:at + 64], xs[:, 2 * th + t2, b, :],
                                           w[:, a:a + D], start=(i == 0), stop=(i == 1))
                last.then_inc(ring_full, 1)

            def soft_scores(ck):
                ring.wait_emptied(pe, ck, "soft", "q")
                ring.wait_emptied(pe, ck, "soft", "k")
                ring.wait_free(pe, ck, "soft", "s", wait_apart)
                bk = bank_of(ck, "soft", "s")
                for t in range(CT):
                    for b in (0, 1):
                        half = slice(64 * b, 64 * b + 64)
                        last = fmm(bk[half, 64 * t:64 * t + 64], qk[half, ck.u, 0, 64 * t:64 * t + 64],
                                   qk[half, ck.u, 1, 64 * t:64 * t + 64])
                last.then_inc(ring_full, 1)

            def soft_turn_p(ck):
                pe.wait_ge(sm_exp, ck.c + 1)
                ring.wait_free(pe, ck, "soft", "pt")
                for th in (0, 1):
                    last = nc.tensor.transpose(bank_of(ck, "soft", "pt")[:, P * th:P * th + P],
                                               pr[:, ck.u, P * th:P * th + P], ident)
                last.then_inc(ring_full, 1)

            def soft_out(ck, t2):
                bk = bank_of(ck, "soft", "o")
                if t2 == 0:
                    ring.wait_emptied(pe, ck, "soft", "pt")
                    ring.wait_emptied(pe, ck, "soft", "v")
                    ring.wait_free(pe, ck, "soft", "o", wait_apart)
                else:
                    wait_apart(pe, out_even, ck.c + 1)
                half = slice(64 * t2, 64 * t2 + 64)
                for th in (0, 1):
                    for b in (0, 1):
                        at = 128 * th + 64 * b
                        t = 2 * th + t2
                        last = fmm(bk[64 * b:64 * b + 64, 64 * t:64 * t + 64], pT[half, at:at + 64],
                                   vv[half, ck.u, at:at + 64])
                last.then_inc(out_even if t2 == 0 else ring_full, 1)

            def clear_bank7():
                mm(bank[7][:, :], ones[0:1, :], zero[:, :], start=True, stop=False, skip_group_check=True)

            def soft_body(ck):
                if has(ck, 2):
                    soft_turn(later(ck, 2))
                if has(ck, 1):
                    soft_proj(later(ck, 1))
                soft_turn_p(ck)
                if has(ck, 1):
                    soft_scores(later(ck, 1))
                soft_out(ck, 0)
                soft_out(ck, 1)

            pe.wait_ge(b2_added, CHUNKS)
            soft_proj(c0)
            soft_scores(c0)
            all_chunks(pe, soft_body, 4)

            pe.wait_ge(bn_sum, CHUNKS)
            fmm(bank[7][:, 0:CT * D], ones[:, :], bn_acc[:, :, :].rearrange("p t d -> p (t d)")).then_inc(bn_total, 1)
            pe.wait_ge(bn_mean, 1)
            pe.wait_ge(bn_var, 1)
            fmm(bank[7][:, 0:2 * D], ones[:, :], sq_half[:, :, :].rearrange("p q d -> p (q d)")).then_inc(bn_total, 1)
            pe.wait_ge(bn_coef, 1)
            clear_bank7()

            def dense_one(ck, k):
                ring.wait_free(pe, ck, "one", f"p{k}")
                xs = x16all[:, ck.c * CN:ck.c * CN + CN] if not ck.looped else x16all[:, DS(ck.c * CN, CN)]
                two_pass(bank_of(ck, "one", f"p{k}")[:, :], xs, "U", P * k, P * k + P, True).then_inc(ring_full, 1)

            def dense_turn(ck):
                pe.wait_ge(x16_ready, ck.c + 3 * CHUNKS)
                if not ck.looped and ck.c >= CHUNKS - 2:
                    dense_one(c0, ck.c - (CHUNKS - 2))
                turn16(bank[6], ck.c, ck.c + 3 * CHUNKS + 1).then_inc(x16_turned, 1)
                for t in range(CT):
                    last = mm(bank[7][0:D, 0:S], xn[:, t, ck.u, :], fold, start=False, stop=False, skip_group_check=True)
                last.then_inc(feat_done, 1)

            all_chunks(pe, dense_turn)
            dense_one(c0, 2)
            dense_one(c0, 3)

            def gate_logits():
                pe.wait_ge(x16_ready, 4 * CHUNKS)
                pe.wait_ge(gate_step, 1)
                fmm(bank[6][0:S, 0:E], feat[:, :], wr1[:, :]).then_inc(gate_pe, 1)

            def gate_turn():
                pe.wait_ge(gate_step, GATE_SHIFTED + 3)
                nc.tensor.transpose(bank[6][0:E, 256:256 + S], gl[:, 3, :], ident[0:S, 0:S])
                for a in range(4):
                    last = fmm(bank[7][:, S * a:S * a + S], gwx[:, 2 * a:2 * a + 2, :].rearrange("f e n -> f (e n)"),
                               ident[0:S, 0:S])
                last.then_inc(gate_pe, 1)

            def gate_bo():
                pe.wait_ge(gate_step, GATE_STEPS - 1)
                fmm(bank[6][:, 384:384 + D], gwT[:, :, :].rearrange("e c f -> e (c f)"), bo1[:, :]).then_inc(gate_pe, 1)

            gate_part = {0: gate_logits, 2: gate_turn, 3: gate_bo}

            def dense_two(ck, k):
                ring.wait_emptied(pe, ck, "one", f"p{k}")
                ring.wait_free(pe, ck, "two", f"p{k}", wait_apart)
                for e2 in (0, 1):
                    half = slice(64 * e2, 64 * e2 + 64)
                    last = fmm(bank_of(ck, "two", f"p{k}")[half, :], u2[half, k, :], h1[half, ck.u, k, :])
                last.then_inc(ring_full, 1)

            def dense_three(ck):
                if ck.looped:
                    pe.wait_ge(weighed, ck.c * 4 + 4)
                ring.wait_free(pe, ck, "three", "z")
                for k in range(4):
                    if not ck.looped:
                        pe.wait_ge(weighed, ck.c * 4 + k + 1)
                    half = slice(64 * (k % 2), 64 * (k % 2) + 64)
                    last = fmm(bank_of(ck, "three", "z")[half, :], uo[:, k, :], h2w[:, ck.u, k, :],
                               start=(k < 2), stop=(k >= 2))
                last.then_inc(ring_full, 1)

            def dense_turn_back(ck):
                ring.wait_emptied(pe, ck, "three", "z")
                ring.wait_free(pe, ck, "three", "y")
                for t in range(CT):
                    last = fmm(bank_of(ck, "three", "y")[:, D * t:D * t + D], zs[:, P * t:P * t + P], fold)
                last.then_inc(ring_full, 1)

            def dense_body(ck):
                nx = Chunk(ck.c + 1, 1 - ck.u, ck.near + 1, ck.looped)
                for k in range(4):
                    if not ck.looped and ck.c == 0 and k in gate_part:
                        gate_part[k]()
                    if ck.looped or ck.c + 1 < CHUNKS:
                        dense_one(nx, k)
                    dense_two(ck, k)
                    if k == 1 and has(ck, -1):
                        dense_three(later(ck, -1))
                    if k == 2 and has(ck, -1):
                        dense_turn_back(later(ck, -1))

            all_chunks(pe, dense_body)
            dense_three(Chunk(CHUNKS - 1, 1, CHUNKS - 1, False))
            dense_turn_back(Chunk(CHUNKS - 1, 1, CHUNKS - 1, False))


_INS = ["x", "L0_tok_W", "L0_tok_b", "L0_attn_Wq", "L0_attn_Wk", "L0_attn_Wv", "L0_attn_Wo",
        "L0_ffn_gamma", "L0_ffn_beta", "L0_ffn_Wr", "L0_ffn_br", "L0_ffn_W1", "L0_ffn_b1", "L0_ffn_W2", "L0_ffn_b2",
        "L1_attn_Wq", "L1_attn_bq", "L1_attn_Wk", "L1_attn_bk", "L1_attn_Wv", "L1_attn_bv", "L1_attn_Wl", "L1_attn_bl",
        "L1_attn_gamma", "L1_attn_beta",
        "L1_ffn_Wr", "L1_ffn_br", "L1_ffn_W1", "L1_ffn_b1", "L1_ffn_g1", "L1_ffn_be1", "L1_ffn_m1", "L1_ffn_v1",
        "L1_ffn_W2", "L1_ffn_b2", "L1_ffn_g2", "L1_ffn_be2", "L1_ffn_m2", "L1_ffn_v2", "L1_ffn_Wo", "L1_ffn_bo"]


def shape_constants():
    import numpy as np

    r2 = 0.5 ** 0.5

    def haar(n, sign):
        m = np.zeros((n // 2, n))
        m[np.arange(n // 2), 2 * np.arange(n // 2)] = r2
        m[np.arange(n // 2), 2 * np.arange(n // 2) + 1] = sign * r2
        return m

    def resize(n, to=8):
        scale = n / to
        at = (np.arange(to) + 0.5) * scale - 0.5
        w = np.maximum(0, 1 - np.abs(at[:, None] - np.arange(n)[None, :]) / scale)
        return w / w.sum(1, keepdims=True)

    lo = haar(R, 1)
    ops = [resize(R // 4) @ haar(R // 2, 1) @ lo, resize(R // 4) @ haar(R // 2, -1) @ lo,
           resize(R // 2) @ lo, resize(R // 2) @ haar(R, -1)]
    c = np.zeros((P, 32 + P + S), np.float32)
    c[:R, :32] = np.concatenate(ops).T
    c[:, 32:32 + P] = np.eye(P)
    c[:, 32 + P:] = np.concatenate([np.eye(S), np.eye(S)])
    return c


def kernel(**inputs):
    import numpy as _np
    import concourse.bacc as _bacc
    from concourse import mybir as _mybir
    from concourse.bass_utils import run_bass_kernel_spmd as _run

    nc = _bacc.Bacc("TRN2", target_bir_lowering=False, num_devices=1)
    arrays, args = {}, []
    for name in _INS:
        a = _np.ascontiguousarray(inputs[name])
        arrays[f"in_{name}_dram"] = a
        args.append(nc.dram_tensor(f"in_{name}_dram", a.shape, _mybir.dt.from_np(a.dtype), kind="ExternalInput").ap())
    consts = shape_constants()
    arrays["shape_constants_dram"] = consts
    args.append(nc.dram_tensor("shape_constants_dram", consts.shape, _mybir.dt.float32, kind="ExternalInput").ap())
    args.append(nc.dram_tensor("out_0_dram", (B, S, D), _mybir.dt.float32, kind="ExternalOutput").ap())
    vit_tower(nc, *args)
    r = _run(nc, [arrays], core_ids=[0])
    return r.results[0]["out_0_dram"]
```
